# Optimizing a Trainium2 kernel written in Bass

```python
import numpy as np
import jax
import jax.numpy as jnp

def _softmax(x, axis=-1):
    return jax.nn.softmax(x, axis=axis)

def _gelu(x):
    return jax.nn.gelu(x, approximate=True)

def _silu(x):
    return jax.nn.silu(x)

def _sigmoid(x):
    return jax.nn.sigmoid(x)

def _layernorm(x, axis=-1, eps=1e-05):
    m = jnp.mean(x, axis=axis, keepdims=True)
    v = jnp.var(x, axis=axis, keepdims=True)
    return (x - m) / jnp.sqrt(v + eps)

def _scatter_add(tgt, idx, src, axis=0):
    return tgt.at[idx].add(src)

def _segment_sum(src, seg, n):
    return jax.ops.segment_sum(src, seg, n)
kernel_name = 'mk_gnn_preln_d2_gnn_r8_ed991d'

def setup_inputs(seed: int=0):
    np.random.seed(seed)
    _w = jnp.asarray

    def _rec_inputs():
        import jax
        import jax.numpy as jnp
        _gk = jax.random.key(seed)
        x = -0.000202 + 1 * jax.random.normal(jax.random.fold_in(_gk, 1), (12500, 128), jnp.float32)
        _s = jax.random.randint(jax.random.fold_in(_gk, 2), (100000,), 0, 12500, jnp.int32)
        _d = jax.random.randint(jax.random.fold_in(_gk, 3), (100000,), 0, 12500, jnp.int32)
        _loop = jnp.arange(12500, dtype=jnp.int32)
        src = jnp.concatenate([_s, _d, _loop])
        dst = jnp.concatenate([_d, _s, _loop])
        _o = jnp.argsort(dst, stable=True)
        src = src[_o]
        dst = dst[_o]
        edge_type_9 = jax.random.randint(jax.random.fold_in(_gk, 12), (212500,), 0, 9, jnp.int32)
        return (x, src, dst, edge_type_9)
    x, src, dst, edge_type_9 = _rec_inputs()

    def _L0_gnn_setup():
        import jax, jax.numpy as jnp
        import numpy as np
        NUM_EDGE_TYPES = 8
        HIDDEN = 128
        N_NODES = 6250
        N_EDGES = 75000

        def _gru_cell(x, h, W_ih, W_hh, b_ih, b_hh):
            H = h.shape[-1]
            gi = x @ W_ih.T + b_ih
            gh = h @ W_hh.T + b_hh
            i_r, i_z, i_n = (gi[:, :H], gi[:, H:2 * H], gi[:, 2 * H:])
            h_r, h_z, h_n = (gh[:, :H], gh[:, H:2 * H], gh[:, 2 * H:])
            r = jax.nn.sigmoid(i_r + h_r)
            z = jax.nn.sigmoid(i_z + h_z)
            n = jnp.tanh(i_n + r * h_n)
            return (1.0 - z) * n + z * h
        key = jax.random.key(seed)
        ks = jax.random.split(key, 10)
        H = HIDDEN
        h = jax.random.normal(ks[0], (N_NODES, H), dtype=jnp.float32)
        edge_index = jax.random.randint(ks[1], (2, N_EDGES), 0, N_NODES, dtype=jnp.int32)
        edge_type = jax.random.randint(ks[2], (N_EDGES,), 0, NUM_EDGE_TYPES + 1, dtype=jnp.int32)
        s = 1.0 / np.sqrt(H)
        W_msg = jax.random.uniform(ks[3], (H, H), jnp.float32, -s, s)
        b_msg = jax.random.uniform(ks[4], (H,), jnp.float32, -s, s)
        edge_embed = jax.random.normal(ks[5], (NUM_EDGE_TYPES + 1, H), dtype=jnp.float32)
        W_ih = jax.random.uniform(ks[6], (3 * H, H), jnp.float32, -s, s)
        W_hh = jax.random.uniform(ks[7], (3 * H, H), jnp.float32, -s, s)
        b_ih = jax.random.uniform(ks[8], (3 * H,), jnp.float32, -s, s)
        b_hh = jax.random.uniform(ks[9], (3 * H,), jnp.float32, -s, s)
        return {'h': h, 'edge_index': edge_index, 'edge_type': edge_type, 'num_nodes': N_NODES, 'W_msg': W_msg, 'b_msg': b_msg, 'edge_embed': edge_embed, 'W_ih': W_ih, 'W_hh': W_hh, 'b_ih': b_ih, 'b_hh': b_hh}
    _L0_gnn_all = _L0_gnn_setup()
    _L0_gnn_in = {k: v for k, v in _L0_gnn_all.items() if k in ('W_msg', 'b_msg', 'edge_embed', 'W_ih', 'W_hh', 'b_ih', 'b_hh')}
    del _L0_gnn_all

    def _L1_gnn_setup():
        import jax, jax.numpy as jnp
        import numpy as np
        N = 12500
        E = 200000
        F_IN = 128
        F_OUT = 128
        BN_EPS = 1e-05
        key = jax.random.key(seed)
        ks = jax.random.split(key, 8)
        x = jax.random.normal(ks[0], (N, F_IN), dtype=jnp.float32)
        edge_index = jax.random.randint(ks[1], (2, E), 0, N, dtype=jnp.int64)
        eps = jnp.zeros((), dtype=jnp.float32)
        lim1 = 1.0 / np.sqrt(F_IN)
        W1 = jax.random.uniform(ks[2], (F_OUT, F_IN), minval=-lim1, maxval=lim1, dtype=jnp.float32)
        b1 = jax.random.uniform(ks[3], (F_OUT,), minval=-lim1, maxval=lim1, dtype=jnp.float32)
        gamma = jnp.ones((F_OUT,), dtype=jnp.float32)
        beta = jnp.zeros((F_OUT,), dtype=jnp.float32)
        lim2 = 1.0 / np.sqrt(F_OUT)
        W2 = jax.random.uniform(ks[4], (F_OUT, F_OUT), minval=-lim2, maxval=lim2, dtype=jnp.float32)
        b2 = jax.random.uniform(ks[5], (F_OUT,), minval=-lim2, maxval=lim2, dtype=jnp.float32)
        return {'x': x, 'edge_index': edge_index, 'eps': eps, 'W1': W1, 'b1': b1, 'gamma': gamma, 'beta': beta, 'W2': W2, 'b2': b2}
    _L1_gnn_all = _L1_gnn_setup()
    _L1_gnn_in = {k: v for k, v in _L1_gnn_all.items() if k in ('eps', 'W1', 'b1', 'gamma', 'beta', 'W2', 'b2')}
    del _L1_gnn_all
    return {'x': x, 'src': src, 'dst': dst, 'edge_type_9': edge_type_9, 'L0_gnn_W_msg': _L0_gnn_in['W_msg'], 'L0_gnn_b_msg': _L0_gnn_in['b_msg'], 'L0_gnn_edge_embed': _L0_gnn_in['edge_embed'], 'L0_gnn_W_ih': _L0_gnn_in['W_ih'], 'L0_gnn_W_hh': _L0_gnn_in['W_hh'], 'L0_gnn_b_ih': _L0_gnn_in['b_ih'], 'L0_gnn_b_hh': _L0_gnn_in['b_hh'], 'L1_gnn_eps': _L1_gnn_in['eps'], 'L1_gnn_W1': _L1_gnn_in['W1'], 'L1_gnn_b1': _L1_gnn_in['b1'], 'L1_gnn_gamma': _L1_gnn_in['gamma'], 'L1_gnn_beta': _L1_gnn_in['beta'], 'L1_gnn_W2': _L1_gnn_in['W2'], 'L1_gnn_b2': _L1_gnn_in['b2']}

def reference(x, src, dst, edge_type_9, L0_gnn_W_msg, L0_gnn_b_msg, L0_gnn_edge_embed, L0_gnn_W_ih, L0_gnn_W_hh, L0_gnn_b_ih, L0_gnn_b_hh, L1_gnn_eps, L1_gnn_W1, L1_gnn_b1, L1_gnn_gamma, L1_gnn_beta, L1_gnn_W2, L1_gnn_b2):
    import jax
    import jax.numpy as jnp

    def _L0_gnn_ref(h, edge_index, edge_type, num_nodes, W_msg, b_msg, edge_embed, W_ih, W_hh, b_ih, b_hh):
        import jax, jax.numpy as jnp
        import numpy as np
        NUM_EDGE_TYPES = 8
        HIDDEN = 128
        N_NODES = 6250
        N_EDGES = 75000

        def _gru_cell(x, h, W_ih, W_hh, b_ih, b_hh):
            H = h.shape[-1]
            gi = x @ W_ih.T + b_ih
            gh = h @ W_hh.T + b_hh
            i_r, i_z, i_n = (gi[:, :H], gi[:, H:2 * H], gi[:, 2 * H:])
            h_r, h_z, h_n = (gh[:, :H], gh[:, H:2 * H], gh[:, 2 * H:])
            r = jax.nn.sigmoid(i_r + h_r)
            z = jax.nn.sigmoid(i_z + h_z)
            n = jnp.tanh(i_n + r * h_n)
            return (1.0 - z) * n + z * h
        src = edge_index[0]
        dst = edge_index[1]
        src_h = h[src] @ W_msg.T + b_msg
        emb = edge_embed[jnp.clip(edge_type, 0, NUM_EDGE_TYPES)]
        msg = src_h + emb
        messages = jax.ops.segment_sum(msg, dst, num_segments=num_nodes)
        h_new = _gru_cell(messages, h[:num_nodes], W_ih, W_hh, b_ih, b_hh)
        result = jnp.zeros_like(h).at[:num_nodes].set(h_new)
        return result

    def _L1_gnn_ref(x, edge_index, eps, W1, b1, gamma, beta, W2, b2):
        import jax, jax.numpy as jnp
        import numpy as np
        N = 12500
        E = 200000
        F_IN = 128
        F_OUT = 128
        BN_EPS = 1e-05
        row, col = (edge_index[0], edge_index[1])
        agg = jax.ops.segment_sum(x[col], row, num_segments=x.shape[0])
        h = (1.0 + eps) * x + agg
        h = h @ W1.T + b1
        mu = jnp.mean(h, axis=0)
        var = jnp.mean(jnp.square(h - mu), axis=0)
        h = (h - mu) * jax.lax.rsqrt(var + BN_EPS) * gamma + beta
        h = jax.nn.relu(h)
        return h @ W2.T + b2
    edge_index = jnp.stack([src, dst])
    h = jnp.maximum(_layernorm(x, axis=-1), 0.0)
    x = x + _L0_gnn_ref(h, edge_index, edge_type_9, 12500, L0_gnn_W_msg, L0_gnn_b_msg, L0_gnn_edge_embed, L0_gnn_W_ih, L0_gnn_W_hh, L0_gnn_b_ih, L0_gnn_b_hh)
    h = jnp.maximum(_layernorm(x, axis=-1), 0.0)
    x = x + _L1_gnn_ref(h, edge_index, L1_gnn_eps, L1_gnn_W1, L1_gnn_b1, L1_gnn_gamma, L1_gnn_beta, L1_gnn_W2, L1_gnn_b2)
    return x

_drawn_inputs = setup_inputs


def setup_inputs(seed=0):
    import zlib

    import numpy as np

    out = dict(_drawn_inputs(seed))
    spreads = {'L1_gnn_gamma': (1.0, 0.2), 'L1_gnn_beta': (0.0, 0.285)}
    factors = {'L0_gnn_b_ih': 6.479, 'L0_gnn_b_hh': 7.439, 'L1_gnn_b1': 8.0}
    for name, (base, spread) in spreads.items():
        noise = np.random.default_rng([zlib.crc32(name.encode()), seed]).standard_normal(out[name].shape)
        drawn = base * np.exp(spread * noise) if base else spread * noise
        out[name] = jnp.asarray(drawn.astype(out[name].dtype))
    for name, factor in factors.items():
        out[name] = (out[name] * factor).astype(out[name].dtype)
    return out
```

```python
from contextlib import ExitStack

import concourse.bass as bass
from concourse import mybir

N, F, E, TYPES = 12500, 128, 212500, 9
P = 128
BLOCKS = -(-N // P)
NPAD = BLOCKS * P
COLS = 1664
EPAD = COLS * P
TILES = EPAD // P
STEPS = E // P + BLOCKS
CH = 16
PAIRS = -(-STEPS // (2 * CH))
CHUNKS = 2 * PAIRS
STEPS_P = CHUNKS * CH
G = 4
GPC = CH // G
GROUPS = STEPS_P // G
SB = -(-STEPS_P // P)
SW = SB * P
RW = 136
KEY = F
FAR = 255.0
NBK = BLOCKS + 1
PADNODE = BLOCKS * P
LNG = 7
LNW = LNG * P
LN_TURNS = BLOCKS // LNG
NG = 2
GW = NG * P
TURNS = BLOCKS // NG
ROWS_D = STEPS_P * P
SKIP = 1 << 20
LN_EPS = 1e-5
BN_EPS = 1e-5
CF = {}
for _name, _width in (("ident", P), ("ones", P), ("before", P), ("iota", P), ("iota_p", 1), ("thr", NBK),
                      ("blk", NBK), ("step", SB), ("lneps", 1), ("bneps", 1), ("pad", RW), ("blk4", NBK * G)):
    CF[_name] = (sum(w for _, w in CF.values()), _width)
CF_W = sum(w for _, w in CF.values())


def build_gnn(nc, x, edges, dst_next, weights, bias_cols, embed, b_msg, b2, eps1, consts, out):
    f32, i32, bf16 = mybir.dt.float32, mybir.dt.int32, mybir.dt.bfloat16
    ALU, ACT, AX = mybir.AluOpType, mybir.ActivationFunctionType, mybir.AxisListType
    ds = bass.ds
    ctx = ExitStack()
    with ctx:
        ctx.enter_context(nc.allow_non_contiguous_dma(reason="small step tables"))
        ctx.enter_context(nc.allow_low_precision(reason="sums of indices into int32: exact below 2**24"))

        def sb(name, shape, dt=f32):
            return ctx.enter_context(nc.sbuf_tensor("sb_" + name, shape, dt))

        held = {}

        def S(name):
            if name not in held:
                held[name] = ctx.enter_context(nc.semaphore(name))
            return held[name]

        def wait(engine, name, value):
            if not isinstance(value, int) or value > 0:
                engine.wait_ge(S(name), value)

        def plain(engine):
            engine.sem_inc(S("passed"), 1)

        table_d = nc.dram_tensor("msg_table", (TYPES * NPAD, F), f32).ap()
        packed_d = nc.dram_tensor("packed_edges", (TILES, P), i32).ap()
        blockrow_d = nc.dram_tensor("step_block_offsets", (2, SW), i32).ap()
        loc_d = nc.dram_tensor("step_targets", (SW, P), bf16).ap()
        rows_d = nc.dram_tensor("rows_by_src", (ROWS_D, RW), f32).ap()
        x1_d = nc.dram_tensor("x_after_layer0", (NPAD, F), f32).ap()

        H = sb("H", [P, NPAD])
        Y = sb("Y", [P, NPAD + (G - 1) * P])
        ring = sb("ring", [P, 2 * CH, RW])
        oh = sb("oh", [P, 2, CH, P])
        locE = sb("locE", [P, SW])
        tabE = sb("tabE", [P, SW])
        skeyE = sb("skeyE", [P, SW])
        sblkE = sb("sblkE", [P, SW], bf16)
        posE = sb("posE", [P, STEPS_P], i32)
        steprow = sb("steprow", [1, STEPS_P], i32)
        idxslot = sb("idxslot", [P, 2, CH], i32)
        cf = sb("cf", [P, CF_W])
        ones_b = sb("ones_b", [P, P], bf16)
        before_b = sb("before_b", [P, P], bf16)
        rest_b = sb("rest_b", [P, P], bf16)
        zeros_b = sb("zeros_b", [P, 512], bf16)
        blk4_b = sb("blk4_b", [P, NBK, G], bf16)
        blk1h = sb("blk1h", [P, G, NBK, G], bf16)
        ranked = sb("ranked", [P, 2, NBK, G])
        wT = sb("wT", [P, 9, P])
        embb = sb("embb", [P, TYPES, P])
        bmsgb = sb("bmsgb", [P, P])
        b2row = sb("b2row", [1, P])
        bcol = sb("bcol", [P, 9])
        scol = sb("scol", [P, 12])
        smalls = sb("smalls", [P, 2100])
        flag = sb("flag", [1, 1], i32)
        lastrow = sb("lastrow", [1, 2, 2, BLOCKS], i32)
        ps = ctx.enter_context(nc.psum_tensor("ps", [P, 8, 512], f32))

        def const(name):
            a, w = CF[name]
            return cf[:, a:a + w]

        ident, ones_f, iota_f, iota_p = const("ident"), const("ones"), const("iota"), const("iota_p")

        def yv(k, dt):
            return Y[:, k * COLS:(k + 1) * COLS].bitcast(dt) if dt is not f32 else Y[:, k * COLS:(k + 1) * COLS]

        raw_dst, raw_src, raw_typ, packed, nxt = (yv(k, i32) for k in range(5))
        dblk, sblk = yv(5, bf16)[:, 0:COLS], yv(5, bf16)[:, COLS:2 * COLS]
        junk_v, junk_a = yv(6, bf16)[:, 0:COLS], yv(6, bf16)[:, COLS:2 * COLS]
        viol = ring[:, :, :].rearrange("p a b -> p (a b)")[:, 0:COLS]
        blktmp = oh[:, :, :, :].rearrange("p a b c -> p (a b c)")[:, 2048:2048 + SB * (BLOCKS - 1)] \
            .rearrange("p (s b) -> p s b", s=SB)
        fld = [Y[:, k * SW:(k + 1) * SW] for k in range(7)]
        fldi = [v.bitcast(i32) for v in fld]

        ringf = ring[:, :, :].rearrange("p a b -> p (a b)")
        ohf = oh[:, :, :, :].rearrange("p a b c -> p (a b c)")
        xbuf = [ringf[:, k * LNW:(k + 1) * LNW] for k in range(2)]
        hbuf = [ringf[:, (2 + k) * LNW:(3 + k) * LNW] for k in range(2)]
        hTs = [ohf[:, k * LNW:(k + 1) * LNW] for k in range(2)]
        TW = TYPES * P
        tabt = [ohf[:, 2 * LNW + k * TW:2 * LNW + (k + 1) * TW] for k in range(2)]

        def ob(k):
            return ohf[:, k * GW:(k + 1) * GW]

        rbuf, zbuf, tbuf, nbuf, hnbuf, cell_x = ([ob(2 * a + k) for k in range(2)] for a in range(6))
        hs = [ob(12 + k) for k in range(2)]
        locb = [ohf[:, k * 1024:(k + 1) * 1024].bitcast(bf16) for k in range(2)]
        pick = [ohf[:, 2048 + k * 512:2048 + (k + 1) * 512] for k in range(4)]
        fin_z, fin_x, fin_o = ([ob(2 * a + k) for k in range(2)] for a in range(3))

        at = [0]

        def small(n, dt=f32):
            v = smalls[:, at[0]:at[0] + n]
            at[0] += n
            return v if dt is f32 else v.bitcast(dt)

        part_d, part_s = small(NBK), small(NBK)
        start_d, start_s = small(NBK), small(NBK)
        lo_i = small(NBK, i32)
        first_d, first_s = small(NBK), small(NBK)
        base_s = small(NBK)
        bstep_d, bstep_s = small(SB), small(SB)
        boff_f = small(SB)
        boff_d, boff_s = small(SB, i32), small(SB, i32)
        tile_f, tile_i = small(SB), small(SB, i32)
        stats = small(LNG * 6)
        mv = small(LNG * 2)
        sd = small(LNG)
        rstd = [small(LNG) for _ in range(2)]
        nbias = [small(LNG) for _ in range(2)]
        mvn = small(BLOCKS * 2)
        sdn, rstdn, nbn = small(BLOCKS), small(BLOCKS), small(BLOCKS)
        fsum = small(TURNS)
        lastf = small(BLOCKS)
        lasti = [small(BLOCKS, i32) for _ in range(2)]
        possl = small(G, i32)
        paysl = small(G, i32)
        vcol = scol[:, 0:1]
        one_eps, brz = scol[:, 1:2], scol[:, 2:4]
        negmu, sq, bsd, brs, scale_c, shift_c, msum = (scol[:, k:k + 1] for k in range(4, 11))

        def bank(k):
            return ps[:, k, :]

        rank_ps = ps[:, 0, 0:NBK * G].rearrange("p (b q) -> p b q", q=G)

        block = ctx.enter_context(nc.Block())

        def rank_before(n_slot):
            o = blk1h[:, n_slot, :, :]
            nc.tensor.matmul(rank_ps, before_b[:, :], o, start=False, stop=True, skip_group_check=True)
            for q in range(G - 1):
                m = nc.tensor.matmul(rank_ps[:, :, q + 1:G], ones_b[:, :],
                                     o[:, :, q:q + 1].to_broadcast([P, NBK, G - 1 - q]),
                                     start=False, stop=True, skip_group_check=True)
            return m

        def rank_after(n_slot):
            o = blk1h[:, n_slot, :, :]
            nc.tensor.matmul(rank_ps, rest_b[:, :], o, start=False, stop=True, skip_group_check=True)
            for q in range(1, G):
                m = nc.tensor.matmul(rank_ps[:, :, 0:q], ones_b[:, :],
                                     o[:, :, q:q + 1].to_broadcast([P, NBK, q]),
                                     start=False, stop=True, skip_group_check=True)
            return m

        @block.sync
        def _(sp):
            sp.dma_start(cf[:, :], consts).then_inc(S("consts_in"), 16)
            for k in range(3):
                sp.dma_start((raw_dst, raw_src, raw_typ)[k], edges[k]).then_inc(S("edges_in"), 16)
            sp.dma_start(nxt, dst_next).then_inc(S("edges_in"), 16)
            xv = x.rearrange("(b p) f -> p b f", p=P)

            def load_x(i, k):
                sp.dma_start(xbuf[k].rearrange("p (b f) -> p b f", f=F), xv[:, ds(i * LNG, LNG), :]) \
                    .then_inc(S(f"x_in{k}"), 16)

            sp.dma_start(wT[:, :, :], weights.rearrange("p (a b) -> p a b", a=9)).then_inc(S("w_in"), 16)
            sp.dma_start(bcol[:, :], bias_cols).then_inc(S("w_in"), 16)
            sp.dma_start(embb[:, :, :].rearrange("p t f -> p (t f)"),
                         embed.rearrange("(a t) f -> a (t f)", a=1).to_broadcast([P, TYPES * F])).then_inc(S("w_in"), 16)
            sp.dma_start(bmsgb[:, :], b_msg.rearrange("(a f) -> a f", a=1).to_broadcast([P, F])).then_inc(S("w_in"), 16)
            sp.dma_start(b2row[:, :], b2.rearrange("(a f) -> a f", a=1)).then_inc(S("w_in"), 16)
            sp.dma_start(one_eps, eps1.to_broadcast([P, 1])).then_inc(S("w_in"), 16)

            sp.wait_ge(S("flag_set"), 1)
            unsorted = sp.value_load(flag[0:1, 0:1], min_val=0, max_val=1)
            with sp.If(unsorted == 0):
                sp.dma_start(packed_d.rearrange("(p a) b -> p (a b)", p=P), packed).then_inc(S("packed_out"), 16)

            sp.wait_ge(S("step_tables"), 1)
            rv = blockrow_d.rearrange("a (s p) -> p a s", p=P)
            sp.dma_start(rv[:, 0, :], boff_d).then_inc(S("rows_out"), 16)
            sp.dma_start(rv[:, 1, :], boff_s).then_inc(S("rows_out"), 16)
            sp.wait_ge(S("rows_out"), 32)
            sp.dma_start(steprow[:, :], blockrow_d[0:1, 0:STEPS_P]).then_inc(S("steprow_in"), 16)

            def table_out(j, k):
                tv = table_d.rearrange("(t b p) f -> b p t f", p=P, b=BLOCKS)
                for b in range(LNG):
                    slot = (k + b) % 2
                    sp.wait_ge(S("tab_ready"), (j * 2 + k) * LNG + b + 1)
                    sp.dma_start(tv[ds((j * 2 + k) * LNG + b, 1), :, :, :].rearrange("a p t f -> (a p) t f"),
                                 tabt[slot].rearrange("p (t f) -> p t f", f=F)).then_inc(S(f"tab_out{slot}"), 16)

            sp.wait_ge(S("viol_read"), 1)
            load_x(0, 0)
            load_x(1, 1)
            sp.wait_ge(S("blocks_found"), 1)
            with sp.Fori(0, LN_TURNS // 2 - 1) as j:
                for k in range(2):
                    sp.wait_ge(S("h_ready"), j * 2 + k + 1)
                    load_x(j * 2 + 2 + k, k)
                    table_out(j, k)
            for k in range(2):
                table_out(LN_TURNS // 2 - 1, k)

            sp.wait_ge(S("loc_ready"), 1)
            sp.dma_start(loc_d.rearrange("(s p) e -> p s e", p=P),
                         fld[1].bitcast(bf16)[:, 0:SW].rearrange("p (s e) -> p s e", e=P)).then_inc(S("loc_out"), 16)

            pad_v = rows_d.rearrange("(c p k) w -> c k p w", p=P, k=CH)
            for t in (STEPS, STEPS + 1):
                sp.dma_start(pad_v[t // CH, t % CH], const("pad")).then_inc(S("pads_out"), 16)
            flat_v = rows_d.rearrange("(c p k) w -> c p (k w)", p=P, k=CH)
            wait(sp, "pads_out", 32)

            def pad_tiles(b):
                for a in range(2):
                    c = sp.value_load(lastrow[0:1, a, 0, ds(b, 1)], min_val=0, max_val=CHUNKS - 1)
                    q = sp.value_load(lastrow[0:1, a, 1, ds(b, 1)], min_val=0, max_val=CH - 1)
                    sp.dma_start(flat_v[ds(c, 1), :, ds(q * RW, RW)].rearrange("a p w -> (a p) w"), const("pad")) \
                        .then_inc(S("pads_out"), 16)
                    sp.wait_ge(S("pads_out"), (b * 2 + a) * 16 + 48)
                    plain(sp)

            with sp.Fori(0, BLOCKS) as b:
                pad_tiles(b)

            sp.wait_ge(S("agg_done"), GROUPS)

            def cell_in(i, k):
                sp.dma_start(cell_x[k].rearrange("p (b f) -> p b f", f=F), xv[:, ds(i * NG, NG), :]) \
                    .then_inc(S(f"cell_x{k}"), 16)

            def x1_out(i):
                x1v = x1_d.rearrange("(b p) f -> p b f", p=P)
                sp.wait_ge(S("x1_ready"), i + 1)
                sp.dma_start(x1v[:, ds(i * NG, NG), :], H[:, ds(i * GW, GW)].rearrange("p (b f) -> p b f", f=F)) \
                    .then_inc(S("x1_out"), 16)

            cell_in(0, 0)
            cell_in(1, 1)
            with sp.Fori(0, (TURNS - 3) // 2) as j:
                for k in range(2):
                    x1_out(j * 2 + k)
                    cell_in(j * 2 + k + 2, k)
            x1_out(TURNS - 3)
            cell_in(TURNS - 1, 0)
            x1_out(TURNS - 2)
            x1_out(TURNS - 1)
            sp.wait_ge(S("x1_out"), TURNS * 16)
            nc.sync.sem_inc(S("x1_stored"), 1)

            def loc_in(c, k):
                sp.dma_start(locb[k], loc_d.rearrange("(a s) e -> a (s e)", s=CH)[ds(c, 1), :].to_broadcast([P, CH * P])) \
                    .then_inc(S(f"locb_in{k}"), 16)

            sp.wait_ge(S("h2_done"), TURNS)
            sp.wait_ge(S("loc_out"), 16)
            loc_in(0, 0)
            loc_in(1, 1)
            with sp.Fori(1, PAIRS) as j:
                for k in range(2):
                    sp.wait_ge(S("pick_oh"), (j * 2 + k - 1) * GPC)
                    loc_in(j * 2 + k, k)

            sp.wait_ge(S("picked"), GROUPS)
            sp.dma_start(steprow[:, :], blockrow_d[1:2, 0:STEPS_P]).then_inc(S("steprow_in"), 16)
            for k in range(2):
                sp.wait_ge(S(f"scattered{k}"), PAIRS * CH * 16)

            def rows_in(c, k):
                sp.dma_start(ring[:, k * CH:(k + 1) * CH, :].rearrange("p a w -> p (a w)"),
                             rows_d.rearrange("(c p k) w -> c p (k w)", p=P, k=CH)[ds(c, 1), :, :]
                             .rearrange("a p w -> (a p) w")).then_inc(S(f"rows_in{k}"), 16)

            rows_in(0, 0)
            rows_in(1, 1)
            with sp.Fori(1, PAIRS) as j:
                for k in range(2):
                    sp.wait_ge(S("sum_done"), (j * 2 + k - 1) * GPC)
                    rows_in(j * 2 + k, k)

            x1v = x1_d.rearrange("(b p) f -> p b f", p=P)
            ov = out.rearrange("(b p) f -> p b f", p=P)
            sp.wait_ge(S("sum_added"), GROUPS)

            def fin_in(i, k):
                sp.dma_start(fin_x[k].rearrange("p (b f) -> p b f", f=F), x1v[:, ds(i * NG, NG), :]) \
                    .then_inc(S(f"fin_x{k}"), 16)

            def fin_out(i, k):
                sp.wait_ge(S("out_ready"), i + 1)
                sp.dma_start(ov[:, ds(i * NG, NG), :], fin_o[k].rearrange("p (b f) -> p b f", f=F)) \
                    .then_inc(S(f"out_done{k}"), 16)

            fin_in(0, 0)
            fin_in(1, 1)
            with sp.Fori(0, (TURNS - 3) // 2) as j:
                for k in range(2):
                    fin_out(j * 2 + k, k)
                    fin_in(j * 2 + k + 2, k)
            fin_out(TURNS - 3, 0)
            fin_in(TURNS - 1, 0)
            fin_out(TURNS - 2, 1)
            fin_out(TURNS - 1, 0)
            sp.wait_ge(S("out_done0"), (TURNS + 1) // 2 * 16)
            sp.wait_ge(S("out_done1"), TURNS // 2 * 16)

        @block.gpsimd
        def _(pool):
            pool.wait_ge(S("flag_set"), 1)
            unsorted = pool.value_load(flag[0:1, 0:1], min_val=0, max_val=1)
            with pool.If(unsorted == 0):
                pool.wait_ge(S("packed_out"), 16)
            with pool.If(unsorted != 0):
                with pool.Fori(0, COLS // G) as n:
                    pool.wait_ge(S("sort_pos"), n + 1)
                    plain(pool)
                    for q in range(G):
                        pool.indirect_dma_start(
                            out=packed_d.rearrange("a (b c) -> (a b) c", c=1),
                            out_offset=bass.IndirectOffsetOnAxis(ap=possl[:, q:q + 1], axis=0),
                            in_=paysl[:, q:q + 1], in_offset=None).then_inc(S("sorted_out"), 16)
                    pool.wait_ge(S("sorted_out"), (n + 1) * (G * 16))
                    nc.gpsimd.sem_inc(S("sort_sent"), 1)
            pool.wait_ge(S("step_tables"), 1)
            for s in range(SB):
                pool.indirect_dma_start(out=fldi[0][:, s * P:(s + 1) * P], out_offset=None, in_=packed_d[:, :],
                                        in_offset=bass.IndirectOffsetOnAxis(ap=tile_i[:, s:s + 1], axis=0)) \
                    .then_inc(S("tiles_in"), 16)
            def keep_h(i, k):
                pool.wait_ge(S("hT_ready"), i + 1)
                nc.gpsimd.tensor_copy(H[:, ds(i * LNW, LNW)], hTs[k]).then_inc(S("hT_kept"), 1)

            with pool.Fori(0, LN_TURNS // 2) as j:
                for k in range(2):
                    keep_h(j * 2 + k, k)

            for k in range(2):
                pool.wait_ge(S(f"tab_out{k}"), BLOCKS // 2 * 16)

            def gather(j, k):
                wait(pool, "agg_done", (j * 2 + k - 1) * GPC)
                pool.wait_ge(S("idx_ready"), j * 2 + k + 1)
                plain(pool)
                for q in range(CH):
                    pool.indirect_dma_start(out=ring[:, k * CH + q, 0:F], out_offset=None, in_=table_d[:, :],
                                            in_offset=bass.IndirectOffsetOnAxis(ap=idxslot[:, k, q:q + 1], axis=0)) \
                        .then_inc(S(f"gathered{k}"), 16)

            for k in range(2):
                gather(0, k)
            with pool.Fori(1, PAIRS) as j:
                for k in range(2):
                    gather(j, k)

            def keep_h2(i, k):
                pool.wait_ge(S("h2_ready"), i + 1)
                nc.gpsimd.tensor_copy(H[:, ds(i * GW, GW)], hs[k]).then_inc(S("h2_kept"), 1)

            keep_h2(0, 0)
            with pool.Fori(0, (TURNS - 1) // 2) as j:
                for k in range(2):
                    keep_h2(j * 2 + k + 1, (k + 1) % 2)

            def scatter(j, k):
                pool.wait_ge(S("keyed"), j * 2 + k + 1)
                for g in range(GPC):
                    pool.wait_ge(S("row_moved"), (j * 2 + k) * GPC + g + 1)
                    plain(pool)
                    for q in range(G):
                        s = g * G + q
                        pool.indirect_dma_start(
                            out=rows_d[:, :], out_offset=bass.IndirectOffsetOnAxis(ap=idxslot[:, k, s:s + 1], axis=0),
                            in_=ring[:, k * CH + s, :], in_offset=None,
                            bounds_check=ROWS_D - 1, oob_is_err=False).then_inc(S(f"scattered{k}"), 16)

            pool.wait_ge(S("pads_out"), (2 * BLOCKS + 2) * 16)
            with pool.Fori(0, PAIRS) as j:
                for k in range(2):
                    scatter(j, k)

        @block.scalar
        def _(act):
            act.wait_ge(S("blocks_ready"), 2)
            with act.Fori(0, NBK) as b:
                nc.scalar.activation(junk_a, sblk, ACT.Sign, bias=cf[:, ds(b + CF["thr"][0], 1)], scale=-1.0,
                                     accum_out=part_s[:, ds(b, 1)]).then_inc(S("hist_s"), 1)
                act.wait_ge(S("hist_s"), b + 1)

            def norm0(j, k):
                i = j * 2 + k
                act.wait_ge(S("stats_ready"), i + 1)
                nc.scalar.activation(sd, mv.rearrange("p (b t) -> p b t", t=2)[:, :, 1], ACT.Sqrt,
                                     bias=const("lneps")).then_inc(S("sd_ready"), 1)
                act.wait_ge(S("rstd_ready"), i + 1)
                wait(act, "hT_ps", i - 1)
                for b in range(LNG):
                    o = nc.scalar.activation(hbuf[k][:, b * P:(b + 1) * P], xbuf[k][:, b * P:(b + 1) * P], ACT.Relu,
                                             bias=nbias[k][:, b:b + 1], scale=rstd[k][:, b:b + 1])
                o.then_inc(S("h_ready"), 1)
                act.wait_ge(S("hT_ps"), i + 1)
                wait(act, "hT_kept", i - 1)
                wait(act, "m_ready", i - 1)
                nc.scalar.copy(hTs[k][:, 0:512], bank(2 * k))
                nc.scalar.copy(hTs[k][:, 512:LNW], bank(2 * k + 1)[:, 0:LNW - 512]).then_inc(S("hT_ready"), 1)

            for k in range(2):
                norm0(0, k)
            with act.Fori(1, LN_TURNS // 2) as j:
                for k in range(2):
                    norm0(j, k)

            for f, dst_t in enumerate((tabE, locE, None)):
                for a in range(4):
                    w = min(512, SW - a * 512)
                    act.wait_ge(S("fields_T"), f * 4 + a + 1)
                    o = dst_t[:, a * 512:a * 512 + w] if dst_t is not None else fldi[2][:, a * 512:a * 512 + w]
                    nc.scalar.copy(o, bank((f % 2) * 4 + a)[:, 0:w]).then_inc(S("fields_moved"), 1)

            def gates(i, k):
                act.wait_ge(S("gates_ps"), i + 1)
                nc.scalar.activation(rbuf[k], bank(2 * k)[:, 0:GW], ACT.Sigmoid, bias=brz[:, 0:1])
                nc.scalar.activation(zbuf[k], bank(2 * k)[:, GW:2 * GW], ACT.Sigmoid, bias=brz[:, 1:2]).then_inc(S("gates_rz"), 1)

            def candidate(i, k):
                act.wait_ge(S("cand_in"), i + 1)
                nc.scalar.activation(nbuf[k], tbuf[k], ACT.Tanh, bias=bcol[:, 2:3]).then_inc(S("cand"), 1)

            act.wait_ge(S("agg_added"), GROUPS)
            act.wait_ge(S("brz_set"), 1)
            gates(0, 0)
            with act.Fori(0, (TURNS - 1) // 2) as j:
                for k in range(2):
                    gates(j * 2 + k + 1, (k + 1) % 2)
                    candidate(j * 2 + k, k)
            candidate(TURNS - 1, 0)

            act.wait_ge(S("x1_ready"), TURNS)
            nc.scalar.activation(sdn, mvn.rearrange("p (b t) -> p b t", t=2)[:, :, 1], ACT.Sqrt,
                                 bias=const("lneps")).then_inc(S("sdn_ready"), 1)
            act.wait_ge(S("rstdn_ready"), 1)
            act.wait_ge(S("x1_stored"), 1)

            def norm1(i, k):
                wait(act, "h2_kept", i - 1)
                wait(act, "h2_ps", i - 1)
                for b in range(NG):
                    o = nc.scalar.activation(hs[k][:, b * P:(b + 1) * P], H[:, ds(i * GW + b * P, P)], ACT.Relu,
                                             bias=nbn[:, ds(i * NG + b, 1)], scale=rstdn[:, ds(i * NG + b, 1)])
                o.then_inc(S("h2_ready"), 1)

            norm1(0, 0)
            norm1(1, 1)
            with act.Fori(0, (TURNS - 3) // 2) as j:
                for k in range(2):
                    norm1(j * 2 + k + 2, k)
            norm1(TURNS - 1, 0)

            def move_rows(j, k):
                wait(act, f"scattered{k}", j * (CH * 16))
                for g in range(GPC):
                    act.wait_ge(S("picked"), (j * 2 + k) * GPC + g + 1)
                    nc.scalar.copy(ring[:, k * CH + g * G:k * CH + (g + 1) * G, 0:F],
                                   bank(g).rearrange("p (q f) -> p q f", f=F)).then_inc(S("row_moved"), 1)

            act.wait_ge(S("ring_cleared"), 1)
            for k in range(2):
                move_rows(0, k)
            with act.Fori(1, PAIRS) as j:
                for k in range(2):
                    move_rows(j, k)

            def lin1(i, k, w):
                act.wait_ge(S("lin1_ps"), i + 1)
                nc.scalar.activation(Y[:, ds(i * GW, w)], bank(4 + k)[:, 0:w], ACT.Identity, bias=bcol[:, 6:7],
                                     accum_out=fsum[:, ds(i, 1)]).then_inc(S("lin1"), 1)

            with act.Fori(0, (TURNS - 1) // 2) as j:
                for k in range(2):
                    lin1(j * 2 + k, k, GW)
            lin1(TURNS - 1, 0, N - (TURNS - 1) * GW)
            act.wait_ge(S("negmu_ready"), 1)
            nc.scalar.activation(H[:, 0:N], Y[:, 0:N], ACT.Square, bias=negmu, accum_out=sq).then_inc(S("sq_ready"), 1)
            act.wait_ge(S("sq_scaled"), 1)
            nc.scalar.activation(bsd, sq, ACT.Sqrt, bias=const("bneps"), scale=1.0 / N).then_inc(S("bsd_ready"), 1)
            act.wait_ge(S("bn_ready"), 1)

            def bn_relu(i, k):
                wait(act, "lin2_ps", i - 1)
                nc.scalar.activation(fin_z[k], Y[:, ds(i * GW, GW)], ACT.Relu, bias=shift_c, scale=scale_c) \
                    .then_inc(S("z_ready"), 1)

            bn_relu(0, 0)
            bn_relu(1, 1)
            with act.Fori(0, (TURNS - 3) // 2) as j:
                for k in range(2):
                    bn_relu(j * 2 + k + 2, k)
            bn_relu(TURNS - 1, 0)

        @block.vector
        def _(dve):
            vs = nc.vector
            seq = [0]

            def link(ins):
                seq[0] += 1
                ins.then_inc(S("dve_seq"), 1)
                dve.wait_ge(S("dve_seq"), seq[0])

            dve.wait_ge(S("consts_in"), 16)
            vs.tensor_copy(ones_b[:, :], ones_f)
            vs.tensor_copy(before_b[:, :], const("before"))
            link(vs.tensor_copy(blk4_b[:, :, :], const("blk4").rearrange("p (b q) -> p b q", q=G)))
            vs.tensor_tensor(rest_b[:, :], ones_b[:, :], before_b[:, :], ALU.subtract)
            vs.memset(zeros_b[:, :], 0.0)

            dve.wait_ge(S("edges_in"), 64)
            packed_f = packed.bitcast(f32)
            link(vs.tensor_tensor(viol, raw_dst, nxt, ALU.is_gt))
            link(vs.tensor_reduce(vcol, viol, axis=AX.X, op=ALU.add))
            link(vs.tensor_scalar(nxt, raw_dst, 7, None, ALU.logical_shift_right))
            vs.tensor_copy(dblk, nxt).then_inc(S("blocks_ready"), 1)
            link(vs.tensor_scalar(packed, raw_src, 7, None, ALU.logical_shift_right))
            vs.tensor_copy(sblk, packed).then_inc(S("blocks_ready"), 1)
            dve.wait_ge(S("blocks_ready"), 2)
            link(vs.tensor_scalar(packed, raw_src, 18, None, ALU.logical_shift_left))
            link(vs.tensor_scalar(nxt, raw_dst, 4, None, ALU.logical_shift_left))
            link(vs.tensor_tensor(packed, packed, nxt, ALU.bitwise_or))
            link(vs.tensor_scalar(raw_typ, raw_typ, 0.0, float(TYPES - 1), ALU.max, ALU.min))
            link(vs.tensor_tensor(packed, packed, raw_typ, ALU.bitwise_or))
            dve.wait_ge(S("viol_ps"), 1)
            link(vs.tensor_scalar(lo_i[0:1, 0:1], bank(7)[0:1, 0:1], 0.0, None, ALU.is_gt))
            vs.tensor_copy(flag[:, :], lo_i[0:1, 0:1]).then_inc(S("flag_set"), 1)
            vs.tensor_copy(scol[:, 11:12], vcol).then_inc(S("viol_read"), 1)

            with dve.Fori(0, NBK) as b:
                vs.tensor_scalar(junk_v, dblk, cf[:, ds(b + CF["thr"][0], 1)], 0.0, ALU.is_lt, ALU.add,
                                 accum_out=part_d[:, ds(b, 1)]).then_inc(S("hist_d"), 1)
                dve.wait_ge(S("hist_d"), b + 1)
            dve.wait_ge(S("starts_ps"), 1)
            vs.tensor_copy(start_d, bank(6)[:, 0:NBK])
            link(vs.tensor_scalar(start_s, bank(6)[:, NBK:2 * NBK], float(EPAD), 0.5, ALU.add, ALU.mult))
            for st, first in ((start_d, first_d), (start_s, first_s)):
                link(vs.tensor_copy(lo_i, st))
                link(vs.tensor_scalar(lo_i, lo_i, 7, None, ALU.logical_shift_right))
                link(vs.tensor_tensor(first, lo_i, const("blk"), ALU.add))
            vs.tensor_scalar(base_s, first_s, float(P), None, ALU.mult)
            for first, bstep in ((first_d, bstep_d), (first_s, bstep_s)):
                link(vs.tensor_tensor(blktmp, const("step").unsqueeze(2).to_broadcast([P, SB, BLOCKS - 1]),
                                      first[:, 1:BLOCKS].unsqueeze(1).to_broadcast([P, SB, BLOCKS - 1]), ALU.is_ge))
                link(vs.tensor_reduce(bstep, blktmp, axis=AX.X, op=ALU.add))
            vs.tensor_scalar(boff_s, bstep_s, float(P), None, ALU.mult)
            vs.tensor_scalar(boff_d, bstep_d, float(P), None, ALU.mult)
            vs.tensor_scalar(boff_f, bstep_d, float(P), None, ALU.mult)
            link(vs.tensor_tensor(tile_f, const("step"), bstep_d, ALU.subtract))
            link(vs.tensor_scalar(tile_i, tile_f, float(TILES - 1), None, ALU.min))
            link(vs.tensor_scalar(lasti[0][0:1, :], first_s[0:1, 1:NBK], -1.0, None, ALU.add))
            link(vs.tensor_scalar(lasti[1][0:1, :], first_s[0:1, 1:NBK], -2.0, 0.0, ALU.add, ALU.max))
            for a in range(2):
                vs.tensor_scalar(lastrow[0:1, a, 0, :], lasti[a][0:1, :], 4, None, ALU.logical_shift_right)
                vs.tensor_scalar(lastrow[0:1, a, 1, :], lasti[a][0:1, :], CH - 1, None, ALU.bitwise_and)
            vs.tensor_copy(lastf[0:1, 0:1], first_s[0:1, 0:1]).then_inc(S("blocks_found"), 1)

            unsorted = dve.value_load(flag[0:1, 0:1], min_val=0, max_val=1)
            with dve.If(unsorted != 0):
                dve.wait_ge(S("hist_d"), NBK)
                with dve.Fori(0, COLS // G) as n:
                    vs.tensor_tensor(blk1h[:, 0, :, :], dblk[:, ds(n * G, G)].unsqueeze(1).to_broadcast([P, NBK, G]),
                                     blk4_b[:, :, :], ALU.is_equal).then_inc(S("sort_oh"), 1)
                    dve.wait_ge(S("sort_ps"), n + 1)
                    vs.tensor_tensor(ranked[:, 0, :, :], rank_ps, blk1h[:, 0, :, :], ALU.mult).then_inc(S("sort_mul"), 1)
                    dve.wait_ge(S("sort_mul"), n + 1)
                    vs.tensor_reduce(possl, ranked[:, 0, :, :].rearrange("p b q -> p q b"), axis=AX.X, op=ALU.add)
                    vs.tensor_copy(paysl, packed[:, ds(n * G, G)]).then_inc(S("sort_pos"), 1)
                    dve.wait_ge(S("sort_sent"), n + 1)
                    dve.wait_ge(S("sort_after"), n + 1)
            vs.tensor_copy(lastf[0:1, 1:2], first_s[0:1, 0:1]).then_inc(S("step_tables"), 1)

            dve.wait_ge(S("w_in"), 96)
            vs.tensor_tensor(embb[:, :, :], embb[:, :, :], bmsgb[:, :].unsqueeze(1).to_broadcast([P, TYPES, P]), ALU.add)
            vs.tensor_scalar(one_eps, one_eps, 1.0, None, ALU.add)
            link(vs.tensor_tensor(brz, bcol[:, 0:2], bcol[:, 3:5], ALU.add))
            vs.tensor_copy(lastf[:, 2:3], brz[:, 0:1]).then_inc(S("brz_set"), 1)

            mvv = mv.rearrange("p (b t) -> p b t", t=2)

            def norm_stats(j, k):
                i = j * 2 + k
                dve.wait_ge(S(f"x_in{k}"), j * 16 + 16)
                wait(dve, "sd_ready", i)
                plain(dve)
                for b in range(LNG):
                    o = vs.bn_stats(stats[:, b * 6:(b + 1) * 6], xbuf[k][:, b * P:(b + 1) * P])
                o.then_inc(S("bn1"), 1)
                dve.wait_ge(S("bn1"), i + 1)
                plain(dve)
                for b in range(LNG):
                    o = vs.bn_aggr(mv[:, 2 * b:2 * b + 2], stats[:, b * 6:(b + 1) * 6])
                o.then_inc(S("stats_ready"), 1)

            def norm_scale(j, k):
                i = j * 2 + k
                dve.wait_ge(S("sd_ready"), i + 1)
                wait(dve, "h_ready", i - 1)
                vs.reciprocal(rstd[k], sd).then_inc(S("rcp"), 1)
                dve.wait_ge(S("rcp"), i + 1)
                vs.scalar_tensor_tensor(out=nbias[k], in0=mvv[:, :, 0], scalar=-1.0, in1=rstd[k],
                                        op0=ALU.mult, op1=ALU.mult).then_inc(S("rstd_ready"), 1)

            def table_rows(j, k):
                i = j * 2 + k
                dve.wait_ge(S("m_ready"), i + 1)
                for b in range(LNG):
                    slot, n = (k + b) % 2, k * LNG + b
                    wait(dve, f"tab_out{slot}", j * (LNG * 16) + n // 2 * 16)
                    m = bank(4 + 2 * k + b // 4)[:, b % 4 * P:(b % 4 + 1) * P]
                    vs.tensor_tensor(tabt[slot].rearrange("p (t f) -> p t f", f=F),
                                     m.unsqueeze(1).to_broadcast([P, TYPES, P]), embb[:, :, :], ALU.add) \
                        .then_inc(S("tab_ready"), 1)

            norm_stats(0, 0)
            norm_scale(0, 0)
            norm_stats(0, 1)
            norm_scale(0, 1)
            table_rows(0, 0)
            with dve.Fori(1, LN_TURNS // 2) as j:
                norm_stats(j, 0)
                norm_scale(j, 0)
                table_rows(j - 1, 1)
                norm_stats(j, 1)
                norm_scale(j, 1)
                table_rows(j, 0)
            table_rows(LN_TURNS // 2 - 1, 1)

            dve.wait_ge(S("tiles_in"), SB * 16)
            LOC, TAB, SRC, VAL = fld[4], fld[5], fld[6], fld[3]
            v3 = lambda a: a.rearrange("p (s e) -> p s e", e=P)
            vs.tensor_scalar(fldi[1], fldi[0], 15, None, ALU.bitwise_and)
            link(vs.tensor_scalar(fldi[2], fldi[0], 18, None, ALU.logical_shift_right))
            vs.scalar_tensor_tensor(out=TAB, in0=fldi[1], scalar=float(NPAD), in1=fldi[2], op0=ALU.mult, op1=ALU.add) \
                .then_inc(S("field"), 1)
            dve.wait_ge(S("field"), 1)
            link(vs.tensor_scalar(fldi[1], fldi[0], 4, 16383, ALU.logical_shift_right, ALU.bitwise_and))
            link(vs.tensor_tensor(v3(LOC), v3(fldi[1]), boff_f.unsqueeze(2).to_broadcast([P, SB, P]), ALU.subtract))
            link(vs.tensor_scalar(VAL, LOC, 0.0, None, ALU.is_ge))
            link(vs.scalar_tensor_tensor(out=VAL, in0=LOC, scalar=float(P), in1=VAL, op0=ALU.is_lt, op1=ALU.mult))
            link(vs.scalar_tensor_tensor(out=LOC, in0=LOC, scalar=-FAR, in1=VAL, op0=ALU.add, op1=ALU.mult))
            link(vs.tensor_scalar(LOC, LOC, FAR, None, ALU.add))
            vs.tensor_copy(lastf[:, 3:4], LOC[:, 0:1]).then_inc(S("field"), 1)
            link(vs.scalar_tensor_tensor(out=SRC, in0=fldi[2], scalar=-16383.0, in1=VAL, op0=ALU.add, op1=ALU.mult))
            link(vs.tensor_scalar(SRC, SRC, 16383.0, None, ALU.add))
            vs.tensor_copy(lastf[:, 4:5], SRC[:, 0:1]).then_inc(S("field"), 1)
            vs.tensor_copy(fld[1].bitcast(bf16)[:, 0:SW], LOC).then_inc(S("loc_ready"), 1)

            def place_idx(c, k):
                vs.tensor_copy(idxslot[:, k, :], tabE[:, ds(c * CH, CH)]).then_inc(S("idx_ready"), 1)

            dve.wait_ge(S("fields_moved"), 4)
            place_idx(0, 0)
            place_idx(1, 1)
            dve.wait_ge(S("fields_moved"), 12)
            link(vs.tensor_scalar(fldi[3], fldi[2], 7, None, ALU.logical_shift_right))
            vs.tensor_copy(sblkE[:, :], fldi[3])
            link(vs.tensor_scalar(fldi[4], fldi[2], P - 1, None, ALU.bitwise_and))
            link(vs.tensor_copy(skeyE[:, :], fldi[4]))
            dve.wait_ge(S("loc_out"), 16)
            link(vs.memset(Y[:, :], 0.0))

            def step_onehots(c, k):
                wait(dve, "agg_done", (c - 1) * GPC)
                vs.tensor_tensor(oh[:, k, :, :], locE[:, ds(c * CH, CH)].unsqueeze(2).to_broadcast([P, CH, P]),
                                 iota_f.unsqueeze(1).to_broadcast([P, CH, P]), ALU.is_equal).then_inc(S("oh_ready"), 1)

            def block_onehots(n, slot):
                wait(dve, "rank_counted", n - 3)
                vs.tensor_tensor(blk1h[:, slot, :, :], sblkE[:, ds(n * G, G)].unsqueeze(1).to_broadcast([P, NBK, G]),
                                 blk4_b[:, :, :], ALU.is_equal).then_inc(S("blk_ready"), 1)

            regs = [dve.alloc_register(f"group_off{q}") for q in range(GPC)]

            def group_offsets(c):
                vs.load(regs, steprow[0:1, ds(c * CH, CH)].rearrange("p (g q) -> p g q", q=G)[:, :, 0])
                return [dve.snap(r, min_val=0, max_val=(BLOCKS - 1) * P) for r in regs]

            def layer0(j, k):
                c = j * 2 + k
                offs = group_offsets(c)
                for g in range(GPC):
                    n = c * GPC + g
                    dve.wait_ge(S("rank_ps"), n + 1)
                    vs.tensor_tensor(ranked[:, g % 2, :, :], rank_ps, blk1h[:, g, :, :], ALU.mult).then_inc(S("rank_read"), 1)
                    block_onehots(n + 1, (g + 1) % G)
                    dve.wait_ge(S("rank_read"), n + 1)
                    vs.tensor_reduce(posE[:, ds(n * G, G)], ranked[:, g % 2, :, :].rearrange("p b q -> p q b"),
                                     axis=AX.X, op=ALU.add)
                    if g == 1:
                        dve.wait_ge(S(f"gathered{k}"), j * (CH * 16) + CH * 16)
                        place_idx(c + 2, k)
                    if g == 2:
                        step_onehots(c + 1, 1 - k)
                    dve.wait_ge(S("agg_done"), n + 1)
                    wait(dve, "agg_added", n)
                    yb = Y[:, ds(offs[g], 512)]
                    vs.tensor_tensor(yb, yb, bank(1 + g), ALU.add).then_inc(S("agg_added"), 1)

            dve.wait_ge(S("steprow_in"), 16)
            dve.wait_ge(S("hT_kept"), LN_TURNS)
            for k in range(2):
                dve.wait_ge(S(f"tab_out{k}"), BLOCKS // 2 * 16)
            step_onehots(0, 0)
            block_onehots(0, 0)
            for k in range(2):
                layer0(0, k)
            with dve.Fori(1, PAIRS) as j:
                for k in range(2):
                    layer0(j, k)

            ta, tb = ringf[:, 0:STEPS_P].bitcast(i32), ringf[:, STEPS_P:2 * STEPS_P].bitcast(i32)
            dve.wait_ge(S("agg_added"), GROUPS)
            pe_, ta_, tb_ = posE[:, :], ta, tb
            vs.tensor_scalar(ta_, pe_, 127, 4, ALU.bitwise_and, ALU.logical_shift_left)
            link(vs.tensor_scalar(tb_, pe_, 7, CH - 1, ALU.logical_shift_right, ALU.bitwise_and))
            link(vs.tensor_tensor(ta_, ta_, tb_, ALU.bitwise_or))
            link(vs.tensor_scalar(tb_, pe_, 11, 11, ALU.logical_shift_right, ALU.logical_shift_left))
            link(vs.tensor_tensor(ta_, ta_, tb_, ALU.bitwise_or))
            link(vs.tensor_scalar(tb_, sblkE[:, 0:STEPS_P], float(BLOCKS), float(SKIP), ALU.is_ge, ALU.mult))
            link(vs.tensor_tensor(pe_, ta_, tb_, ALU.max))
            link(vs.memset(ringf, 0.0))
            vs.tensor_copy(lastf[:, 5:6], ringf[:, 0:1]).then_inc(S("ring_cleared"), 1)

            def cell_a(i, k):
                dve.wait_ge(S("gates_rz"), i + 1)
                wait(dve, "cand", i - 1)
                vs.scalar_tensor_tensor(out=tbuf[k], in0=bank(2 * k + 1)[:, GW:2 * GW], scalar=bcol[:, 5:6], in1=rbuf[k],
                                        op0=ALU.add, op1=ALU.mult).then_inc(S("cell_t"), 1)
                dve.wait_ge(S("cell_t"), i + 1)
                vs.tensor_tensor(tbuf[k], tbuf[k], bank(2 * k + 1)[:, 0:GW], ALU.add).then_inc(S("cand_in"), 1)

            def cell_b(i, k):
                dve.wait_ge(S("cand"), i + 1)
                wait(dve, "hn_ps", i - 1)
                vs.tensor_tensor(hnbuf[k], H[:, ds(i * GW, GW)], nbuf[k], ALU.subtract).then_inc(S("cell_h"), 1)
                dve.wait_ge(S("cell_h"), i * 2 + 1)
                vs.tensor_tensor(hnbuf[k], hnbuf[k], zbuf[k], ALU.mult).then_inc(S("cell_h"), 1)
                dve.wait_ge(S("cell_h"), i * 2 + 2)
                vs.tensor_tensor(hnbuf[k], hnbuf[k], nbuf[k], ALU.add).then_inc(S("hn_ready"), 1)

            def cell_c(i, k):
                dve.wait_ge(S("hn_ps"), i + 1)
                dve.wait_ge(S(f"cell_x{k}"), cell_count(i, k))
                hb = H[:, ds(i * GW, GW)]
                vs.tensor_tensor(hb, cell_x[k], bank(4 + k)[:, 0:GW], ALU.add).then_inc(S("x1_sum"), 1)
                dve.wait_ge(S("x1_sum"), i + 1)
                plain(dve)
                for b in range(NG):
                    o = vs.bn_stats(stats[:, b * 6:(b + 1) * 6], H[:, ds(i * GW + b * P, P)])
                o.then_inc(S("bn2"), 1)
                dve.wait_ge(S("bn2"), i + 1)
                plain(dve)
                for b in range(NG):
                    o = vs.bn_aggr(mv[:, 2 * b:2 * b + 2], stats[:, b * 6:(b + 1) * 6])
                o.then_inc(S("bn3"), 1)
                dve.wait_ge(S("bn3"), i + 1)
                vs.tensor_copy(mvn[:, ds(i * 2 * NG, 2 * NG)], mv[:, 0:2 * NG]).then_inc(S("x1_ready"), 1)

            cell_a(0, 0)
            cell_a(1, 1)
            cell_b(0, 0)
            with dve.Fori(0, (TURNS - 3) // 2) as j:
                for k in range(2):
                    i = j * 2 + k + 2

                    def cell_count(t, kk, j=j, k=k):
                        return j * 16 + 16
                    cell_a(i, k)
                    cell_b(i - 1, (k + 1) % 2)
                    cell_c(i - 2, k)

            def cell_count(t, kk):
                return (t // 2 + 1) * 16
            T = TURNS
            cell_a(T - 1, 0)
            cell_b(T - 2, 1)
            cell_c(T - 3, 0)
            cell_b(T - 1, 0)
            cell_c(T - 2, 1)
            cell_c(T - 1, 0)

            dve.wait_ge(S("sdn_ready"), 1)
            link(vs.reciprocal(rstdn, sdn))
            vs.scalar_tensor_tensor(out=nbn, in0=mvn.rearrange("p (b t) -> p b t", t=2)[:, :, 0], scalar=-1.0, in1=rstdn,
                                    op0=ALU.mult, op1=ALU.mult).then_inc(S("rstdn_ready"), 1)

            def h2_own(i, k):
                dve.wait_ge(S("h2_ps"), i + 1)
                vs.tensor_scalar(Y[:, ds(i * GW, GW)], bank(k)[:, 0:GW], one_eps, None, ALU.mult).then_inc(S("h2_done"), 1)

            h2_own(0, 0)
            with dve.Fori(0, (TURNS - 1) // 2) as j:
                for k in range(2):
                    h2_own(j * 2 + k + 1, (k + 1) % 2)

            dve.wait_ge(S("h2_kept"), TURNS)
            def layer1_pick(j, k):
                c = j * 2 + k
                wait(dve, f"scattered{k}", j * (CH * 16))
                vs.tensor_copy(ring[:, k * CH:(k + 1) * CH, KEY:KEY + 1],
                               skeyE[:, ds(c * CH, CH)].unsqueeze(2))
                vs.tensor_copy(idxslot[:, k, :], posE[:, ds(c * CH, CH)]).then_inc(S("keyed"), 1)
                dve.wait_ge(S(f"locb_in{k}"), j * 16 + 16)
                for g in range(GPC):
                    wait(dve, "picked", c * GPC + g - 3)
                    vs.tensor_scalar(pick[g], locb[k][:, g * 512:(g + 1) * 512], iota_p, None, ALU.is_equal) \
                        .then_inc(S("pick_oh"), 1)

            for k in range(2):
                layer1_pick(0, k)
            with dve.Fori(1, PAIRS) as j:
                for k in range(2):
                    layer1_pick(j, k)

            def key_onehots(c, jn, k):
                dve.wait_ge(S(f"rows_in{k}"), jn * 16 + 16)
                wait(dve, "sum_done", (c - 1) * GPC)
                vs.tensor_tensor(oh[:, k, :, :], ring[:, k * CH:(k + 1) * CH, KEY:KEY + 1].to_broadcast([P, CH, P]),
                                 iota_f.unsqueeze(1).to_broadcast([P, CH, P]), ALU.is_equal).then_inc(S("key_oh"), 1)

            def layer1_sum(j, k, last=False):
                c = j * 2 + k
                offs = group_offsets(c)
                for g in range(GPC):
                    n = c * GPC + g
                    if g == 1 and not last:
                        key_onehots(c + 1, j + k, 1 - k)
                    dve.wait_ge(S("sum_done"), n + 1)
                    wait(dve, "sum_added", n)
                    yb = Y[:, ds(offs[g], 512)]
                    vs.tensor_tensor(yb, yb, bank(1 + g), ALU.add).then_inc(S("sum_added"), 1)

            dve.wait_ge(S("steprow_in"), 32)
            dve.wait_ge(S("picked"), GROUPS)
            key_onehots(0, 0, 0)
            for k in range(2):
                layer1_sum(0, k)
            with dve.Fori(1, PAIRS - 1) as j:
                for k in range(2):
                    layer1_sum(j, k)
            layer1_sum(PAIRS - 1, 0)
            layer1_sum(PAIRS - 1, 1, last=True)

            dve.wait_ge(S("lin1"), TURNS)
            link(vs.tensor_reduce(msum, fsum, axis=AX.X, op=ALU.add))
            vs.tensor_scalar(negmu, msum, -1.0 / N, None, ALU.mult).then_inc(S("negmu_ready"), 1)
            dve.wait_ge(S("sq_ready"), 1)
            vs.tensor_copy(lastf[:, 6:7], sq).then_inc(S("sq_scaled"), 1)
            dve.wait_ge(S("bsd_ready"), 1)
            link(vs.reciprocal(brs, bsd))
            link(vs.tensor_tensor(scale_c, brs, bcol[:, 7:8], ALU.mult))
            vs.scalar_tensor_tensor(out=shift_c, in0=negmu, scalar=scale_c, in1=bcol[:, 8:9],
                                    op0=ALU.mult, op1=ALU.add).then_inc(S("bn_ready"), 1)

            def final(i, k, count):
                dve.wait_ge(S("lin2_ps"), i + 1)
                dve.wait_ge(S(f"fin_x{k}"), count * 16 + 16)
                wait(dve, f"out_done{k}", count * 16)
                vs.tensor_tensor(fin_o[k], fin_x[k], bank(k)[:, 0:GW], ALU.add).then_inc(S("out_ready"), 1)

            final(0, 0, 0)
            final(1, 1, 0)
            with dve.Fori(1, (TURNS - 1) // 2) as j:
                for k in range(2):
                    final(j * 2 + k, k, j)
            final(TURNS - 1, 0, (TURNS - 1) // 2)

        @block.tensor
        def _(pe):
            mm = nc.tensor.matmul
            pe.wait_ge(S("blocks_ready"), 1)
            mm(bank(7)[:, 0:1], ones_f, vcol, start=True, stop=True).then_inc(S("viol_ps"), 1)
            pe.wait_ge(S("hist_d"), NBK)
            mm(bank(6)[:, 0:NBK], ones_f, part_d, start=True, stop=True)
            pe.wait_ge(S("hist_s"), NBK)
            mm(bank(6)[:, NBK:2 * NBK], ones_f, part_s, start=True, stop=True).then_inc(S("starts_ps"), 1)
            unsorted = pe.value_load(flag[0:1, 0:1], min_val=0, max_val=1)
            with pe.If(unsorted != 0):
                pe.wait_ge(S("blocks_found"), 1)
                mm(rank_ps, ident, start_d.unsqueeze(2).to_broadcast([P, NBK, G]), start=True, stop=True)
                with pe.Fori(0, COLS // G) as n:
                    pe.wait_ge(S("sort_oh"), n + 1)
                    rank_before(0).then_inc(S("sort_ps"), 1)
                    pe.wait_ge(S("sort_mul"), n + 1)
                    rank_after(0).then_inc(S("sort_after"), 1)

            pe.wait_ge(S("w_in"), 96)
            pe.wait_ge(S("step_tables"), 1)

            def norm0(j, k):
                i = j * 2 + k
                pe.wait_ge(S("h_ready"), i + 1)
                for b in range(LNG):
                    o = nc.tensor.transpose(bank(2 * k + b // 4)[:, b % 4 * P:(b % 4 + 1) * P],
                                            hbuf[k][:, b * P:(b + 1) * P], ident)
                o.then_inc(S("hT_ps"), 1)
                pe.wait_ge(S("hT_ready"), i + 1)
                wait(pe, "tab_ready", (i - 1) * LNG)
                for b in range(LNG):
                    o = mm(bank(4 + 2 * k + b // 4)[:, b % 4 * P:(b % 4 + 1) * P], hTs[k][:, b * P:(b + 1) * P],
                           wT[:, 0, :], start=True, stop=True)
                o.then_inc(S("m_ready"), 1)

            for k in range(2):
                norm0(0, k)
            with pe.Fori(1, LN_TURNS // 2) as j:
                for k in range(2):
                    norm0(j, k)

            pe.wait_ge(S("tab_ready"), BLOCKS)
            for f, (src_f, need) in enumerate(((fld[5], 1), (fld[4], 2), (fld[6], 3))):
                pe.wait_ge(S("field"), need)
                for a in range(4):
                    if f == 2:
                        pe.wait_ge(S("fields_moved"), a + 1)
                    for s in range(a * 4, min(a * 4 + 4, SB)):
                        o = nc.tensor.transpose(bank((f % 2) * 4 + a)[:, s % 4 * P:(s % 4 + 1) * P],
                                                src_f[:, s * P:(s + 1) * P], ident)
                    o.then_inc(S("fields_T"), 1)

            regs = [pe.alloc_register(f"step_off{q}") for q in range(CH)]

            def step_offsets(c):
                nc.tensor.load(regs, steprow[0:1, ds(c * CH, CH)])

            def rel(g, q):
                first = pe.snap(regs[g * G], min_val=0, max_val=(BLOCKS - 1) * P)
                own = pe.snap(regs[g * G + q], min_val=0, max_val=(BLOCKS - 1) * P)
                return nc.s_assert_within(pe.snap(own - first), 0, q * P, 
                                          skip_runtime_bounds_check_because="consecutive steps' blocks differ by 0 or 1")

            def sum_group(g, k, free, free_value, done):
                wait(pe, free, free_value)
                mm(bank(1 + g), zeros_b[:, 0:P], zeros_b[:, :], start=True, stop=True, skip_group_check=True)
                for q in range(G):
                    s = g * G + q
                    o = bank(1 + g)[:, 0:P] if q == 0 else ps[:, 1 + g, ds(rel(g, q), P)]
                    m = mm(o, ring[:, k * CH + s, 0:F], oh[:, k, s, :], start=False, stop=True, skip_group_check=True)
                m.then_inc(S(done), 1)

            def layer0(j, k):
                c = j * 2 + k
                step_offsets(c)
                for g in range(GPC):
                    n = c * GPC + g
                    if not isinstance(n, int) or n > 0:
                        pe.wait_ge(S("rank_read"), n)
                        rank_after((g + 3) % G).then_inc(S("rank_counted"), 1)
                    pe.wait_ge(S("blk_ready"), n + 1)
                    rank_before(g).then_inc(S("rank_ps"), 1)
                    if g == 0:
                        pe.wait_ge(S("oh_ready"), c + 1)
                        pe.wait_ge(S(f"gathered{k}"), j * (CH * 16) + CH * 16)
                    sum_group(g, k, "agg_added", n - 3, "agg_done")

            pe.wait_ge(S("fields_moved"), 12)
            pe.wait_ge(S("steprow_in"), 16)
            mm(rank_ps, ident, base_s.unsqueeze(2).to_broadcast([P, NBK, G]), start=True, stop=True)
            for k in range(2):
                layer0(0, k)
            with pe.Fori(1, PAIRS) as j:
                for k in range(2):
                    layer0(j, k)

            pe.wait_ge(S("agg_added"), GROUPS)

            def gates(i, k):
                wait(pe, "cand_in", i - 1)
                msg, h = Y[:, ds(i * GW, GW)], H[:, ds(i * GW, GW)]
                for a in range(2):
                    o = bank(2 * k)[:, a * GW:(a + 1) * GW]
                    mm(o, wT[:, 1 + a, :], msg, start=True, stop=False)
                    mm(o, wT[:, 4 + a, :], h, start=False, stop=True)
                mm(bank(2 * k + 1)[:, 0:GW], wT[:, 3, :], msg, start=True, stop=True)
                mm(bank(2 * k + 1)[:, GW:2 * GW], wT[:, 6, :], h, start=True, stop=True).then_inc(S("gates_ps"), 1)

            def back(i, k):
                pe.wait_ge(S("hn_ready"), i + 1)
                wait(pe, "x1_sum", i - 1)
                for b in range(NG):
                    o = nc.tensor.transpose(bank(4 + k)[:, b * P:(b + 1) * P], hnbuf[k][:, b * P:(b + 1) * P], ident)
                o.then_inc(S("hn_ps"), 1)

            gates(0, 0)
            gates(1, 1)
            back(0, 0)
            with pe.Fori(0, (TURNS - 3) // 2) as j:
                for k in range(2):
                    gates(j * 2 + k + 2, k)
                    back(j * 2 + k + 1, (k + 1) % 2)
            gates(TURNS - 1, 0)
            back(TURNS - 2, 1)
            back(TURNS - 1, 0)

            def h2T(i, k):
                pe.wait_ge(S("h2_ready"), i + 1)
                wait(pe, "h2_done", i - 1)
                for b in range(NG):
                    o = nc.tensor.transpose(bank(k)[:, b * P:(b + 1) * P], hs[k][:, b * P:(b + 1) * P], ident)
                o.then_inc(S("h2_ps"), 1)

            h2T(0, 0)
            h2T(1, 1)
            with pe.Fori(0, (TURNS - 3) // 2) as j:
                for k in range(2):
                    h2T(j * 2 + k + 2, k)
            h2T(TURNS - 1, 0)

            def picks(j, k):
                c = j * 2 + k
                step_offsets(c)
                for g in range(GPC):
                    n = c * GPC + g
                    pe.wait_ge(S("pick_oh"), n + 1)
                    wait(pe, "row_moved", n - 3)
                    for q in range(G):
                        off = pe.snap(regs[g * G + q], min_val=0, max_val=(BLOCKS - 1) * P)
                        m = mm(bank(g)[:, q * P:(q + 1) * P], pick[g][:, q * P:(q + 1) * P], H[:, ds(off, P)],
                               start=True, stop=True)
                    m.then_inc(S("picked"), 1)

            pe.wait_ge(S("h2_kept"), TURNS)
            pe.wait_ge(S("h2_done"), TURNS)
            for k in range(2):
                picks(0, k)
            with pe.Fori(1, PAIRS) as j:
                for k in range(2):
                    picks(j, k)

            def layer1_sum(j, k):
                c = j * 2 + k
                step_offsets(c)
                pe.wait_ge(S("key_oh"), c + 1)
                for g in range(GPC):
                    sum_group(g, k, "sum_added", c * GPC + g - 3, "sum_done")

            pe.wait_ge(S("steprow_in"), 32)
            pe.wait_ge(S("row_moved"), GROUPS)
            for k in range(2):
                layer1_sum(0, k)
            with pe.Fori(1, PAIRS) as j:
                for k in range(2):
                    layer1_sum(j, k)

            pe.wait_ge(S("sum_added"), GROUPS)

            def lin1(i, k):
                wait(pe, "lin1", i - 1)
                mm(bank(4 + k)[:, 0:GW], wT[:, 7, :], Y[:, ds(i * GW, GW)], start=True, stop=True).then_inc(S("lin1_ps"), 1)

            lin1(0, 0)
            lin1(1, 1)
            with pe.Fori(1, (TURNS - 1) // 2) as j:
                for k in range(2):
                    lin1(j * 2 + k, k)
            lin1(TURNS - 1, 0)

            def lin2(i, k):
                pe.wait_ge(S("z_ready"), i + 1)
                wait(pe, "out_ready", i - 1)
                for b in range(NG):
                    o = bank(k)[:, b * P:(b + 1) * P]
                    mm(o, fin_z[k][:, b * P:(b + 1) * P], wT[:, 8, :], start=True, stop=False)
                    m = mm(o, ones_f[0:1, :], b2row[:, :], start=False, stop=True)
                m.then_inc(S("lin2_ps"), 1)

            lin2(0, 0)
            lin2(1, 1)
            with pe.Fori(1, (TURNS - 1) // 2) as j:
                for k in range(2):
                    lin2(j * 2 + k, k)
            lin2(TURNS - 1, 0)


def shape_constants(np):
    c = np.zeros((P, CF_W), np.float32)

    def put(name, value):
        a, w = CF[name]
        c[:, a:a + w] = value

    put("ident", np.eye(P))
    put("ones", 1.0)
    put("before", np.triu(np.ones((P, P)), 1))
    put("iota", np.arange(P))
    put("iota_p", np.arange(P)[:, None])
    put("thr", np.arange(NBK) - 0.5)
    put("blk", np.arange(NBK))
    put("step", np.arange(SB) * P + np.arange(P)[:, None])
    put("lneps", LN_EPS)
    put("bneps", BN_EPS)
    put("pad", np.where(np.arange(RW) == KEY, FAR, 0.0))
    put("blk4", np.repeat(np.arange(NBK), G))
    return c


def kernel(x, src, dst, edge_type_9, L0_gnn_W_msg, L0_gnn_b_msg, L0_gnn_edge_embed, L0_gnn_W_ih, L0_gnn_W_hh,
           L0_gnn_b_ih, L0_gnn_b_hh, L1_gnn_eps, L1_gnn_W1, L1_gnn_b1, L1_gnn_gamma, L1_gnn_beta, L1_gnn_W2, L1_gnn_b2):
    import numpy as np
    import concourse.bacc as bacc
    from concourse.bass_utils import run_bass_kernel_spmd

    def a(v):
        return np.asarray(v)

    def edge_rows(v, pad):
        return np.concatenate([a(v).astype(np.int32), np.full(EPAD - len(v), pad, np.int32)]).reshape(P, COLS)

    w_ih, w_hh = a(L0_gnn_W_ih), a(L0_gnn_W_hh)
    mats = [a(L0_gnn_W_msg)] + [w_ih[k * F:(k + 1) * F] for k in range(3)] + [w_hh[k * F:(k + 1) * F] for k in range(3)] \
        + [a(L1_gnn_W1), a(L1_gnn_W2)]
    b_ih, b_hh = a(L0_gnn_b_ih).reshape(3, F), a(L0_gnn_b_hh).reshape(3, F)
    arrays = {
        "in_x": np.concatenate([a(x), np.zeros((NPAD - N, F), np.float32)]),
        "in_edges": np.stack([edge_rows(dst, PADNODE), edge_rows(src, PADNODE), edge_rows(edge_type_9, 0)]),
        "in_dst_next": edge_rows(a(dst)[1:], PADNODE),
        "in_weights": np.ascontiguousarray(np.concatenate([m.T for m in mats], axis=1)),
        "in_bias_cols": np.ascontiguousarray(np.stack([*b_ih, *b_hh, a(L1_gnn_b1), a(L1_gnn_gamma), a(L1_gnn_beta)], axis=1)),
        "in_embed": a(L0_gnn_edge_embed),
        "in_b_msg": a(L0_gnn_b_msg),
        "in_b2": a(L1_gnn_b2),
        "in_eps": a(L1_gnn_eps).reshape(1, 1),
        "in_consts": shape_constants(np),
    }
    nc = bacc.Bacc("TRN2", target_bir_lowering=False, num_devices=1)
    args = [nc.dram_tensor(n, v.shape, mybir.dt.from_np(v.dtype), kind="ExternalInput").ap() for n, v in arrays.items()]
    out = nc.dram_tensor("out_x", (NPAD, F), mybir.dt.float32, kind="ExternalOutput").ap()
    build_gnn(nc, *args, out)
    r = run_bass_kernel_spmd(nc, [arrays], core_ids=[0])
    return r.results[0]["out_x"][:N]
```

```python
from contextlib import ExitStack

import concourse.bass as bass
from concourse import mybir

N, F, E, TYPES = 12500, 128, 212500, 9
P = 128
BLOCKS = -(-N // P)
NPAD = BLOCKS * P
COLS = 1664
EPAD = COLS * P
TILES = EPAD // P
TPP = TILES // P
STEPS = E // P + BLOCKS
CH = 16
PAIRS = -(-STEPS // (2 * CH))
CHUNKS = 2 * PAIRS
STEPS_P = CHUNKS * CH
G = 4
GPC = CH // G
GROUPS = STEPS_P // G
SB = -(-STEPS_P // P)
SW = SB * P
RW = 136
KEY = F
FAR = 255.0
NBK = BLOCKS + 1
PADNODE = BLOCKS * P
LNG = 7
LNW = LNG * P
LN_TURNS = BLOCKS // LNG
PER_TURN = 6
EARLY = BLOCKS - PER_TURN * LN_TURNS
NG = 2
GW = NG * P
TURNS = BLOCKS // NG
ROWS_D = STEPS_P * P
SKIP = 1 << 20
LN_EPS = 1e-5
BN_EPS = 1e-5
CF = {}
for _name, _width in (("ident", P), ("ones", P), ("before", P), ("iota", P), ("iota_p", 1), ("thr", NBK), ("node", NBK),
                      ("blk", NBK), ("step", SB), ("lneps", 1), ("bneps", 1), ("pad", RW), ("blk4", NBK * G)):
    CF[_name] = (sum(w for _, w in CF.values()), _width)
CF_W = sum(w for _, w in CF.values())


def build_gnn(nc, x, edges, dst_next, weights, bias_cols, embed, b_msg, b2, eps1, consts, out):
    f32, i32, bf16 = mybir.dt.float32, mybir.dt.int32, mybir.dt.bfloat16
    ALU, ACT, AX = mybir.AluOpType, mybir.ActivationFunctionType, mybir.AxisListType
    ds = bass.ds
    ctx = ExitStack()
    with ctx:
        ctx.enter_context(nc.allow_non_contiguous_dma(reason="small step tables"))
        ctx.enter_context(nc.allow_low_precision(reason="sums of indices into int32: exact below 2**24"))

        def sb(name, shape, dt=f32):
            return ctx.enter_context(nc.sbuf_tensor("sb_" + name, shape, dt))

        held = {}

        def S(name):
            if name not in held:
                held[name] = ctx.enter_context(nc.semaphore(name))
            return held[name]

        def wait(engine, name, value):
            if not isinstance(value, int) or value > 0:
                engine.wait_ge(S(name), value)

        def plain(engine):
            engine.sem_inc(S("passed"), 1)

        table_d = nc.dram_tensor("msg_table", (TYPES * NPAD, F), f32).ap()
        packed_d = nc.dram_tensor("packed_edges", (TILES, P), i32).ap()
        blockrow_d = nc.dram_tensor("step_block_offsets", (2, SW), i32).ap()
        loc_d = nc.dram_tensor("step_targets", (SW, P), bf16).ap()
        rows_d = nc.dram_tensor("rows_by_src", (ROWS_D, RW), f32).ap()
        x1_d = nc.dram_tensor("x_after_layer0", (NPAD, F), f32).ap()

        H = sb("H", [P, NPAD])
        Y = sb("Y", [P, NPAD + (G - 1) * P])
        ring = sb("ring", [P, 2 * CH, RW])
        oh = sb("oh", [P, 2, CH, P])
        locE = sb("locE", [P, SW])
        tabE = sb("tabE", [P, SW])
        skeyE = sb("skeyE", [P, SW])
        sblkE = sb("sblkE", [P, SW], bf16)
        posE = sb("posE", [P, STEPS_P], i32)
        steprow = sb("steprow", [1, STEPS_P], i32)
        idxslot = sb("idxslot", [P, 2, CH], i32)
        cf = sb("cf", [P, CF_W])
        ones_b = sb("ones_b", [P, P], bf16)
        before_b = sb("before_b", [P, P], bf16)
        rest_b = sb("rest_b", [P, P], bf16)
        zeros_b = sb("zeros_b", [P, 512], bf16)
        blk4_b = sb("blk4_b", [P, NBK, G], bf16)
        blk1h = sb("blk1h", [P, G, NBK, G], bf16)
        ranked = sb("ranked", [P, 2, NBK, G])
        wT = sb("wT", [P, 9, P])
        embb = sb("embb", [P, TYPES, P])
        bmsgb = sb("bmsgb", [P, P])
        b2row = sb("b2row", [1, P])
        bcol = sb("bcol", [P, 9])
        scol = sb("scol", [P, 12])
        smalls = sb("smalls", [P, 2100])
        flag = sb("flag", [1, 1], i32)
        lastrow = sb("lastrow", [1, 2, 2, BLOCKS], i32)
        ps = ctx.enter_context(nc.psum_tensor("ps", [P, 8, 512], f32))

        def const(name):
            a, w = CF[name]
            return cf[:, a:a + w]

        ident, ones_f, iota_f, iota_p = const("ident"), const("ones"), const("iota"), const("iota_p")

        def yv(k, dt):
            return Y[:, k * COLS:(k + 1) * COLS].bitcast(dt) if dt is not f32 else Y[:, k * COLS:(k + 1) * COLS]

        raw_dst, raw_src, raw_typ, packed, nxt = (yv(k, i32) for k in range(5))
        dblk, sblk = yv(5, bf16)[:, 0:COLS], yv(5, bf16)[:, COLS:2 * COLS]
        junk_v, junk_a = yv(6, bf16)[:, 0:COLS], yv(6, bf16)[:, COLS:2 * COLS]
        viol = H[:, 0:COLS]
        tile_lt = viol[:, 0:NBK * TPP].rearrange("p (b t) -> p b t", t=TPP)
        blktmp = Y[:, 7 * COLS:7 * COLS + 1024].bitcast(bf16)[:, 0:SB * (BLOCKS - 1)] \
            .rearrange("p (s b) -> p s b", s=SB)
        fld = [Y[:, k * SW:(k + 1) * SW] for k in range(7)]
        fldi = [v.bitcast(i32) for v in fld]

        ringf = ring[:, :, :].rearrange("p a b -> p (a b)")
        ohf = oh[:, :, :, :].rearrange("p a b c -> p (a b c)")
        xbuf = [ringf[:, k * LNW:(k + 1) * LNW] for k in range(2)]
        hbuf = [ringf[:, (2 + k) * LNW:(3 + k) * LNW] for k in range(2)]
        hTs = [ohf[:, k * LNW:(k + 1) * LNW] for k in range(2)]
        TW = TYPES * P
        tabt = [ohf[:, 2 * LNW + k * TW:2 * LNW + (k + 1) * TW] for k in range(2)]

        def ob(k):
            return ohf[:, k * GW:(k + 1) * GW]

        rbuf, zbuf, tbuf, nbuf, hnbuf, cell_x = ([ob(2 * a + k) for k in range(2)] for a in range(6))
        hs = [ob(12 + k) for k in range(2)]
        locb = [ohf[:, k * 1024:(k + 1) * 1024].bitcast(bf16) for k in range(2)]
        pick = [ohf[:, 2048 + k * 512:2048 + (k + 1) * 512] for k in range(4)]
        fin_z, fin_x, fin_o = ([ob(2 * a + k) for k in range(2)] for a in range(3))

        at = [0]

        def small(n, dt=f32):
            v = smalls[:, at[0]:at[0] + n]
            at[0] += n
            return v if dt is f32 else v.bitcast(dt)

        part_d, part_s = small(NBK), small(NBK)
        start_d, start_s = small(NBK), small(NBK)
        lo_i = small(NBK, i32)
        ramp_s = small(NBK)
        tile_end = small(TPP)
        first_d, first_s = small(NBK), small(NBK)
        base_s = small(NBK)
        bstep_d, bstep_s = small(SB), small(SB)
        boff_f = small(SB)
        boff_d, boff_s = small(SB, i32), small(SB, i32)
        tile_f, tile_i = small(SB), small(SB, i32)
        stats = small(LNG * 6)
        mv = small(LNG * 2)
        sd = small(LNG)
        rstd = [small(LNG) for _ in range(2)]
        nbias = [small(LNG) for _ in range(2)]
        mvn = small(BLOCKS * 2)
        sdn, rstdn, nbn = small(BLOCKS), small(BLOCKS), small(BLOCKS)
        fsum = small(TURNS)
        lastf = small(BLOCKS)
        lasti = [small(BLOCKS, i32) for _ in range(2)]
        possl = small(G, i32)
        paysl = small(G, i32)
        vcol = scol[:, 0:1]
        one_eps, brz = scol[:, 1:2], scol[:, 2:4]
        negmu, sq, bsd, brs, scale_c, shift_c, msum = (scol[:, k:k + 1] for k in range(4, 11))

        def bank(k):
            return ps[:, k, :]

        rank_ps = ps[:, 0, 0:NBK * G].rearrange("p (b q) -> p b q", q=G)

        block = ctx.enter_context(nc.Block())

        def rank_before(n_slot):
            o = blk1h[:, n_slot, :, :]
            nc.tensor.matmul(rank_ps, before_b[:, :], o, start=False, stop=True, skip_group_check=True)
            for q in range(G - 1):
                m = nc.tensor.matmul(rank_ps[:, :, q + 1:G], ones_b[:, :],
                                     o[:, :, q:q + 1].to_broadcast([P, NBK, G - 1 - q]),
                                     start=False, stop=True, skip_group_check=True)
            return m

        def rank_after(n_slot):
            o = blk1h[:, n_slot, :, :]
            nc.tensor.matmul(rank_ps, rest_b[:, :], o, start=False, stop=True, skip_group_check=True)
            for q in range(1, G):
                m = nc.tensor.matmul(rank_ps[:, :, 0:q], ones_b[:, :],
                                     o[:, :, q:q + 1].to_broadcast([P, NBK, q]),
                                     start=False, stop=True, skip_group_check=True)
            return m

        @block.sync
        def _(sp):
            sp.dma_start(cf[:, :], consts).then_inc(S("consts_in"), 16)
            sp.dma_start(raw_dst, edges[0]).then_inc(S("dst_in"), 16)
            sp.dma_start(nxt, dst_next).then_inc(S("dst_in"), 16)
            sp.dma_start(raw_src, edges[1]).then_inc(S("src_in"), 16)
            sp.dma_start(raw_typ, edges[2]).then_inc(S("type_in"), 16)
            xv = x.rearrange("(b p) f -> p b f", p=P)

            def load_x(i, k):
                sp.dma_start(xbuf[k].rearrange("p (b f) -> p b f", f=F), xv[:, ds(i * LNG, LNG), :]) \
                    .then_inc(S(f"x_in{k}"), 16)

            load_x(0, 0)
            load_x(1, 1)
            sp.dma_start(wT[:, :, :], weights.rearrange("p (a b) -> p a b", a=9)).then_inc(S("w_in"), 16)
            sp.dma_start(bcol[:, :], bias_cols).then_inc(S("w_in"), 16)
            sp.dma_start(embb[:, :, :].rearrange("p t f -> p (t f)"),
                         embed.rearrange("(a t) f -> a (t f)", a=1).to_broadcast([P, TYPES * F])).then_inc(S("w_in"), 16)
            sp.dma_start(bmsgb[:, :], b_msg.rearrange("(a f) -> a f", a=1).to_broadcast([P, F])).then_inc(S("w_in"), 16)
            sp.dma_start(b2row[:, :], b2.rearrange("(a f) -> a f", a=1)).then_inc(S("w_in"), 16)
            sp.dma_start(one_eps, eps1.to_broadcast([P, 1])).then_inc(S("w_in"), 16)

            sp.wait_ge(S("flag_set"), 1)
            unsorted = sp.value_load(flag[0:1, 0:1], min_val=0, max_val=1)
            with sp.If(unsorted == 0):
                sp.wait_ge(S("packed"), 1)
                sp.dma_start(packed_d.rearrange("(p a) b -> p (a b)", p=P), packed).then_inc(S("packed_out"), 16)

            sp.wait_ge(S("step_tables"), 1)
            rv = blockrow_d.rearrange("a (s p) -> p a s", p=P)
            sp.dma_start(rv[:, 0, :], boff_d).then_inc(S("row_out_d"), 16)
            sp.wait_ge(S("row_out_d"), 16)
            sp.dma_start(steprow[:, :], blockrow_d[0:1, 0:STEPS_P]).then_inc(S("steprow_in"), 16)

            def table_out(j, k):
                tv = table_d.rearrange("(t b p) f -> b p t f", p=P, b=BLOCKS)
                for b in range(LNG):
                    slot = (k + b) % 2
                    sp.wait_ge(S("tab_ready"), (j * 2 + k) * LNG + b + 1)
                    sp.dma_start(tv[ds((j * 2 + k) * LNG + b, 1), :, :, :].rearrange("a p t f -> (a p) t f"),
                                 tabt[slot].rearrange("p (t f) -> p t f", f=F)).then_inc(S(f"tab_out{slot}"), 16)

            with sp.Fori(0, LN_TURNS // 2 - 1) as j:
                for k in range(2):
                    sp.wait_ge(S("h_ready"), j * 2 + k + 1)
                    load_x(j * 2 + 2 + k, k)
                    table_out(j, k)
            for k in range(2):
                table_out(LN_TURNS // 2 - 1, k)

            sp.wait_ge(S("loc_ready"), 1)
            sp.dma_start(loc_d.rearrange("(s p) e -> p s e", p=P),
                         fld[1].bitcast(bf16)[:, 0:SW].rearrange("p (s e) -> p s e", e=P)).then_inc(S("loc_out"), 16)

            sp.wait_ge(S("src_tables"), 1)
            sp.dma_start(rv[:, 1, :], boff_s).then_inc(S("row_out_s"), 16)

            pad_v = rows_d.rearrange("(c p k) w -> c k p w", p=P, k=CH)
            for t in (STEPS, STEPS + 1):
                sp.dma_start(pad_v[t // CH, t % CH], const("pad")).then_inc(S("pads_out"), 16)
            flat_v = rows_d.rearrange("(c p k) w -> c p (k w)", p=P, k=CH)
            wait(sp, "pads_out", 32)

            def pad_tiles(b):
                for a in range(2):
                    c = sp.value_load(lastrow[0:1, a, 0, ds(b, 1)], min_val=0, max_val=CHUNKS - 1)
                    q = sp.value_load(lastrow[0:1, a, 1, ds(b, 1)], min_val=0, max_val=CH - 1)
                    sp.dma_start(flat_v[ds(c, 1), :, ds(q * RW, RW)].rearrange("a p w -> (a p) w"), const("pad")) \
                        .then_inc(S("pads_out"), 16)
                    sp.wait_ge(S("pads_out"), (b * 2 + a) * 16 + 48)
                    plain(sp)

            with sp.Fori(0, BLOCKS) as b:
                pad_tiles(b)

            sp.wait_ge(S("agg_done"), GROUPS)

            def cell_in(i, k):
                sp.dma_start(cell_x[k].rearrange("p (b f) -> p b f", f=F), xv[:, ds(i * NG, NG), :]) \
                    .then_inc(S(f"cell_x{k}"), 16)

            def x1_out(i):
                x1v = x1_d.rearrange("(b p) f -> p b f", p=P)
                sp.wait_ge(S("x1_kept"), i + 1)
                sp.dma_start(x1v[:, ds(i * NG, NG), :], H[:, ds(i * GW, GW)].rearrange("p (b f) -> p b f", f=F)) \
                    .then_inc(S("x1_out"), 16)

            cell_in(0, 0)
            cell_in(1, 1)
            with sp.Fori(0, (TURNS - 3) // 2) as j:
                for k in range(2):
                    x1_out(j * 2 + k)
                    cell_in(j * 2 + k + 2, k)
            x1_out(TURNS - 3)
            cell_in(TURNS - 1, 0)
            x1_out(TURNS - 2)
            x1_out(TURNS - 1)
            sp.wait_ge(S("x1_out"), TURNS * 16)
            nc.sync.sem_inc(S("x1_stored"), 1)

            def loc_in(c, k):
                sp.dma_start(locb[k], loc_d.rearrange("(a s) e -> a (s e)", s=CH)[ds(c, 1), :].to_broadcast([P, CH * P])) \
                    .then_inc(S(f"locb_in{k}"), 16)

            sp.wait_ge(S("h2_done"), TURNS)
            sp.wait_ge(S("loc_out"), 16)
            loc_in(0, 0)
            loc_in(1, 1)
            with sp.Fori(1, PAIRS) as j:
                for k in range(2):
                    sp.wait_ge(S("pick_oh"), (j * 2 + k - 1) * GPC)
                    loc_in(j * 2 + k, k)

            sp.wait_ge(S("picked"), GROUPS)
            sp.wait_ge(S("row_out_s"), 16)
            sp.dma_start(steprow[:, :], blockrow_d[1:2, 0:STEPS_P]).then_inc(S("steprow_in"), 16)
            for k in range(2):
                sp.wait_ge(S(f"scattered{k}"), PAIRS * CH * 16)

            def rows_in(c, k):
                sp.dma_start(ring[:, k * CH:(k + 1) * CH, :].rearrange("p a w -> p (a w)"),
                             rows_d.rearrange("(c p k) w -> c p (k w)", p=P, k=CH)[ds(c, 1), :, :]
                             .rearrange("a p w -> (a p) w")).then_inc(S(f"rows_in{k}"), 16)

            rows_in(0, 0)
            rows_in(1, 1)
            with sp.Fori(1, PAIRS) as j:
                for k in range(2):
                    sp.wait_ge(S("sum_done"), (j * 2 + k - 1) * GPC)
                    rows_in(j * 2 + k, k)

            x1v = x1_d.rearrange("(b p) f -> p b f", p=P)
            ov = out.rearrange("(b p) f -> p b f", p=P)
            sp.wait_ge(S("sum_added"), GROUPS)

            def fin_in(i, k):
                sp.dma_start(fin_x[k].rearrange("p (b f) -> p b f", f=F), x1v[:, ds(i * NG, NG), :]) \
                    .then_inc(S(f"fin_x{k}"), 16)

            def fin_out(i, k):
                sp.wait_ge(S("out_ready"), i + 1)
                sp.dma_start(ov[:, ds(i * NG, NG), :], fin_o[k].rearrange("p (b f) -> p b f", f=F)) \
                    .then_inc(S(f"out_done{k}"), 16)

            fin_in(0, 0)
            fin_in(1, 1)
            with sp.Fori(0, (TURNS - 3) // 2) as j:
                for k in range(2):
                    fin_out(j * 2 + k, k)
                    fin_in(j * 2 + k + 2, k)
            fin_out(TURNS - 3, 0)
            fin_in(TURNS - 1, 0)
            fin_out(TURNS - 2, 1)
            fin_out(TURNS - 1, 0)
            sp.wait_ge(S("out_done0"), (TURNS + 1) // 2 * 16)
            sp.wait_ge(S("out_done1"), TURNS // 2 * 16)

        @block.gpsimd
        def _(pool):
            pool.wait_ge(S("flag_set"), 1)
            unsorted = pool.value_load(flag[0:1, 0:1], min_val=0, max_val=1)
            with pool.If(unsorted == 0):
                pool.wait_ge(S("packed_out"), 16)
            with pool.If(unsorted != 0):
                with pool.Fori(0, COLS // G) as n:
                    pool.wait_ge(S("sort_pos"), n + 1)
                    plain(pool)
                    for q in range(G):
                        pool.indirect_dma_start(
                            out=packed_d.rearrange("a (b c) -> (a b) c", c=1),
                            out_offset=bass.IndirectOffsetOnAxis(ap=possl[:, q:q + 1], axis=0),
                            in_=paysl[:, q:q + 1], in_offset=None).then_inc(S("sorted_out"), 16)
                    pool.wait_ge(S("sorted_out"), (n + 1) * (G * 16))
                    nc.gpsimd.sem_inc(S("sort_sent"), 1)
            pool.wait_ge(S("step_tables"), 1)
            for s in range(SB):
                pool.indirect_dma_start(out=fldi[0][:, s * P:(s + 1) * P], out_offset=None, in_=packed_d[:, :],
                                        in_offset=bass.IndirectOffsetOnAxis(ap=tile_i[:, s:s + 1], axis=0)) \
                    .then_inc(S("tiles_in"), 16)
            def keep_h(i, k):
                pool.wait_ge(S("hT_ready"), i + 1)
                nc.gpsimd.tensor_copy(H[:, ds(i * LNW, LNW)], hTs[k]).then_inc(S("hT_kept"), 1)

            with pool.Fori(0, LN_TURNS // 2) as j:
                for k in range(2):
                    keep_h(j * 2 + k, k)

            for k in range(2):
                pool.wait_ge(S(f"tab_out{k}"), BLOCKS // 2 * 16)

            def gather(j, k):
                wait(pool, "agg_done", (j * 2 + k - 1) * GPC)
                pool.wait_ge(S("idx_ready"), j * 2 + k + 1)
                plain(pool)
                for q in range(CH):
                    pool.indirect_dma_start(out=ring[:, k * CH + q, 0:F], out_offset=None, in_=table_d[:, :],
                                            in_offset=bass.IndirectOffsetOnAxis(ap=idxslot[:, k, q:q + 1], axis=0)) \
                        .then_inc(S(f"gathered{k}"), 16)

            for k in range(2):
                gather(0, k)
            with pool.Fori(1, PAIRS) as j:
                for k in range(2):
                    gather(j, k)

            def scatter(j, k):
                pool.wait_ge(S("keyed"), j * 2 + k + 1)
                for g in range(GPC):
                    pool.wait_ge(S("row_moved"), (j * 2 + k) * GPC + g + 1)
                    plain(pool)
                    for q in range(G):
                        s = g * G + q
                        pool.indirect_dma_start(
                            out=rows_d[:, :], out_offset=bass.IndirectOffsetOnAxis(ap=idxslot[:, k, s:s + 1], axis=0),
                            in_=ring[:, k * CH + s, :], in_offset=None,
                            bounds_check=ROWS_D - 1, oob_is_err=False).then_inc(S(f"scattered{k}"), 16)

            pool.wait_ge(S("pads_out"), (2 * BLOCKS + 2) * 16)
            with pool.Fori(0, PAIRS) as j:
                for k in range(2):
                    scatter(j, k)

        @block.scalar
        def _(act):
            def ramp(b):
                nc.scalar.activation(junk_a, sblk, ACT.Relu, bias=cf[:, ds(b + CF["blk"][0], 1)], scale=-1.0,
                                     accum_out=ramp_s[:, ds(b, 1)]).then_inc(S("ramp_s"), 1)

            def ramps(first, count):
                for b in range(count):
                    act.wait_ge(S("ramp_s"), first + b - 1)
                    ramp(first + b)

            def deviation(i):
                act.wait_ge(S("stats_ready"), i + 1)
                nc.scalar.activation(sd, mv.rearrange("p (b t) -> p b t", t=2)[:, :, 1], ACT.Sqrt,
                                     bias=const("lneps")).then_inc(S("sd_ready"), 1)

            def norm0(j, k, last=False):
                i = j * 2 + k
                act.wait_ge(S("rstd_ready"), i + 1)
                wait(act, "hT_ps", i - 1)
                for b in range(LNG):
                    o = nc.scalar.activation(hbuf[k][:, b * P:(b + 1) * P], xbuf[k][:, b * P:(b + 1) * P], ACT.Relu,
                                             bias=nbias[k][:, b:b + 1], scale=rstd[k][:, b:b + 1])
                o.then_inc(S("h_ready"), 1)
                if not last:
                    deviation(i + 1)
                ramps(EARLY + i * PER_TURN + 1, 3)
                act.wait_ge(S("hT_ps"), i + 1)
                wait(act, "hT_kept", i - 1)
                wait(act, "m_ready", i - 1)
                nc.scalar.copy(hTs[k][:, 0:512], bank(2 * k))
                nc.scalar.copy(hTs[k][:, 512:LNW], bank(2 * k + 1)[:, 0:LNW - 512]).then_inc(S("hT_ready"), 1)
                ramps(EARLY + i * PER_TURN + 4, PER_TURN - 3)

            act.wait_ge(S("src_blocks"), 1)
            ramp(1)
            ramps(2, EARLY - 1)
            deviation(0)
            for k in range(2):
                norm0(0, k)
            with act.Fori(1, LN_TURNS // 2 - 1) as j:
                for k in range(2):
                    norm0(j, k)
            norm0(LN_TURNS // 2 - 1, 0)
            norm0(LN_TURNS // 2 - 1, 1, last=True)

            for f, dst_t in enumerate((tabE, locE, None)):
                for a in range(4):
                    w = min(512, SW - a * 512)
                    act.wait_ge(S("fields_T"), f * 4 + a + 1)
                    o = dst_t[:, a * 512:a * 512 + w] if dst_t is not None else fldi[2][:, a * 512:a * 512 + w]
                    nc.scalar.copy(o, bank((f % 2) * 4 + a)[:, 0:w]).then_inc(S("fields_moved"), 1)

            def gates(i, k):
                act.wait_ge(S("gates_ps"), i + 1)
                nc.scalar.activation(rbuf[k], bank(2 * k)[:, 0:GW], ACT.Sigmoid, bias=brz[:, 0:1])
                wait(act, "hn_ready", i - 1)
                nc.scalar.activation(zbuf[k], bank(2 * k)[:, GW:2 * GW], ACT.Sigmoid, bias=brz[:, 1:2]).then_inc(S("gates_rz"), 1)

            def candidate(i, k):
                act.wait_ge(S("cand_in"), i + 1)
                wait(act, "x1_ps", i - 1)
                nc.scalar.activation(nbuf[k], tbuf[k], ACT.Tanh, bias=bcol[:, 2:3]).then_inc(S("cand"), 1)

            act.wait_ge(S("agg_added"), GROUPS)
            act.wait_ge(S("brz_set"), 1)
            def keep_x1(i, k):
                act.wait_ge(S("x1_ps"), i + 1)
                nc.scalar.copy(H[:, ds(i * GW, GW)], bank(4 + k)[:, 0:GW]).then_inc(S("x1_kept"), 1)

            gates(0, 0)
            gates(1, 1)
            candidate(0, 0)
            with act.Fori(0, (TURNS - 3) // 2) as j:
                for k in range(2):
                    gates(j * 2 + k + 2, k)
                    candidate(j * 2 + k + 1, 1 - k)
                    keep_x1(j * 2 + k, k)
            gates(TURNS - 1, 0)
            candidate(TURNS - 2, 1)
            keep_x1(TURNS - 3, 0)
            candidate(TURNS - 1, 0)
            keep_x1(TURNS - 2, 1)
            keep_x1(TURNS - 1, 0)

            act.wait_ge(S("x1_stats"), TURNS)
            nc.scalar.activation(sdn, mvn.rearrange("p (b t) -> p b t", t=2)[:, :, 1], ACT.Sqrt,
                                 bias=const("lneps")).then_inc(S("sdn_ready"), 1)
            act.wait_ge(S("rstdn_ready"), 1)
            act.wait_ge(S("x1_stored"), 1)

            def norm1(i, k):
                wait(act, "h2_kept", i - 1)
                wait(act, "h2_ps", i - 1)
                for b in range(NG):
                    o = nc.scalar.activation(hs[k][:, b * P:(b + 1) * P], H[:, ds(i * GW + b * P, P)], ACT.Relu,
                                             bias=nbn[:, ds(i * NG + b, 1)], scale=rstdn[:, ds(i * NG + b, 1)])
                o.then_inc(S("h2_ready"), 1)

            norm1(0, 0)
            norm1(1, 1)
            with act.Fori(0, (TURNS - 3) // 2) as j:
                for k in range(2):
                    norm1(j * 2 + k + 2, k)
            norm1(TURNS - 1, 0)

            def move_rows(j, k):
                wait(act, f"scattered{k}", j * (CH * 16))
                for g in range(GPC):
                    act.wait_ge(S("picked"), (j * 2 + k) * GPC + g + 1)
                    nc.scalar.copy(ring[:, k * CH + g * G:k * CH + (g + 1) * G, 0:F],
                                   bank(g).rearrange("p (q f) -> p q f", f=F)).then_inc(S("row_moved"), 1)

            act.wait_ge(S("ring_cleared"), 1)
            for k in range(2):
                move_rows(0, k)
            with act.Fori(1, PAIRS) as j:
                for k in range(2):
                    move_rows(j, k)

            def lin1(i, k, w):
                act.wait_ge(S("lin1_ps"), i + 1)
                nc.scalar.activation(Y[:, ds(i * GW, w)], bank(4 + k)[:, 0:w], ACT.Identity, bias=bcol[:, 6:7],
                                     accum_out=fsum[:, ds(i, 1)]).then_inc(S("lin1"), 1)

            with act.Fori(0, (TURNS - 1) // 2) as j:
                for k in range(2):
                    lin1(j * 2 + k, k, GW)
            lin1(TURNS - 1, 0, N - (TURNS - 1) * GW)
            act.wait_ge(S("negmu_ready"), 1)
            nc.scalar.activation(H[:, 0:N], Y[:, 0:N], ACT.Square, bias=negmu, accum_out=sq).then_inc(S("sq_ready"), 1)
            act.wait_ge(S("sq_scaled"), 1)
            nc.scalar.activation(bsd, sq, ACT.Sqrt, bias=const("bneps"), scale=1.0 / N).then_inc(S("bsd_ready"), 1)
            act.wait_ge(S("bn_ready"), 1)

            def bn_relu(i, k):
                wait(act, "lin2_ps", i - 1)
                nc.scalar.activation(fin_z[k], Y[:, ds(i * GW, GW)], ACT.Relu, bias=shift_c, scale=scale_c) \
                    .then_inc(S("z_ready"), 1)

            bn_relu(0, 0)
            bn_relu(1, 1)
            with act.Fori(0, (TURNS - 3) // 2) as j:
                for k in range(2):
                    bn_relu(j * 2 + k + 2, k)
            bn_relu(TURNS - 1, 0)

        @block.vector
        def _(dve):
            vs = nc.vector
            seq = [0]

            def link(ins):
                seq[0] += 1
                ins.then_inc(S("dve_seq"), 1)
                dve.wait_ge(S("dve_seq"), seq[0])

            dve.wait_ge(S("consts_in"), 16)
            vs.tensor_copy(ones_b[:, :], ones_f)
            vs.tensor_copy(before_b[:, :], const("before"))
            link(vs.tensor_copy(blk4_b[:, :, :], const("blk4").rearrange("p (b q) -> p b q", q=G)))
            vs.tensor_tensor(rest_b[:, :], ones_b[:, :], before_b[:, :], ALU.subtract)
            vs.memset(zeros_b[:, :], 0.0)

            dve.wait_ge(S("dst_in"), 32)
            link(vs.tensor_tensor(viol, raw_dst, nxt, ALU.is_gt))
            vs.tensor_reduce(vcol, viol, axis=AX.X, op=ALU.add).then_inc(S("viol_summed"), 1)
            dve.wait_ge(S("src_in"), 16)
            link(vs.tensor_scalar(packed, raw_src, 7, None, ALU.logical_shift_right))
            vs.tensor_copy(sblk, packed).then_inc(S("src_blocks"), 1)
            dve.wait_ge(S("src_blocks"), 1)
            dve.wait_ge(S("type_in"), 16)
            vs.tensor_scalar(packed, raw_src, 18, None, ALU.logical_shift_left)
            link(vs.tensor_scalar(nxt, raw_dst, 4, None, ALU.logical_shift_left))
            link(vs.tensor_tensor(packed, packed, nxt, ALU.bitwise_or))
            link(vs.tensor_scalar(raw_typ, raw_typ, 0.0, float(TYPES - 1), ALU.max, ALU.min))
            vs.tensor_tensor(packed, packed, raw_typ, ALU.bitwise_or).then_inc(S("packed"), 1)
            dve.wait_ge(S("viol_ps"), 1)
            link(vs.tensor_scalar(lo_i[0:1, 0:1], bank(7)[0:1, 0:1], 0.0, None, ALU.is_gt))
            vs.tensor_copy(flag[:, :], lo_i[0:1, 0:1]).then_inc(S("flag_set"), 1)

            link(vs.tensor_copy(tile_end, raw_dst[:, P - 1:COLS:P]))
            dve.wait_ge(S("viol_summed"), 1)
            link(vs.tensor_tensor(tile_lt, tile_end.unsqueeze(1).to_broadcast([P, NBK, TPP]),
                                  const("node").unsqueeze(2).to_broadcast([P, NBK, TPP]), ALU.is_lt))
            vs.tensor_reduce(part_d, tile_lt, axis=AX.X, op=ALU.add).then_inc(S("tiles_counted"), 1)
            dve.wait_ge(S("tiles_ps"), 1)
            link(vs.tensor_tensor(first_d, bank(6)[:, 0:NBK], const("blk"), ALU.add))

            unsorted = dve.value_load(flag[0:1, 0:1], min_val=0, max_val=1)
            with dve.If(unsorted != 0):
                vs.tensor_scalar(raw_dst, raw_dst, 7, None, ALU.logical_shift_right).then_inc(S("dst_blocks"), 1)
                dve.wait_ge(S("dst_blocks"), 1)
                vs.tensor_copy(dblk, raw_dst).then_inc(S("dst_blocks"), 1)
                dve.wait_ge(S("dst_blocks"), 2)
                with dve.Fori(0, NBK) as b:
                    vs.tensor_scalar(junk_v, dblk, cf[:, ds(b + CF["thr"][0], 1)], 0.0, ALU.is_lt, ALU.add,
                                     accum_out=part_d[:, ds(b, 1)]).then_inc(S("hist_d"), 1)
                    dve.wait_ge(S("hist_d"), b + 1)
                dve.wait_ge(S("starts_ps"), 1)
                vs.tensor_copy(start_d, bank(6)[:, 0:NBK])
                vs.tensor_copy(lo_i, bank(6)[:, 0:NBK]).then_inc(S("starts_d"), 1)
                dve.wait_ge(S("starts_d"), 1)
                vs.tensor_scalar(lo_i, lo_i, 7, None, ALU.logical_shift_right).then_inc(S("starts_d"), 1)
                dve.wait_ge(S("starts_d"), 2)
                vs.tensor_tensor(first_d, lo_i, const("blk"), ALU.add).then_inc(S("starts_d"), 1)
                dve.wait_ge(S("starts_d"), 3)
                with dve.Fori(0, COLS // G) as n:
                    vs.tensor_tensor(blk1h[:, 0, :, :], dblk[:, ds(n * G, G)].unsqueeze(1).to_broadcast([P, NBK, G]),
                                     blk4_b[:, :, :], ALU.is_equal).then_inc(S("sort_oh"), 1)
                    dve.wait_ge(S("sort_ps"), n + 1)
                    vs.tensor_tensor(ranked[:, 0, :, :], rank_ps, blk1h[:, 0, :, :], ALU.mult).then_inc(S("sort_mul"), 1)
                    dve.wait_ge(S("sort_mul"), n + 1)
                    vs.tensor_reduce(possl, ranked[:, 0, :, :].rearrange("p b q -> p q b"), axis=AX.X, op=ALU.add)
                    vs.tensor_copy(paysl, packed[:, ds(n * G, G)]).then_inc(S("sort_pos"), 1)
                    dve.wait_ge(S("sort_sent"), n + 1)
                    dve.wait_ge(S("sort_after"), n + 1)

            def step_blocks(first, bstep, tmp):
                link(vs.tensor_tensor(tmp, const("step").unsqueeze(2).to_broadcast([P, SB, BLOCKS - 1]),
                                      first[:, 1:BLOCKS].unsqueeze(1).to_broadcast([P, SB, BLOCKS - 1]), ALU.is_ge))
                link(vs.tensor_reduce(bstep, tmp, axis=AX.X, op=ALU.add))

            step_blocks(first_d, bstep_d, blktmp)
            vs.tensor_scalar(boff_d, bstep_d, float(P), None, ALU.mult)
            vs.tensor_scalar(boff_f, bstep_d, float(P), None, ALU.mult)
            link(vs.tensor_tensor(tile_f, const("step"), bstep_d, ALU.subtract))
            vs.tensor_scalar(tile_i, tile_f, float(TILES - 1), None, ALU.min).then_inc(S("step_tables"), 1)
            vs.memset(ramp_s[:, 0:1], 0.0)

            dve.wait_ge(S("w_in"), 96)
            vs.tensor_tensor(embb[:, :, :], embb[:, :, :], bmsgb[:, :].unsqueeze(1).to_broadcast([P, TYPES, P]), ALU.add)
            vs.tensor_scalar(one_eps, one_eps, 1.0, None, ALU.add)
            link(vs.tensor_tensor(brz, bcol[:, 0:2], bcol[:, 3:5], ALU.add))
            vs.tensor_copy(lastf[:, 2:3], brz[:, 0:1]).then_inc(S("brz_set"), 1)

            mvv = mv.rearrange("p (b t) -> p b t", t=2)

            def norm_stats(j, k):
                i = j * 2 + k
                dve.wait_ge(S(f"x_in{k}"), j * 16 + 16)
                wait(dve, "sd_ready", i)
                plain(dve)
                for b in range(LNG):
                    o = vs.bn_stats(stats[:, b * 6:(b + 1) * 6], xbuf[k][:, b * P:(b + 1) * P])
                o.then_inc(S("bn1"), 1)
                dve.wait_ge(S("bn1"), i + 1)
                plain(dve)
                for b in range(LNG):
                    o = vs.bn_aggr(mv[:, 2 * b:2 * b + 2], stats[:, b * 6:(b + 1) * 6])
                o.then_inc(S("stats_ready"), 1)

            def norm_scale(j, k):
                i = j * 2 + k
                dve.wait_ge(S("sd_ready"), i + 1)
                wait(dve, "h_ready", i - 1)
                vs.reciprocal(rstd[k], sd).then_inc(S("rcp"), 1)
                dve.wait_ge(S("rcp"), i + 1)
                vs.scalar_tensor_tensor(out=nbias[k], in0=mvv[:, :, 0], scalar=-1.0, in1=rstd[k],
                                        op0=ALU.mult, op1=ALU.mult).then_inc(S("rstd_ready"), 1)

            def table_rows(j, k):
                i = j * 2 + k
                dve.wait_ge(S("m_ready"), i + 1)
                for b in range(LNG):
                    slot, n = (k + b) % 2, k * LNG + b
                    wait(dve, f"tab_out{slot}", j * (LNG * 16) + n // 2 * 16)
                    m = bank(4 + 2 * k + b // 4)[:, b % 4 * P:(b % 4 + 1) * P]
                    vs.tensor_tensor(tabt[slot].rearrange("p (t f) -> p t f", f=F),
                                     m.unsqueeze(1).to_broadcast([P, TYPES, P]), embb[:, :, :], ALU.add) \
                        .then_inc(S("tab_ready"), 1)

            norm_stats(0, 0)
            norm_scale(0, 0)
            norm_stats(0, 1)
            with dve.Fori(1, LN_TURNS // 2) as j:
                norm_scale(j - 1, 1)
                norm_stats(j, 0)
                table_rows(j - 1, 0)
                norm_scale(j, 0)
                norm_stats(j, 1)
                table_rows(j - 1, 1)
            norm_scale(LN_TURNS // 2 - 1, 1)
            table_rows(LN_TURNS // 2 - 1, 0)

            dve.wait_ge(S("tiles_in"), SB * 16)
            LOC, TAB, SRC, VAL = fld[4], fld[3], fld[6], fld[5]
            v3 = lambda a: a.rearrange("p (s e) -> p s e", e=P)
            vs.tensor_scalar(fldi[1], fldi[0], 15, None, ALU.bitwise_and)
            link(vs.tensor_scalar(fldi[2], fldi[0], 18, None, ALU.logical_shift_right))
            vs.scalar_tensor_tensor(out=TAB, in0=fldi[1], scalar=float(NPAD), in1=fldi[2], op0=ALU.mult, op1=ALU.add) \
                .then_inc(S("field"), 1)
            dve.wait_ge(S("field"), 1)
            table_rows(LN_TURNS // 2 - 1, 1)
            dve.wait_ge(S("ramp_s"), BLOCKS)
            vs.memset(part_s[:, 0:1], 0.0)
            vs.tensor_tensor(part_s[:, 1:NBK], ramp_s[:, 1:NBK], ramp_s[:, 0:NBK - 1], ALU.subtract) \
                .then_inc(S("src_counted"), 1)
            link(vs.tensor_scalar(fldi[1], fldi[0], 4, 16383, ALU.logical_shift_right, ALU.bitwise_and))
            link(vs.tensor_tensor(v3(LOC), v3(fldi[1]), boff_f.unsqueeze(2).to_broadcast([P, SB, P]), ALU.subtract))
            link(vs.tensor_scalar(VAL, LOC, 0.0, None, ALU.is_ge))
            link(vs.scalar_tensor_tensor(out=VAL, in0=LOC, scalar=float(P), in1=VAL, op0=ALU.is_lt, op1=ALU.mult))
            link(vs.scalar_tensor_tensor(out=LOC, in0=LOC, scalar=-FAR, in1=VAL, op0=ALU.add, op1=ALU.mult))
            link(vs.tensor_scalar(LOC, LOC, FAR, None, ALU.add))
            vs.tensor_copy(lastf[:, 3:4], LOC[:, 0:1]).then_inc(S("field"), 1)
            link(vs.scalar_tensor_tensor(out=SRC, in0=fldi[2], scalar=-16383.0, in1=VAL, op0=ALU.add, op1=ALU.mult))
            link(vs.tensor_scalar(SRC, SRC, 16383.0, None, ALU.add))
            vs.tensor_copy(lastf[:, 4:5], SRC[:, 0:1]).then_inc(S("field"), 1)
            vs.tensor_copy(fld[1].bitcast(bf16)[:, 0:SW], LOC).then_inc(S("loc_ready"), 1)

            def place_idx(c, k):
                vs.tensor_copy(idxslot[:, k, :], tabE[:, ds(c * CH, CH)]).then_inc(S("idx_ready"), 1)

            dve.wait_ge(S("fields_moved"), 4)
            place_idx(0, 0)
            place_idx(1, 1)
            dve.wait_ge(S("starts_ps_s"), 1)
            dve.wait_ge(S("fields_moved"), 8)
            link(vs.tensor_copy(lo_i, bank(7)[:, 256:256 + NBK]))
            link(vs.tensor_scalar(lo_i, lo_i, 7, None, ALU.logical_shift_right))
            link(vs.tensor_tensor(first_s, lo_i, const("blk"), ALU.add))
            vs.tensor_scalar(base_s, first_s, float(P), None, ALU.mult).then_inc(S("base_s"), 1)
            link(vs.tensor_scalar(lasti[0][0:1, :], first_s[0:1, 1:NBK], -1.0, None, ALU.add))
            link(vs.tensor_scalar(lasti[1][0:1, :], first_s[0:1, 1:NBK], -2.0, 0.0, ALU.add, ALU.max))
            for a in range(2):
                vs.tensor_scalar(lastrow[0:1, a, 0, :], lasti[a][0:1, :], 4, None, ALU.logical_shift_right)
                link(vs.tensor_scalar(lastrow[0:1, a, 1, :], lasti[a][0:1, :], CH - 1, None, ALU.bitwise_and))
            dve.wait_ge(S("fields_moved"), 12)
            step_blocks(first_s, bstep_s, blktmp)
            vs.tensor_scalar(boff_s, bstep_s, float(P), None, ALU.mult).then_inc(S("src_tables"), 1)
            link(vs.tensor_scalar(fldi[3], fldi[2], 7, None, ALU.logical_shift_right))
            vs.tensor_copy(sblkE[:, :], fldi[3])
            link(vs.tensor_scalar(fldi[4], fldi[2], P - 1, None, ALU.bitwise_and))
            link(vs.tensor_copy(skeyE[:, :], fldi[4]))
            dve.wait_ge(S("loc_out"), 16)
            link(vs.memset(Y[:, :], 0.0))

            def step_onehots(c, k):
                wait(dve, "agg_done", (c - 1) * GPC)
                vs.tensor_tensor(oh[:, k, :, :], locE[:, ds(c * CH, CH)].unsqueeze(2).to_broadcast([P, CH, P]),
                                 iota_f.unsqueeze(1).to_broadcast([P, CH, P]), ALU.is_equal).then_inc(S("oh_ready"), 1)

            def block_onehots(n, slot):
                wait(dve, "rank_counted", n - 3)
                vs.tensor_tensor(blk1h[:, slot, :, :], sblkE[:, ds(n * G, G)].unsqueeze(1).to_broadcast([P, NBK, G]),
                                 blk4_b[:, :, :], ALU.is_equal).then_inc(S("blk_ready"), 1)

            regs = [dve.alloc_register(f"group_off{q}") for q in range(GPC)]

            def group_offsets(c):
                vs.load(regs, steprow[0:1, ds(c * CH, CH)].rearrange("p (g q) -> p g q", q=G)[:, :, 0])
                return [dve.snap(r, min_val=0, max_val=(BLOCKS - 1) * P) for r in regs]

            def layer0(j, k):
                c = j * 2 + k
                offs = group_offsets(c)
                for g in range(GPC):
                    n = c * GPC + g
                    dve.wait_ge(S("rank_ps"), n + 1)
                    vs.tensor_tensor(ranked[:, g % 2, :, :], rank_ps, blk1h[:, g, :, :], ALU.mult).then_inc(S("rank_read"), 1)
                    block_onehots(n + 1, (g + 1) % G)
                    dve.wait_ge(S("rank_read"), n + 1)
                    vs.tensor_reduce(posE[:, ds(n * G, G)], ranked[:, g % 2, :, :].rearrange("p b q -> p q b"),
                                     axis=AX.X, op=ALU.add)
                    if g == 1:
                        dve.wait_ge(S(f"gathered{k}"), j * (CH * 16) + CH * 16)
                        place_idx(c + 2, k)
                    if g == 2:
                        step_onehots(c + 1, 1 - k)
                    dve.wait_ge(S("agg_done"), n + 1)
                    wait(dve, "agg_added", n)
                    yb = Y[:, ds(offs[g], 512)]
                    vs.tensor_tensor(yb, yb, bank(1 + g), ALU.add).then_inc(S("agg_added"), 1)

            dve.wait_ge(S("steprow_in"), 16)
            dve.wait_ge(S("hT_kept"), LN_TURNS)
            for k in range(2):
                dve.wait_ge(S(f"tab_out{k}"), BLOCKS // 2 * 16)
            step_onehots(0, 0)
            block_onehots(0, 0)
            for k in range(2):
                layer0(0, k)
            with dve.Fori(1, PAIRS) as j:
                for k in range(2):
                    layer0(j, k)

            ta, tb = ringf[:, 0:STEPS_P].bitcast(i32), ringf[:, STEPS_P:2 * STEPS_P].bitcast(i32)
            dve.wait_ge(S("agg_added"), GROUPS)
            pe_, ta_, tb_ = posE[:, :], ta, tb
            vs.tensor_scalar(ta_, pe_, 127, 4, ALU.bitwise_and, ALU.logical_shift_left)
            link(vs.tensor_scalar(tb_, pe_, 7, CH - 1, ALU.logical_shift_right, ALU.bitwise_and))
            link(vs.tensor_tensor(ta_, ta_, tb_, ALU.bitwise_or))
            link(vs.tensor_scalar(tb_, pe_, 11, 11, ALU.logical_shift_right, ALU.logical_shift_left))
            link(vs.tensor_tensor(ta_, ta_, tb_, ALU.bitwise_or))
            link(vs.tensor_scalar(tb_, sblkE[:, 0:STEPS_P], float(BLOCKS), float(SKIP), ALU.is_ge, ALU.mult))
            link(vs.tensor_tensor(pe_, ta_, tb_, ALU.max))
            link(vs.memset(ringf, 0.0))
            vs.tensor_copy(lastf[:, 5:6], ringf[:, 0:1]).then_inc(S("ring_cleared"), 1)

            def cell_a(i, k):
                dve.wait_ge(S("gates_rz"), i + 1)
                wait(dve, "cand", i - 1)
                vs.scalar_tensor_tensor(out=tbuf[k], in0=bank(2 * k + 1)[:, GW:2 * GW], scalar=bcol[:, 5:6], in1=rbuf[k],
                                        op0=ALU.add, op1=ALU.mult).then_inc(S("cell_t"), 1)
                dve.wait_ge(S("cell_t"), i + 1)
                vs.tensor_tensor(tbuf[k], tbuf[k], bank(2 * k + 1)[:, 0:GW], ALU.add).then_inc(S("cand_in"), 1)

            def cell_b(i, k):
                dve.wait_ge(S("cand"), i + 1)
                wait(dve, "x1_ps", i - 1)
                vs.tensor_tensor(hnbuf[k], H[:, ds(i * GW, GW)], nbuf[k], ALU.subtract).then_inc(S("cell_h"), 1)
                dve.wait_ge(S("cell_h"), i + 1)
                vs.tensor_tensor(hnbuf[k], hnbuf[k], zbuf[k], ALU.mult).then_inc(S("hn_ready"), 1)

            def cell_c(i, k):
                dve.wait_ge(S("x1_kept"), i + 1)
                plain(dve)
                for b in range(NG):
                    o = vs.bn_stats(stats[:, b * 6:(b + 1) * 6], H[:, ds(i * GW + b * P, P)])
                o.then_inc(S("bn2"), 1)
                dve.wait_ge(S("bn2"), i + 1)
                plain(dve)
                for b in range(NG):
                    o = vs.bn_aggr(mv[:, 2 * b:2 * b + 2], stats[:, b * 6:(b + 1) * 6])
                o.then_inc(S("bn3"), 1)
                dve.wait_ge(S("bn3"), i + 1)
                vs.tensor_copy(mvn[:, ds(i * 2 * NG, 2 * NG)], mv[:, 0:2 * NG]).then_inc(S("x1_stats"), 1)

            cell_a(0, 0)
            cell_a(1, 1)
            cell_b(0, 0)
            with dve.Fori(0, (TURNS - 3) // 2) as j:
                for k in range(2):
                    i = j * 2 + k + 2
                    cell_a(i, k)
                    cell_b(i - 1, 1 - k)
                    cell_c(i - 2, k)
            cell_a(TURNS - 1, 0)
            cell_b(TURNS - 2, 1)
            cell_c(TURNS - 3, 0)
            cell_b(TURNS - 1, 0)
            cell_c(TURNS - 2, 1)
            cell_c(TURNS - 1, 0)

            dve.wait_ge(S("sdn_ready"), 1)
            link(vs.reciprocal(rstdn, sdn))
            vs.scalar_tensor_tensor(out=nbn, in0=mvn.rearrange("p (b t) -> p b t", t=2)[:, :, 0], scalar=-1.0, in1=rstdn,
                                    op0=ALU.mult, op1=ALU.mult).then_inc(S("rstdn_ready"), 1)

            def h2_own(i, k):
                dve.wait_ge(S("h2_ready"), i + 1)
                vs.tensor_copy(H[:, ds(i * GW, GW)], hs[k]).then_inc(S("h2_kept"), 1)
                dve.wait_ge(S("h2_ps"), i + 1)
                vs.tensor_scalar(Y[:, ds(i * GW, GW)], bank(k)[:, 0:GW], one_eps, None, ALU.mult).then_inc(S("h2_done"), 1)

            h2_own(0, 0)
            with dve.Fori(0, (TURNS - 1) // 2) as j:
                for k in range(2):
                    h2_own(j * 2 + k + 1, (k + 1) % 2)

            dve.wait_ge(S("h2_kept"), TURNS)
            def layer1_pick(j, k):
                c = j * 2 + k
                wait(dve, f"scattered{k}", j * (CH * 16))
                vs.tensor_copy(ring[:, k * CH:(k + 1) * CH, KEY:KEY + 1],
                               skeyE[:, ds(c * CH, CH)].unsqueeze(2))
                vs.tensor_copy(idxslot[:, k, :], posE[:, ds(c * CH, CH)]).then_inc(S("keyed"), 1)
                dve.wait_ge(S(f"locb_in{k}"), j * 16 + 16)
                for g in range(GPC):
                    wait(dve, "picked", c * GPC + g - 3)
                    vs.tensor_scalar(pick[g], locb[k][:, g * 512:(g + 1) * 512], iota_p, None, ALU.is_equal) \
                        .then_inc(S("pick_oh"), 1)

            for k in range(2):
                layer1_pick(0, k)
            with dve.Fori(1, PAIRS) as j:
                for k in range(2):
                    layer1_pick(j, k)

            def key_onehots(c, jn, k):
                dve.wait_ge(S(f"rows_in{k}"), jn * 16 + 16)
                wait(dve, "sum_done", (c - 1) * GPC)
                vs.tensor_tensor(oh[:, k, :, :], ring[:, k * CH:(k + 1) * CH, KEY:KEY + 1].to_broadcast([P, CH, P]),
                                 iota_f.unsqueeze(1).to_broadcast([P, CH, P]), ALU.is_equal).then_inc(S("key_oh"), 1)

            def layer1_sum(j, k, last=False):
                c = j * 2 + k
                offs = group_offsets(c)
                for g in range(GPC):
                    n = c * GPC + g
                    if g == 1 and not last:
                        key_onehots(c + 1, j + k, 1 - k)
                    dve.wait_ge(S("sum_done"), n + 1)
                    wait(dve, "sum_added", n)
                    yb = Y[:, ds(offs[g], 512)]
                    vs.tensor_tensor(yb, yb, bank(1 + g), ALU.add).then_inc(S("sum_added"), 1)

            dve.wait_ge(S("steprow_in"), 32)
            dve.wait_ge(S("picked"), GROUPS)
            key_onehots(0, 0, 0)
            for k in range(2):
                layer1_sum(0, k)
            with dve.Fori(1, PAIRS - 1) as j:
                for k in range(2):
                    layer1_sum(j, k)
            layer1_sum(PAIRS - 1, 0)
            layer1_sum(PAIRS - 1, 1, last=True)

            dve.wait_ge(S("lin1"), TURNS)
            link(vs.tensor_reduce(msum, fsum, axis=AX.X, op=ALU.add))
            vs.tensor_scalar(negmu, msum, -1.0 / N, None, ALU.mult).then_inc(S("negmu_ready"), 1)
            dve.wait_ge(S("sq_ready"), 1)
            vs.tensor_copy(lastf[:, 6:7], sq).then_inc(S("sq_scaled"), 1)
            dve.wait_ge(S("bsd_ready"), 1)
            link(vs.reciprocal(brs, bsd))
            link(vs.tensor_tensor(scale_c, brs, bcol[:, 7:8], ALU.mult))
            vs.scalar_tensor_tensor(out=shift_c, in0=negmu, scalar=scale_c, in1=bcol[:, 8:9],
                                    op0=ALU.mult, op1=ALU.add).then_inc(S("bn_ready"), 1)

            def final(i, k, count):
                dve.wait_ge(S("lin2_ps"), i + 1)
                dve.wait_ge(S(f"fin_x{k}"), count * 16 + 16)
                wait(dve, f"out_done{k}", count * 16)
                vs.tensor_tensor(fin_o[k], fin_x[k], bank(k)[:, 0:GW], ALU.add).then_inc(S("out_ready"), 1)

            final(0, 0, 0)
            final(1, 1, 0)
            with dve.Fori(1, (TURNS - 1) // 2) as j:
                for k in range(2):
                    final(j * 2 + k, k, j)
            final(TURNS - 1, 0, (TURNS - 1) // 2)

        @block.tensor
        def _(pe):
            mm = nc.tensor.matmul
            pe.wait_ge(S("viol_summed"), 1)
            mm(bank(7)[:, 0:1], ones_f, vcol, start=True, stop=True).then_inc(S("viol_ps"), 1)
            pe.wait_ge(S("tiles_counted"), 1)
            mm(bank(6)[:, 0:NBK], ones_f, part_d, start=True, stop=True).then_inc(S("tiles_ps"), 1)
            pe.wait_ge(S("flag_set"), 1)
            unsorted = pe.value_load(flag[0:1, 0:1], min_val=0, max_val=1)
            with pe.If(unsorted != 0):
                pe.wait_ge(S("hist_d"), NBK)
                mm(bank(6)[:, 0:NBK], ones_f, part_d, start=True, stop=True).then_inc(S("starts_ps"), 1)
                pe.wait_ge(S("starts_d"), 1)
                mm(rank_ps, ident, start_d.unsqueeze(2).to_broadcast([P, NBK, G]), start=True, stop=True)
                with pe.Fori(0, COLS // G) as n:
                    pe.wait_ge(S("sort_oh"), n + 1)
                    rank_before(0).then_inc(S("sort_ps"), 1)
                    pe.wait_ge(S("sort_mul"), n + 1)
                    rank_after(0).then_inc(S("sort_after"), 1)

            pe.wait_ge(S("w_in"), 96)
            pe.wait_ge(S("step_tables"), 1)

            def norm0(j, k):
                i = j * 2 + k
                pe.wait_ge(S("h_ready"), i + 1)
                for b in range(LNG):
                    o = nc.tensor.transpose(bank(2 * k + b // 4)[:, b % 4 * P:(b % 4 + 1) * P],
                                            hbuf[k][:, b * P:(b + 1) * P], ident)
                o.then_inc(S("hT_ps"), 1)
                pe.wait_ge(S("hT_ready"), i + 1)
                wait(pe, "tab_ready", (i - 1) * LNG)
                for b in range(LNG):
                    o = mm(bank(4 + 2 * k + b // 4)[:, b % 4 * P:(b % 4 + 1) * P], hTs[k][:, b * P:(b + 1) * P],
                           wT[:, 0, :], start=True, stop=True)
                o.then_inc(S("m_ready"), 1)

            for k in range(2):
                norm0(0, k)
            with pe.Fori(1, LN_TURNS // 2) as j:
                for k in range(2):
                    norm0(j, k)

            pe.wait_ge(S("hT_ready"), LN_TURNS)
            for f, (src_f, need) in enumerate(((fld[3], 1), (fld[4], 2), (fld[6], 3))):
                pe.wait_ge(S("field"), need)
                if f == 1:
                    pe.wait_ge(S("tab_ready"), BLOCKS)
                    pe.wait_ge(S("src_counted"), 1)
                    mm(bank(7)[:, 256:256 + NBK], ones_f, part_s, start=True, stop=True).then_inc(S("starts_ps_s"), 1)
                for a in range(4):
                    if f == 2:
                        pe.wait_ge(S("fields_moved"), a + 1)
                    for s in range(a * 4, min(a * 4 + 4, SB)):
                        o = nc.tensor.transpose(bank((f % 2) * 4 + a)[:, s % 4 * P:(s % 4 + 1) * P],
                                                src_f[:, s * P:(s + 1) * P], ident)
                    o.then_inc(S("fields_T"), 1)

            regs = [pe.alloc_register(f"step_off{q}") for q in range(CH)]

            def step_offsets(c):
                nc.tensor.load(regs, steprow[0:1, ds(c * CH, CH)])

            def rel(g, q):
                first = pe.snap(regs[g * G], min_val=0, max_val=(BLOCKS - 1) * P)
                own = pe.snap(regs[g * G + q], min_val=0, max_val=(BLOCKS - 1) * P)
                return nc.s_assert_within(pe.snap(own - first), 0, q * P, 
                                          skip_runtime_bounds_check_because="consecutive steps' blocks differ by 0 or 1")

            def sum_group(g, k, free, free_value, done):
                wait(pe, free, free_value)
                mm(bank(1 + g), zeros_b[:, 0:P], zeros_b[:, :], start=True, stop=True, skip_group_check=True)
                for q in range(G):
                    s = g * G + q
                    o = bank(1 + g)[:, 0:P] if q == 0 else ps[:, 1 + g, ds(rel(g, q), P)]
                    m = mm(o, ring[:, k * CH + s, 0:F], oh[:, k, s, :], start=False, stop=True, skip_group_check=True)
                m.then_inc(S(done), 1)

            def layer0(j, k):
                c = j * 2 + k
                step_offsets(c)
                for g in range(GPC):
                    n = c * GPC + g
                    if not isinstance(n, int) or n > 0:
                        pe.wait_ge(S("rank_read"), n)
                        rank_after((g + 3) % G).then_inc(S("rank_counted"), 1)
                    pe.wait_ge(S("blk_ready"), n + 1)
                    rank_before(g).then_inc(S("rank_ps"), 1)
                    if g == 0:
                        pe.wait_ge(S("oh_ready"), c + 1)
                        pe.wait_ge(S(f"gathered{k}"), j * (CH * 16) + CH * 16)
                    sum_group(g, k, "agg_added", n - 3, "agg_done")

            pe.wait_ge(S("fields_moved"), 12)
            pe.wait_ge(S("steprow_in"), 16)
            pe.wait_ge(S("base_s"), 1)
            mm(rank_ps, ident, base_s.unsqueeze(2).to_broadcast([P, NBK, G]), start=True, stop=True)
            for k in range(2):
                layer0(0, k)
            with pe.Fori(1, PAIRS) as j:
                for k in range(2):
                    layer0(j, k)

            pe.wait_ge(S("agg_added"), GROUPS)

            def gates(i, k):
                wait(pe, "cand_in", i - 1)
                msg, h = Y[:, ds(i * GW, GW)], H[:, ds(i * GW, GW)]
                for a in range(2):
                    o = bank(2 * k)[:, a * GW:(a + 1) * GW]
                    mm(o, wT[:, 1 + a, :], msg, start=True, stop=False)
                    mm(o, wT[:, 4 + a, :], h, start=False, stop=True)
                mm(bank(2 * k + 1)[:, 0:GW], wT[:, 3, :], msg, start=True, stop=True)
                mm(bank(2 * k + 1)[:, GW:2 * GW], wT[:, 6, :], h, start=True, stop=True).then_inc(S("gates_ps"), 1)

            def back(i, k, count):
                pe.wait_ge(S("hn_ready"), i + 1)
                pe.wait_ge(S(f"cell_x{k}"), count * 16 + 16)
                wait(pe, "x1_kept", i - 1)
                for b in range(NG):
                    own = slice(b * P, (b + 1) * P)
                    o = bank(4 + k)[:, own]
                    mm(o, nbuf[k][:, own], ident, start=True, stop=False)
                    mm(o, hnbuf[k][:, own], ident, start=False, stop=False)
                    m = mm(o, ident, cell_x[k][:, own], start=False, stop=True)
                m.then_inc(S("x1_ps"), 1)

            gates(0, 0)
            gates(1, 1)
            for k in range(2):
                gates(k + 2, k)
                back(k, k, 0)
            with pe.Fori(1, (TURNS - 3) // 2) as j:
                for k in range(2):
                    gates(j * 2 + k + 2, k)
                    back(j * 2 + k, k, j)
            gates(TURNS - 1, 0)
            for i in range(TURNS - 3, TURNS):
                back(i, i % 2, i // 2)

            def h2T(i, k):
                pe.wait_ge(S("h2_ready"), i + 1)
                wait(pe, "h2_done", i - 1)
                for b in range(NG):
                    o = nc.tensor.transpose(bank(k)[:, b * P:(b + 1) * P], hs[k][:, b * P:(b + 1) * P], ident)
                o.then_inc(S("h2_ps"), 1)

            h2T(0, 0)
            h2T(1, 1)
            with pe.Fori(0, (TURNS - 3) // 2) as j:
                for k in range(2):
                    h2T(j * 2 + k + 2, k)
            h2T(TURNS - 1, 0)

            def picks(j, k):
                c = j * 2 + k
                step_offsets(c)
                for g in range(GPC):
                    n = c * GPC + g
                    pe.wait_ge(S("pick_oh"), n + 1)
                    wait(pe, "row_moved", n - 3)
                    for q in range(G):
                        off = pe.snap(regs[g * G + q], min_val=0, max_val=(BLOCKS - 1) * P)
                        m = mm(bank(g)[:, q * P:(q + 1) * P], pick[g][:, q * P:(q + 1) * P], H[:, ds(off, P)],
                               start=True, stop=True)
                    m.then_inc(S("picked"), 1)

            pe.wait_ge(S("h2_kept"), TURNS)
            pe.wait_ge(S("h2_done"), TURNS)
            for k in range(2):
                picks(0, k)
            with pe.Fori(1, PAIRS) as j:
                for k in range(2):
                    picks(j, k)

            def layer1_sum(j, k):
                c = j * 2 + k
                step_offsets(c)
                pe.wait_ge(S("key_oh"), c + 1)
                for g in range(GPC):
                    sum_group(g, k, "sum_added", c * GPC + g - 3, "sum_done")

            pe.wait_ge(S("steprow_in"), 32)
            pe.wait_ge(S("row_moved"), GROUPS)
            for k in range(2):
                layer1_sum(0, k)
            with pe.Fori(1, PAIRS) as j:
                for k in range(2):
                    layer1_sum(j, k)

            pe.wait_ge(S("sum_added"), GROUPS)

            def lin1(i, k):
                wait(pe, "lin1", i - 1)
                mm(bank(4 + k)[:, 0:GW], wT[:, 7, :], Y[:, ds(i * GW, GW)], start=True, stop=True).then_inc(S("lin1_ps"), 1)

            lin1(0, 0)
            lin1(1, 1)
            with pe.Fori(1, (TURNS - 1) // 2) as j:
                for k in range(2):
                    lin1(j * 2 + k, k)
            lin1(TURNS - 1, 0)

            def lin2(i, k):
                pe.wait_ge(S("z_ready"), i + 1)
                wait(pe, "out_ready", i - 1)
                for b in range(NG):
                    o = bank(k)[:, b * P:(b + 1) * P]
                    mm(o, fin_z[k][:, b * P:(b + 1) * P], wT[:, 8, :], start=True, stop=False)
                    m = mm(o, ones_f[0:1, :], b2row[:, :], start=False, stop=True)
                m.then_inc(S("lin2_ps"), 1)

            lin2(0, 0)
            lin2(1, 1)
            with pe.Fori(1, (TURNS - 1) // 2) as j:
                for k in range(2):
                    lin2(j * 2 + k, k)
            lin2(TURNS - 1, 0)


def shape_constants(np):
    c = np.zeros((P, CF_W), np.float32)

    def put(name, value):
        a, w = CF[name]
        c[:, a:a + w] = value

    put("ident", np.eye(P))
    put("ones", 1.0)
    put("before", np.triu(np.ones((P, P)), 1))
    put("iota", np.arange(P))
    put("iota_p", np.arange(P)[:, None])
    put("thr", np.arange(NBK) - 0.5)
    put("node", np.arange(NBK) * P - 0.5)
    put("blk", np.arange(NBK))
    put("step", np.arange(SB) * P + np.arange(P)[:, None])
    put("lneps", LN_EPS)
    put("bneps", BN_EPS)
    put("pad", np.where(np.arange(RW) == KEY, FAR, 0.0))
    put("blk4", np.repeat(np.arange(NBK), G))
    return c


def kernel(x, src, dst, edge_type_9, L0_gnn_W_msg, L0_gnn_b_msg, L0_gnn_edge_embed, L0_gnn_W_ih, L0_gnn_W_hh,
           L0_gnn_b_ih, L0_gnn_b_hh, L1_gnn_eps, L1_gnn_W1, L1_gnn_b1, L1_gnn_gamma, L1_gnn_beta, L1_gnn_W2, L1_gnn_b2):
    import numpy as np
    import concourse.bacc as bacc
    from concourse.bass_utils import run_bass_kernel_spmd

    def a(v):
        return np.asarray(v)

    def edge_rows(v, pad):
        return np.concatenate([a(v).astype(np.int32), np.full(EPAD - len(v), pad, np.int32)]).reshape(P, COLS)

    w_ih, w_hh = a(L0_gnn_W_ih), a(L0_gnn_W_hh)
    mats = [a(L0_gnn_W_msg)] + [w_ih[k * F:(k + 1) * F] for k in range(3)] + [w_hh[k * F:(k + 1) * F] for k in range(3)] \
        + [a(L1_gnn_W1), a(L1_gnn_W2)]
    b_ih, b_hh = a(L0_gnn_b_ih).reshape(3, F), a(L0_gnn_b_hh).reshape(3, F)
    arrays = {
        "in_x": np.concatenate([a(x), np.zeros((NPAD - N, F), np.float32)]),
        "in_edges": np.stack([edge_rows(dst, PADNODE), edge_rows(src, PADNODE), edge_rows(edge_type_9, 0)]),
        "in_dst_next": edge_rows(a(dst)[1:], PADNODE),
        "in_weights": np.ascontiguousarray(np.concatenate([m.T for m in mats], axis=1)),
        "in_bias_cols": np.ascontiguousarray(np.stack([*b_ih, *b_hh, a(L1_gnn_b1), a(L1_gnn_gamma), a(L1_gnn_beta)], axis=1)),
        "in_embed": a(L0_gnn_edge_embed),
        "in_b_msg": a(L0_gnn_b_msg),
        "in_b2": a(L1_gnn_b2),
        "in_eps": a(L1_gnn_eps).reshape(1, 1),
        "in_consts": shape_constants(np),
    }
    nc = bacc.Bacc("TRN2", target_bir_lowering=False, num_devices=1)
    args = [nc.dram_tensor(n, v.shape, mybir.dt.from_np(v.dtype), kind="ExternalInput").ap() for n, v in arrays.items()]
    out = nc.dram_tensor("out_x", (NPAD, F), mybir.dt.float32, kind="ExternalOutput").ap()
    build_gnn(nc, *args, out)
    r = run_bass_kernel_spmd(nc, [arrays], core_ids=[0])
    return r.results[0]["out_x"][:N]
```

```python
from contextlib import ExitStack

import concourse.bass as bass
from concourse import mybir

N, F, E, TYPES = 12500, 128, 212500, 9
P = 128
BLOCKS = -(-N // P)
NPAD = BLOCKS * P
COLS = 1664
EPAD = COLS * P
TILES = EPAD // P
TPP = TILES // P
STEPS = E // P + BLOCKS
CH = 16
PAIRS = -(-STEPS // (2 * CH))
CHUNKS = 2 * PAIRS
STEPS_P = CHUNKS * CH
G = 4
GPC = CH // G
GROUPS = STEPS_P // G
RSLOTS = 4
BODIES = CHUNKS // RSLOTS
V_PIECES = 3
OH_V, OH_P = 7, 5
SB = -(-STEPS_P // P)
SW = SB * P
RW = 136
KEY = F
FAR = 255.0
NBK = BLOCKS + 1
PADNODE = BLOCKS * P
LNG = 7
LNW = LNG * P
LN_TURNS = BLOCKS // LNG
EARLY, PER_TURN = 14, 5
RAMPS = EARLY + PER_TURN * LN_TURNS
TSLOTS = 4
TUSES = [len(range(r, 2 * LNG, TSLOTS)) for r in range(TSLOTS)]
NG = 2
GW = NG * P
TURNS = BLOCKS // NG
HSLOTS = 4
FIN = 7
SQ_PASSES = 4
SQW = N // SQ_PASSES
FINW = NPAD // FIN
ROWS_D = STEPS_P * P
SKIP = 1 << 20
LN_EPS = 1e-5
BN_EPS = 1e-5
CF = {}
for _name, _width in (("ident", P), ("ones", P), ("before", P), ("iota", P), ("iota_p", 1), ("thr", NBK), ("node", NBK),
                      ("blk", NBK), ("step", SB), ("lneps", 1), ("bneps", 1), ("pad", RW), ("blk4", NBK * G)):
    CF[_name] = (sum(w for _, w in CF.values()), _width)
CF_W = sum(w for _, w in CF.values())


def build_gnn(nc, x, edges, dst_next, weights, bias_cols, embed, b_msg, b2, eps1, consts, out):
    f32, i32, bf16 = mybir.dt.float32, mybir.dt.int32, mybir.dt.bfloat16
    ALU, ACT, AX = mybir.AluOpType, mybir.ActivationFunctionType, mybir.AxisListType
    ds = bass.ds
    ctx = ExitStack()
    with ctx:
        ctx.enter_context(nc.allow_non_contiguous_dma(reason="small step tables"))
        ctx.enter_context(nc.allow_low_precision(reason="sums of indices into int32: exact below 2**24"))

        def sb(name, shape, dt=f32):
            return ctx.enter_context(nc.sbuf_tensor("sb_" + name, shape, dt))

        held = {}

        def S(name):
            if name not in held:
                held[name] = ctx.enter_context(nc.semaphore(name))
            return held[name]

        def wait(engine, name, value):
            if not isinstance(value, int) or value > 0:
                engine.wait_ge(S(name), value)

        def plain(engine):
            engine.sem_inc(S("passed"), 1)

        table_d = nc.dram_tensor("msg_table", (TYPES * NPAD, F), f32).ap()
        packed_d = nc.dram_tensor("packed_edges", (TILES, P), i32).ap()
        blockrow_d = nc.dram_tensor("step_block_offsets", (2, SW), i32).ap()
        loc_d = nc.dram_tensor("step_targets", (SW, P), bf16).ap()
        rows_d = nc.dram_tensor("rows_by_src", (ROWS_D, RW), f32).ap()
        x1_d = nc.dram_tensor("x_after_layer0", (NPAD, F), f32).ap()

        H = sb("H", [P, NPAD])
        Y = sb("Y", [P, NPAD + (G - 1) * P])
        ring = sb("ring", [P, 2 * CH, RW])
        oh = sb("oh", [P, 2, CH, P])
        locE = sb("locE", [P, SW])
        tabE = sb("tabE", [P, SW])
        skeyE = sb("skeyE", [P, SW])
        sblkE = sb("sblkE", [P, SW], bf16)
        posE = sb("posE", [P, STEPS_P], i32)
        steprow = sb("steprow", [1, STEPS_P], i32)
        idxslot = sb("idxslot", [P, 2, CH], i32)
        cf = sb("cf", [P, CF_W])
        ones_b = sb("ones_b", [P, P], bf16)
        before_b = sb("before_b", [P, P], bf16)
        rest_b = sb("rest_b", [P, P], bf16)
        zeros_b = sb("zeros_b", [P, 512], bf16)
        blk4_b = sb("blk4_b", [P, NBK, G], bf16)
        blk1h = sb("blk1h", [P, G, NBK, G], bf16)
        ranked = sb("ranked", [P, 2, NBK, G])
        wT = sb("wT", [P, 9, P])
        embb = sb("embb", [P, TYPES, P])
        bmsgb = sb("bmsgb", [P, P])
        b2b = sb("b2b", [P, P])
        bcol = sb("bcol", [P, 9])
        scol = sb("scol", [P, 12])
        smalls = sb("smalls", [P, 2100])
        flag = sb("flag", [1, 1], i32)
        lastrow = sb("lastrow", [1, 2, 2, BLOCKS], i32)
        ps = ctx.enter_context(nc.psum_tensor("ps", [P, 8, 512], f32))

        def const(name):
            a, w = CF[name]
            return cf[:, a:a + w]

        ident, ones_f, iota_f, iota_p = const("ident"), const("ones"), const("iota"), const("iota_p")

        def yv(k, dt):
            return Y[:, k * COLS:(k + 1) * COLS].bitcast(dt) if dt is not f32 else Y[:, k * COLS:(k + 1) * COLS]

        raw_dst, raw_src, raw_typ, packed, nxt = (yv(k, i32) for k in range(5))
        dblk, sblk = yv(5, bf16)[:, 0:COLS], yv(5, bf16)[:, COLS:2 * COLS]
        junk_v, junk_a = yv(6, bf16)[:, 0:COLS], yv(6, bf16)[:, COLS:2 * COLS]
        viol = H[:, 0:COLS]
        tile_lt = viol[:, 0:NBK * TPP].rearrange("p (b t) -> p b t", t=TPP)
        blktmp = Y[:, 7 * COLS:7 * COLS + 1024].bitcast(bf16)[:, 0:SB * (BLOCKS - 1)] \
            .rearrange("p (s b) -> p s b", s=SB)
        fld = [Y[:, k * SW:(k + 1) * SW] for k in range(7)]
        fldi = [v.bitcast(i32) for v in fld]

        rrows = [H[:, k * CH * RW:(k + 1) * CH * RW].rearrange("p (s w) -> p s w", w=RW) for k in range(RSLOTS)]
        ringf = ring[:, :, :].rearrange("p a b -> p (a b)")
        ohf = oh[:, :, :, :].rearrange("p a b c -> p (a b c)")
        xbuf = [ringf[:, k * LNW:(k + 1) * LNW] for k in range(2)]
        hbuf = [ringf[:, (2 + k) * LNW:(3 + k) * LNW] for k in range(2)]
        hTs = [ohf[:, k * LNW:(k + 1) * LNW] for k in range(2)]
        TW = TYPES * P
        tabt = [ohf[:, 2 * LNW + k * TW:2 * LNW + (k + 1) * TW] for k in range(2)] \
            + [posE[:, 0:TW].bitcast(f32), skeyE[:, 0:TW]]

        def ob(k):
            return ohf[:, k * GW:(k + 1) * GW]

        rbuf, zbuf, tbuf, nbuf, hnbuf, cell_x = ([ob(2 * a + k) for k in range(2)] for a in range(6))
        hs = [ob(12 + k) for k in range(HSLOTS)]
        locb = [ohf[:, k * 1024:(k + 1) * 1024].bitcast(bf16) for k in range(2)]
        pick = [ohf[:, 2048 + k * 512:2048 + (k + 1) * 512] for k in range(4)]
        fin_z = [ob(k) for k in range(2)]

        at = [0]

        def small(n, dt=f32):
            v = smalls[:, at[0]:at[0] + n]
            at[0] += n
            return v if dt is f32 else v.bitcast(dt)

        part_d, part_s = small(NBK), small(NBK)
        start_d, start_s = small(NBK), small(NBK)
        lo_i = small(NBK, i32)
        ramp_s = small(NBK)
        tile_end = small(TPP)
        first_d, first_s = small(NBK), small(NBK)
        base_s = small(NBK)
        bstep_d, bstep_s = small(SB), small(SB)
        boff_f = small(SB)
        boff_d, boff_s = small(SB, i32), small(SB, i32)
        tile_f, tile_i = small(SB), small(SB, i32)
        stats = small(LNG * 6)
        mv = small(LNG * 2)
        sd = small(LNG)
        rstd = [small(LNG) for _ in range(2)]
        nbias = [small(LNG) for _ in range(2)]
        mvn = small(BLOCKS * 2)
        sdn, rstdn, nbn = small(BLOCKS), small(BLOCKS), small(BLOCKS)
        fsum = small(TURNS)
        sq_part = small(SQ_PASSES)
        lastf = small(BLOCKS)
        lasti = [small(BLOCKS, i32) for _ in range(2)]
        possl = small(G, i32)
        paysl = small(G, i32)
        vcol = scol[:, 0:1]
        one_eps, brz = scol[:, 1:2], scol[:, 2:4]
        negmu, sq, bsd, brs, scale_c, shift_c, msum = (scol[:, k:k + 1] for k in range(4, 11))

        def bank(k):
            return ps[:, k, :]

        rank_ps = ps[:, 0, 0:NBK * G].rearrange("p (b q) -> p b q", q=G)

        block = ctx.enter_context(nc.Block())

        def rank_before(n_slot):
            o = blk1h[:, n_slot, :, :]
            nc.tensor.matmul(rank_ps, before_b[:, :], o, start=False, stop=True, skip_group_check=True)
            for q in range(G - 1):
                m = nc.tensor.matmul(rank_ps[:, :, q + 1:G], ones_b[:, :],
                                     o[:, :, q:q + 1].to_broadcast([P, NBK, G - 1 - q]),
                                     start=False, stop=True, skip_group_check=True)
            return m

        def rank_after(n_slot):
            o = blk1h[:, n_slot, :, :]
            nc.tensor.matmul(rank_ps, rest_b[:, :], o, start=False, stop=True, skip_group_check=True)
            for q in range(1, G):
                m = nc.tensor.matmul(rank_ps[:, :, 0:q], ones_b[:, :],
                                     o[:, :, q:q + 1].to_broadcast([P, NBK, q]),
                                     start=False, stop=True, skip_group_check=True)
            return m

        def norm_loop(engine, body):
            for k in range(HSLOTS):
                body(k, k)
            with engine.Fori(1, TURNS // HSLOTS) as j:
                for k in range(HSLOTS):
                    body(j * HSLOTS + k, k)
            for i in range(TURNS // HSLOTS * HSLOTS, TURNS):
                body(i, i % HSLOTS)

        def sum_loop(engine, body):
            with engine.Fori(0, BODIES) as j:
                for r in range(RSLOTS):
                    body(j * RSLOTS, j, r)
            for r in range(CHUNKS - BODIES * RSLOTS):
                body(BODIES * RSLOTS, BODIES, r)

        @block.sync
        def _(sp):
            sp.dma_start(cf[:, :], consts).then_inc(S("consts_in"), 16)
            sp.dma_start(raw_dst, edges[0]).then_inc(S("dst_in"), 16)
            sp.dma_start(nxt, dst_next).then_inc(S("dst_in"), 16)
            sp.dma_start(raw_src, edges[1]).then_inc(S("src_in"), 16)
            sp.dma_start(raw_typ, edges[2]).then_inc(S("type_in"), 16)
            xv = x.rearrange("(b p) f -> p b f", p=P)

            def load_x(i, k):
                sp.dma_start(xbuf[k].rearrange("p (b f) -> p b f", f=F), xv[:, ds(i * LNG, LNG), :]) \
                    .then_inc(S(f"x_in{k}"), 16)

            load_x(0, 0)
            load_x(1, 1)
            sp.dma_start(wT[:, :, :], weights.rearrange("p (a b) -> p a b", a=9)).then_inc(S("w_in"), 16)
            sp.dma_start(bcol[:, :], bias_cols).then_inc(S("w_in"), 16)
            sp.dma_start(embb[:, :, :].rearrange("p t f -> p (t f)"),
                         embed.rearrange("(a t) f -> a (t f)", a=1).to_broadcast([P, TYPES * F])).then_inc(S("w_in"), 16)
            sp.dma_start(bmsgb[:, :], b_msg.rearrange("(a f) -> a f", a=1).to_broadcast([P, F])).then_inc(S("w_in"), 16)
            sp.dma_start(b2b[:, :], b2.rearrange("(a f) -> a f", a=1).to_broadcast([P, F])).then_inc(S("w_in"), 16)
            sp.dma_start(one_eps, eps1.to_broadcast([P, 1])).then_inc(S("w_in"), 16)

            sp.wait_ge(S("flag_set"), 1)
            unsorted = sp.value_load(flag[0:1, 0:1], min_val=0, max_val=1)
            with sp.If(unsorted == 0):
                sp.wait_ge(S("packed"), 1)
                sp.dma_start(packed_d.rearrange("(p a) b -> p (a b)", p=P), packed).then_inc(S("packed_out"), 16)

            sp.wait_ge(S("step_tables"), 1)
            rv = blockrow_d.rearrange("a (s p) -> p a s", p=P)
            sp.dma_start(rv[:, 0, :], boff_d).then_inc(S("row_out_d"), 16)
            sp.wait_ge(S("row_out_d"), 16)
            sp.dma_start(steprow[:, :], blockrow_d[0:1, 0:STEPS_P]).then_inc(S("steprow_in"), 16)

            def table_out(j, k):
                tv = table_d.rearrange("(t b p) f -> b p t f", p=P, b=BLOCKS)
                for b in range(LNG):
                    slot = (k * LNG + b) % TSLOTS
                    sp.wait_ge(S("tab_ready"), (j * 2 + k) * LNG + b + 1)
                    sp.dma_start(tv[ds((j * 2 + k) * LNG + b, 1), :, :, :].rearrange("a p t f -> (a p) t f"),
                                 tabt[slot].rearrange("p (t f) -> p t f", f=F)).then_inc(S(f"tab_out{slot}"), 16)

            with sp.Fori(0, LN_TURNS // 2 - 1) as j:
                for k in range(2):
                    sp.wait_ge(S("h_ready"), j * 2 + k + 1)
                    load_x(j * 2 + 2 + k, k)
                    table_out(j, k)
            for k in range(2):
                table_out(LN_TURNS // 2 - 1, k)

            sp.wait_ge(S("loc_ready"), 1)
            sp.dma_start(loc_d.rearrange("(s p) e -> p s e", p=P),
                         fld[1].bitcast(bf16)[:, 0:SW].rearrange("p (s e) -> p s e", e=P)).then_inc(S("loc_out"), 16)

            sp.wait_ge(S("src_tables"), 1)
            sp.dma_start(rv[:, 1, :], boff_s).then_inc(S("row_out_s"), 16)

            pad_v = rows_d.rearrange("(c p k) w -> c k p w", p=P, k=CH)
            for t in (STEPS, STEPS + 1):
                sp.dma_start(pad_v[t // CH, t % CH], const("pad")).then_inc(S("pads_out"), 16)
            flat_v = rows_d.rearrange("(c p k) w -> c p (k w)", p=P, k=CH)
            wait(sp, "pads_out", 32)

            def pad_tiles(b):
                for a in range(2):
                    c = sp.value_load(lastrow[0:1, a, 0, ds(b, 1)], min_val=0, max_val=CHUNKS - 1)
                    q = sp.value_load(lastrow[0:1, a, 1, ds(b, 1)], min_val=0, max_val=CH - 1)
                    sp.dma_start(flat_v[ds(c, 1), :, ds(q * RW, RW)].rearrange("a p w -> (a p) w"), const("pad")) \
                        .then_inc(S("pads_out"), 16)
                    sp.wait_ge(S("pads_out"), (b * 2 + a) * 16 + 48)
                    plain(sp)

            with sp.Fori(0, BLOCKS) as b:
                pad_tiles(b)

            sp.wait_ge(S("agg_done"), GROUPS)

            def cell_in(i, k):
                sp.dma_start(cell_x[k].rearrange("p (b f) -> p b f", f=F), xv[:, ds(i * NG, NG), :]) \
                    .then_inc(S(f"cell_x{k}"), 16)

            def x1_out(i):
                x1v = x1_d.rearrange("(b p) f -> p b f", p=P)
                sp.wait_ge(S("x1_kept"), i + 1)
                sp.dma_start(x1v[:, ds(i * NG, NG), :], H[:, ds(i * GW, GW)].rearrange("p (b f) -> p b f", f=F)) \
                    .then_inc(S("x1_out"), 16)

            cell_in(0, 0)
            cell_in(1, 1)
            with sp.Fori(0, (TURNS - 3) // 2) as j:
                for k in range(2):
                    x1_out(j * 2 + k)
                    cell_in(j * 2 + k + 2, k)
            x1_out(TURNS - 3)
            cell_in(TURNS - 1, 0)
            x1_out(TURNS - 2)
            x1_out(TURNS - 1)
            sp.wait_ge(S("x1_out"), TURNS * 16)
            nc.sync.sem_inc(S("x1_stored"), 1)

            def loc_in(c, k):
                sp.dma_start(locb[k], loc_d.rearrange("(a s) e -> a (s e)", s=CH)[ds(c, 1), :].to_broadcast([P, CH * P])) \
                    .then_inc(S(f"locb_in{k}"), 16)

            sp.wait_ge(S("h2_done"), TURNS)
            sp.wait_ge(S("loc_out"), 16)
            loc_in(0, 0)
            loc_in(1, 1)
            with sp.Fori(1, PAIRS) as j:
                for k in range(2):
                    sp.wait_ge(S("pick_oh"), (j * 2 + k - 1) * GPC)
                    loc_in(j * 2 + k, k)

            sp.wait_ge(S("picked"), GROUPS)
            sp.wait_ge(S("row_out_s"), 16)
            sp.dma_start(steprow[:, :], blockrow_d[1:2, 0:STEPS_P]).then_inc(S("steprow_in"), 16)
            for k in range(2):
                sp.wait_ge(S(f"scattered{k}"), PAIRS * CH * 16)

            def rows_in(c, r):
                sp.dma_start(rrows[r].rearrange("p a w -> p (a w)"),
                             rows_d.rearrange("(c p k) w -> c p (k w)", p=P, k=CH)[ds(c, 1), :, :]
                             .rearrange("a p w -> (a p) w")).then_inc(S(f"rows_in{r}"), 16)

            for r in range(RSLOTS):
                rows_in(r, r)
            with sp.Fori(1, BODIES) as j:
                for r in range(RSLOTS):
                    sp.wait_ge(S("sum_done"), ((j - 1) * RSLOTS + r + 3) * GPC)
                    rows_in(j * RSLOTS + r, r)
            for r in range(CHUNKS - BODIES * RSLOTS):
                sp.wait_ge(S("sum_done"), ((BODIES - 1) * RSLOTS + r + 3) * GPC)
                rows_in(BODIES * RSLOTS + r, r)

            x1v = x1_d.rearrange("(b p) f -> p b f", p=P)
            ov = out.rearrange("(b p) f -> p b f", p=P)
            sp.wait_ge(S("sum_done"), GROUPS + 2 * GPC)
            for i in range(FIN):
                sp.dma_start(H[:, i * FINW:(i + 1) * FINW].rearrange("p (b f) -> p b f", f=F),
                             x1v[:, i * (BLOCKS // FIN):(i + 1) * (BLOCKS // FIN), :]).then_inc(S("fin_x"), 16)
            with sp.Fori(0, FIN) as i:
                sp.wait_ge(S("out_ready"), (i + 1) * (TURNS // FIN))
                sp.dma_start(ov[:, ds(i * (BLOCKS // FIN), BLOCKS // FIN), :],
                             H[:, ds(i * FINW, FINW)].rearrange("p (b f) -> p b f", f=F)).then_inc(S("out_done"), 16)
            sp.wait_ge(S("out_done"), FIN * 16)

        @block.gpsimd
        def _(pool):
            pool.wait_ge(S("flag_set"), 1)
            unsorted = pool.value_load(flag[0:1, 0:1], min_val=0, max_val=1)
            with pool.If(unsorted == 0):
                pool.wait_ge(S("packed_out"), 16)
            with pool.If(unsorted != 0):
                with pool.Fori(0, COLS // G) as n:
                    pool.wait_ge(S("sort_pos"), n + 1)
                    plain(pool)
                    for q in range(G):
                        pool.indirect_dma_start(
                            out=packed_d.rearrange("a (b c) -> (a b) c", c=1),
                            out_offset=bass.IndirectOffsetOnAxis(ap=possl[:, q:q + 1], axis=0),
                            in_=paysl[:, q:q + 1], in_offset=None).then_inc(S("sorted_out"), 16)
                    pool.wait_ge(S("sorted_out"), (n + 1) * (G * 16))
                    nc.gpsimd.sem_inc(S("sort_sent"), 1)
            pool.wait_ge(S("step_tables"), 1)
            for s in range(SB):
                pool.indirect_dma_start(out=fldi[0][:, s * P:(s + 1) * P], out_offset=None, in_=packed_d[:, :],
                                        in_offset=bass.IndirectOffsetOnAxis(ap=tile_i[:, s:s + 1], axis=0)) \
                    .then_inc(S("tiles_in"), 16)
            def keep_h(i, k):
                pool.wait_ge(S("hT_ready"), i + 1)
                nc.gpsimd.tensor_copy(H[:, ds(i * LNW, LNW)], hTs[k]).then_inc(S("hT_kept"), 1)

            with pool.Fori(0, LN_TURNS // 2) as j:
                for k in range(2):
                    keep_h(j * 2 + k, k)

            for r in range(TSLOTS):
                pool.wait_ge(S(f"tab_out{r}"), LN_TURNS // 2 * TUSES[r] * 16)

            def gather(j, k):
                wait(pool, "agg_done", (j * 2 + k - 1) * GPC)
                pool.wait_ge(S("idx_ready"), j * 2 + k + 1)
                plain(pool)
                for q in range(CH):
                    pool.indirect_dma_start(out=ring[:, k * CH + q, 0:F], out_offset=None, in_=table_d[:, :],
                                            in_offset=bass.IndirectOffsetOnAxis(ap=idxslot[:, k, q:q + 1], axis=0)) \
                        .then_inc(S(f"gathered{k}"), 16)

            for k in range(2):
                gather(0, k)
            with pool.Fori(1, PAIRS) as j:
                for k in range(2):
                    gather(j, k)

            def cell_n(i, k):
                pool.wait_ge(S("zhn_ready"), i + 1)
                nc.gpsimd.tensor_tensor(hnbuf[k], hnbuf[k], nbuf[k], ALU.add).then_inc(S("hn_ready"), 1)

            with pool.Fori(0, (TURNS - 1) // 2) as j:
                for k in range(2):
                    cell_n(j * 2 + k, k)
            cell_n(TURNS - 1, 0)

            def scatter(j, k):
                pool.wait_ge(S("keyed"), j * 2 + k + 1)
                for g in range(GPC):
                    pool.wait_ge(S("row_moved"), (j * 2 + k) * GPC + g + 1)
                    plain(pool)
                    for q in range(G):
                        s = g * G + q
                        pool.indirect_dma_start(
                            out=rows_d[:, :], out_offset=bass.IndirectOffsetOnAxis(ap=idxslot[:, k, s:s + 1], axis=0),
                            in_=ring[:, k * CH + s, :], in_offset=None,
                            bounds_check=ROWS_D - 1, oob_is_err=False).then_inc(S(f"scattered{k}"), 16)

            pool.wait_ge(S("pads_out"), (2 * BLOCKS + 2) * 16)
            with pool.Fori(0, PAIRS) as j:
                for k in range(2):
                    scatter(j, k)

            def key_onehots(c0, j, r):
                k = r % 2
                pool.wait_ge(S(f"rows_in{r}"), j * 16 + 16)
                pool.wait_ge(S("sum_done"), (c0 + r + 1) * GPC)
                plain(pool)
                for q in range(OH_V, OH_V + OH_P):
                    o = nc.gpsimd.tensor_scalar(oh[:, k, q, :], iota_f, rrows[r][:, q, KEY:KEY + 1], None, ALU.is_equal)
                o.then_inc(S("key_oh_p"), 1)

            sum_loop(pool, key_onehots)

        @block.scalar
        def _(act):
            def ramp(b):
                nc.scalar.activation(junk_a, sblk, ACT.Relu, bias=cf[:, ds(b + CF["blk"][0], 1)], scale=-1.0,
                                     accum_out=ramp_s[:, ds(b, 1)]).then_inc(S("ramp_s"), 1)

            def ramps(first, count):
                for b in range(count):
                    act.wait_ge(S("ramp_s"), first + b - 1)
                    ramp(first + b)

            def deviation(i):
                act.wait_ge(S("stats_ready"), i + 1)
                nc.scalar.activation(sd, mv.rearrange("p (b t) -> p b t", t=2)[:, :, 1], ACT.Sqrt,
                                     bias=const("lneps")).then_inc(S("sd_ready"), 1)

            def norm0(j, k, last=False):
                i = j * 2 + k
                act.wait_ge(S("rstd_ready"), i + 1)
                wait(act, "hT_ps", i - 1)
                for b in range(LNG):
                    o = nc.scalar.activation(hbuf[k][:, b * P:(b + 1) * P], xbuf[k][:, b * P:(b + 1) * P], ACT.Relu,
                                             bias=nbias[k][:, b:b + 1], scale=rstd[k][:, b:b + 1])
                o.then_inc(S("h_ready"), 1)
                if not last:
                    deviation(i + 1)
                ramps(EARLY + i * PER_TURN + 1, 3)
                act.wait_ge(S("hT_ps"), i + 1)
                wait(act, "hT_kept", i - 1)
                wait(act, "m_ready", i - 1)
                nc.scalar.copy(hTs[k][:, 0:512], bank(2 * k))
                nc.scalar.copy(hTs[k][:, 512:LNW], bank(2 * k + 1)[:, 0:LNW - 512]).then_inc(S("hT_ready"), 1)
                ramps(EARLY + i * PER_TURN + 4, PER_TURN - 3)

            act.wait_ge(S("src_blocks"), 1)
            ramp(1)
            ramps(2, EARLY - 1)
            deviation(0)
            for k in range(2):
                norm0(0, k)
            with act.Fori(1, LN_TURNS // 2 - 1) as j:
                for k in range(2):
                    norm0(j, k)
            norm0(LN_TURNS // 2 - 1, 0)
            norm0(LN_TURNS // 2 - 1, 1, last=True)

            for f, dst_t in enumerate((tabE, locE, None)):
                for a in range(4):
                    w = min(512, SW - a * 512)
                    act.wait_ge(S("fields_T"), f * 4 + a + 1)
                    o = dst_t[:, a * 512:a * 512 + w] if dst_t is not None else fldi[2][:, a * 512:a * 512 + w]
                    nc.scalar.copy(o, bank((f % 2) * 4 + a)[:, 0:w]).then_inc(S("fields_moved"), 1)

            act.wait_ge(S("fields_read"), 1)
            act.wait_ge(S("loc_out"), 16)
            yw = Y.shape[1]
            nc.scalar.copy(Y[:, 0:yw // 512 * 512].rearrange("p (a b) -> p a b", b=512),
                           zeros_b[:, :].unsqueeze(1).to_broadcast([P, yw // 512, 512]))
            nc.scalar.copy(Y[:, yw // 512 * 512:yw], zeros_b[:, 0:yw % 512]).then_inc(S("y_zero"), 1)

            def gates(i, k):
                act.wait_ge(S("gates_ps"), i + 1)
                nc.scalar.activation(rbuf[k], bank(2 * k)[:, 0:GW], ACT.Sigmoid, bias=brz[:, 0:1])
                wait(act, "zhn_ready", i - 1)
                nc.scalar.activation(zbuf[k], bank(2 * k)[:, GW:2 * GW], ACT.Sigmoid, bias=brz[:, 1:2]).then_inc(S("gates_rz"), 1)

            def candidate(i, k):
                act.wait_ge(S("cand_in"), i + 1)
                wait(act, "hn_ready", i - 1)
                nc.scalar.activation(nbuf[k], tbuf[k], ACT.Tanh, bias=bcol[:, 2:3]).then_inc(S("cand"), 1)

            act.wait_ge(S("agg_added"), GROUPS)
            act.wait_ge(S("brz_set"), 1)
            gates(0, 0)
            gates(1, 1)
            candidate(0, 0)
            with act.Fori(0, (TURNS - 3) // 2) as j:
                for k in range(2):
                    gates(j * 2 + k + 2, k)
                    candidate(j * 2 + k + 1, 1 - k)
            gates(TURNS - 1, 0)
            candidate(TURNS - 2, 1)
            candidate(TURNS - 1, 0)

            act.wait_ge(S("x1_stats"), TURNS)
            nc.scalar.activation(sdn, mvn.rearrange("p (b t) -> p b t", t=2)[:, :, 1], ACT.Sqrt,
                                 bias=const("lneps")).then_inc(S("sdn_ready"), 1)
            act.wait_ge(S("rstdn_ready"), 1)
            act.wait_ge(S("x1_stored"), 1)

            def norm1(i, k):
                wait(act, "h2_kept", i - HSLOTS + 1)
                wait(act, "h2_ps", i - HSLOTS + 1)
                for b in range(NG):
                    o = nc.scalar.activation(hs[k][:, b * P:(b + 1) * P], H[:, ds(i * GW + b * P, P)], ACT.Relu,
                                             bias=nbn[:, ds(i * NG + b, 1)], scale=rstdn[:, ds(i * NG + b, 1)])
                o.then_inc(S("h2_ready"), 1)

            norm_loop(act, norm1)

            def move_rows(j, k):
                wait(act, f"scattered{k}", j * (CH * 16))
                for g in range(GPC):
                    act.wait_ge(S("picked"), (j * 2 + k) * GPC + g + 1)
                    nc.scalar.copy(ring[:, k * CH + g * G:k * CH + (g + 1) * G, 0:F],
                                   bank(g).rearrange("p (q f) -> p q f", f=F)).then_inc(S("row_moved"), 1)

            act.wait_ge(S("ring_cleared"), 1)
            for k in range(2):
                move_rows(0, k)
            with act.Fori(1, PAIRS) as j:
                for k in range(2):
                    move_rows(j, k)

            def key_onehots(c0, j, r):
                k = r % 2
                act.wait_ge(S(f"rows_in{r}"), j * 16 + 16)
                act.wait_ge(S("sum_done"), (c0 + r + 1) * GPC)
                for q in range(OH_V + OH_P, CH):
                    o = nc.scalar.activation(oh[:, k, q, :], iota_f, ACT.Abs, bias=rrows[r][:, q, KEY:KEY + 1], scale=-1.0)
                o.then_inc(S("key_dist"), 1)
                act.wait_ge(S("key_dist"), c0 + r + 1)
                nc.scalar.activation(oh[:, k, OH_V + OH_P:CH, :], oh[:, k, OH_V + OH_P:CH, :], ACT.Relu,
                                     bias=ones_f[:, 0:1], scale=-1.0).then_inc(S("key_oh_a"), 1)
                for g in range(GPC):
                    act.wait_ge(S("bank_free"), (c0 + r) * GPC + g + 1)
                    nc.scalar.copy(bank(r % 2 * GPC + g), zeros_b[:, :]).then_inc(S("bank_zero"), 1)

            sum_loop(act, key_onehots)

            def lin1(i, k, w):
                act.wait_ge(S("lin1_ps"), i + 1)
                nc.scalar.activation(Y[:, ds(i * GW, w)], bank(4 + k)[:, 0:w], ACT.Identity, bias=bcol[:, 6:7],
                                     accum_out=fsum[:, ds(i, 1)]).then_inc(S("lin1"), 1)

            with act.Fori(0, (TURNS - 1) // 2) as j:
                for k in range(2):
                    lin1(j * 2 + k, k, GW)
            lin1(TURNS - 1, 0, N - (TURNS - 1) * GW)
            act.wait_ge(S("negmu_ready"), 1)
            for a in range(SQ_PASSES):
                wait(act, "sq_ready", a)
                nc.scalar.activation(ohf[:, 0:SQW], Y[:, a * SQW:(a + 1) * SQW], ACT.Square, bias=negmu,
                                     accum_out=sq_part[:, a:a + 1]).then_inc(S("sq_ready"), 1)
            act.wait_ge(S("sq_scaled"), 1)
            nc.scalar.activation(bsd, sq, ACT.Sqrt, bias=const("bneps"), scale=1.0 / N).then_inc(S("bsd_ready"), 1)
            act.wait_ge(S("bn_ready"), 1)

            def bn_relu(i, k):
                wait(act, "lin2_ps", i - 1)
                nc.scalar.activation(fin_z[k], Y[:, ds(i * GW, GW)], ACT.Relu, bias=shift_c, scale=scale_c) \
                    .then_inc(S("z_ready"), 1)

            bn_relu(0, 0)
            bn_relu(1, 1)
            with act.Fori(0, (TURNS - 3) // 2) as j:
                for k in range(2):
                    bn_relu(j * 2 + k + 2, k)
            bn_relu(TURNS - 1, 0)

        @block.vector
        def _(dve):
            vs = nc.vector
            seq = [0]

            def link(ins):
                seq[0] += 1
                ins.then_inc(S("dve_seq"), 1)
                dve.wait_ge(S("dve_seq"), seq[0])

            dve.wait_ge(S("consts_in"), 16)
            vs.tensor_copy(ones_b[:, :], ones_f)
            vs.tensor_copy(before_b[:, :], const("before"))
            link(vs.tensor_copy(blk4_b[:, :, :], const("blk4").rearrange("p (b q) -> p b q", q=G)))
            vs.tensor_tensor(rest_b[:, :], ones_b[:, :], before_b[:, :], ALU.subtract)
            vs.memset(zeros_b[:, :], 0.0)

            dve.wait_ge(S("dst_in"), 32)
            link(vs.tensor_tensor(viol, raw_dst, nxt, ALU.is_gt))
            vs.tensor_reduce(vcol, viol, axis=AX.X, op=ALU.add).then_inc(S("viol_summed"), 1)
            dve.wait_ge(S("src_in"), 16)
            link(vs.tensor_scalar(packed, raw_src, 7, None, ALU.logical_shift_right))
            vs.tensor_copy(sblk, packed).then_inc(S("src_blocks"), 1)
            dve.wait_ge(S("src_blocks"), 1)
            dve.wait_ge(S("type_in"), 16)
            vs.tensor_scalar(packed, raw_src, 18, None, ALU.logical_shift_left)
            link(vs.tensor_scalar(nxt, raw_dst, 4, None, ALU.logical_shift_left))
            link(vs.tensor_tensor(packed, packed, nxt, ALU.bitwise_or))
            link(vs.tensor_scalar(raw_typ, raw_typ, 0.0, float(TYPES - 1), ALU.max, ALU.min))
            vs.tensor_tensor(packed, packed, raw_typ, ALU.bitwise_or).then_inc(S("packed"), 1)
            dve.wait_ge(S("viol_ps"), 1)
            link(vs.tensor_scalar(lo_i[0:1, 0:1], bank(7)[0:1, 0:1], 0.0, None, ALU.is_gt))
            vs.tensor_copy(flag[:, :], lo_i[0:1, 0:1]).then_inc(S("flag_set"), 1)

            link(vs.tensor_copy(tile_end, raw_dst[:, P - 1:COLS:P]))
            dve.wait_ge(S("viol_summed"), 1)
            link(vs.tensor_tensor(tile_lt, tile_end.unsqueeze(1).to_broadcast([P, NBK, TPP]),
                                  const("node").unsqueeze(2).to_broadcast([P, NBK, TPP]), ALU.is_lt))
            vs.tensor_reduce(part_d, tile_lt, axis=AX.X, op=ALU.add).then_inc(S("tiles_counted"), 1)
            dve.wait_ge(S("tiles_ps"), 1)
            link(vs.tensor_tensor(first_d, bank(6)[:, 0:NBK], const("blk"), ALU.add))

            unsorted = dve.value_load(flag[0:1, 0:1], min_val=0, max_val=1)
            with dve.If(unsorted != 0):
                vs.tensor_scalar(raw_dst, raw_dst, 7, None, ALU.logical_shift_right).then_inc(S("dst_blocks"), 1)
                dve.wait_ge(S("dst_blocks"), 1)
                vs.tensor_copy(dblk, raw_dst).then_inc(S("dst_blocks"), 1)
                dve.wait_ge(S("dst_blocks"), 2)
                with dve.Fori(0, NBK) as b:
                    vs.tensor_scalar(junk_v, dblk, cf[:, ds(b + CF["thr"][0], 1)], 0.0, ALU.is_lt, ALU.add,
                                     accum_out=part_d[:, ds(b, 1)]).then_inc(S("hist_d"), 1)
                    dve.wait_ge(S("hist_d"), b + 1)
                dve.wait_ge(S("starts_ps"), 1)
                vs.tensor_copy(start_d, bank(6)[:, 0:NBK])
                vs.tensor_copy(lo_i, bank(6)[:, 0:NBK]).then_inc(S("starts_d"), 1)
                dve.wait_ge(S("starts_d"), 1)
                vs.tensor_scalar(lo_i, lo_i, 7, None, ALU.logical_shift_right).then_inc(S("starts_d"), 1)
                dve.wait_ge(S("starts_d"), 2)
                vs.tensor_tensor(first_d, lo_i, const("blk"), ALU.add).then_inc(S("starts_d"), 1)
                dve.wait_ge(S("starts_d"), 3)
                with dve.Fori(0, COLS // G) as n:
                    vs.tensor_tensor(blk1h[:, 0, :, :], dblk[:, ds(n * G, G)].unsqueeze(1).to_broadcast([P, NBK, G]),
                                     blk4_b[:, :, :], ALU.is_equal).then_inc(S("sort_oh"), 1)
                    dve.wait_ge(S("sort_ps"), n + 1)
                    vs.tensor_tensor(ranked[:, 0, :, :], rank_ps, blk1h[:, 0, :, :], ALU.mult).then_inc(S("sort_mul"), 1)
                    dve.wait_ge(S("sort_mul"), n + 1)
                    vs.tensor_reduce(possl, ranked[:, 0, :, :].rearrange("p b q -> p q b"), axis=AX.X, op=ALU.add)
                    vs.tensor_copy(paysl, packed[:, ds(n * G, G)]).then_inc(S("sort_pos"), 1)
                    dve.wait_ge(S("sort_sent"), n + 1)
                    dve.wait_ge(S("sort_after"), n + 1)

            def step_blocks(first, bstep, tmp):
                link(vs.tensor_tensor(tmp, const("step").unsqueeze(2).to_broadcast([P, SB, BLOCKS - 1]),
                                      first[:, 1:BLOCKS].unsqueeze(1).to_broadcast([P, SB, BLOCKS - 1]), ALU.is_ge))
                link(vs.tensor_reduce(bstep, tmp, axis=AX.X, op=ALU.add))

            step_blocks(first_d, bstep_d, blktmp)
            vs.tensor_scalar(boff_d, bstep_d, float(P), None, ALU.mult)
            vs.tensor_scalar(boff_f, bstep_d, float(P), None, ALU.mult)
            link(vs.tensor_tensor(tile_f, const("step"), bstep_d, ALU.subtract))
            vs.tensor_scalar(tile_i, tile_f, float(TILES - 1), None, ALU.min).then_inc(S("step_tables"), 1)
            vs.memset(ramp_s[:, 0:1], 0.0)

            dve.wait_ge(S("w_in"), 96)
            vs.tensor_tensor(embb[:, :, :], embb[:, :, :], bmsgb[:, :].unsqueeze(1).to_broadcast([P, TYPES, P]), ALU.add)
            vs.tensor_scalar(one_eps, one_eps, 1.0, None, ALU.add)
            link(vs.tensor_tensor(brz, bcol[:, 0:2], bcol[:, 3:5], ALU.add))
            vs.tensor_copy(lastf[:, 2:3], brz[:, 0:1]).then_inc(S("brz_set"), 1)

            mvv = mv.rearrange("p (b t) -> p b t", t=2)

            def norm_stats(j, k):
                i = j * 2 + k
                dve.wait_ge(S(f"x_in{k}"), j * 16 + 16)
                wait(dve, "sd_ready", i)
                plain(dve)
                for b in range(LNG):
                    o = vs.bn_stats(stats[:, b * 6:(b + 1) * 6], xbuf[k][:, b * P:(b + 1) * P])
                o.then_inc(S("bn1"), 1)
                dve.wait_ge(S("bn1"), i + 1)
                plain(dve)
                for b in range(LNG):
                    o = vs.bn_aggr(mv[:, 2 * b:2 * b + 2], stats[:, b * 6:(b + 1) * 6])
                o.then_inc(S("stats_ready"), 1)

            def norm_scale(j, k):
                i = j * 2 + k
                dve.wait_ge(S("sd_ready"), i + 1)
                wait(dve, "h_ready", i - 1)
                vs.reciprocal(rstd[k], sd).then_inc(S("rcp"), 1)
                dve.wait_ge(S("rcp"), i + 1)
                vs.scalar_tensor_tensor(out=nbias[k], in0=mvv[:, :, 0], scalar=-1.0, in1=rstd[k],
                                        op0=ALU.mult, op1=ALU.mult).then_inc(S("rstd_ready"), 1)

            def table_rows(j, k):
                i = j * 2 + k
                dve.wait_ge(S("m_ready"), i + 1)
                for b in range(LNG):
                    n = k * LNG + b
                    slot = n % TSLOTS
                    wait(dve, f"tab_out{slot}", j * (TUSES[slot] * 16) + n // TSLOTS * 16)
                    m = bank(4 + 2 * k + b // 4)[:, b % 4 * P:(b % 4 + 1) * P]
                    vs.tensor_tensor(tabt[slot].rearrange("p (t f) -> p t f", f=F),
                                     m.unsqueeze(1).to_broadcast([P, TYPES, P]), embb[:, :, :], ALU.add) \
                        .then_inc(S("tab_ready"), 1)

            norm_stats(0, 0)
            norm_scale(0, 0)
            norm_stats(0, 1)
            def count_src(i):
                wait(dve, "hist_s", i)
                vs.tensor_scalar(junk_v, sblk, cf[:, ds(i + CF["thr"][0] + RAMPS + 1, 1)], 0.0, ALU.is_lt, ALU.add,
                                 accum_out=part_s[:, ds(i + RAMPS + 1, 1)]).then_inc(S("hist_s"), 1)

            with dve.Fori(1, LN_TURNS // 2) as j:
                norm_scale(j - 1, 1)
                norm_stats(j, 0)
                table_rows(j - 1, 0)
                count_src((j - 1) * 2)
                norm_scale(j, 0)
                norm_stats(j, 1)
                table_rows(j - 1, 1)
                count_src((j - 1) * 2 + 1)
            for i in range(LN_TURNS - 2, BLOCKS - RAMPS):
                count_src(i)
            norm_scale(LN_TURNS // 2 - 1, 1)
            table_rows(LN_TURNS // 2 - 1, 0)

            dve.wait_ge(S("tiles_in"), SB * 16)
            LOC, TAB, SRC, VAL = fld[4], fld[3], fld[6], fld[5]
            v3 = lambda a: a.rearrange("p (s e) -> p s e", e=P)
            vs.tensor_scalar(fldi[1], fldi[0], 15, None, ALU.bitwise_and)
            link(vs.tensor_scalar(fldi[2], fldi[0], 18, None, ALU.logical_shift_right))
            vs.scalar_tensor_tensor(out=TAB, in0=fldi[1], scalar=float(NPAD), in1=fldi[2], op0=ALU.mult, op1=ALU.add) \
                .then_inc(S("field"), 1)
            dve.wait_ge(S("field"), 1)
            table_rows(LN_TURNS // 2 - 1, 1)
            dve.wait_ge(S("ramp_s"), RAMPS)
            dve.wait_ge(S("hist_s"), BLOCKS - RAMPS)
            vs.memset(part_s[:, 0:1], 0.0)
            vs.tensor_tensor(part_s[:, 1:RAMPS + 1], ramp_s[:, 1:RAMPS + 1], ramp_s[:, 0:RAMPS], ALU.subtract) \
                .then_inc(S("src_counted"), 1)

            def place_idx(c, k):
                vs.tensor_copy(idxslot[:, k, :], tabE[:, ds(c * CH, CH)]).then_inc(S("idx_ready"), 1)

            dve.wait_ge(S("fields_moved"), 4)
            place_idx(0, 0)
            place_idx(1, 1)
            link(vs.tensor_scalar(fldi[1], fldi[0], 4, 16383, ALU.logical_shift_right, ALU.bitwise_and))
            link(vs.tensor_tensor(v3(LOC), v3(fldi[1]), boff_f.unsqueeze(2).to_broadcast([P, SB, P]), ALU.subtract))
            link(vs.tensor_scalar(VAL, LOC, 0.0, None, ALU.is_ge))
            link(vs.scalar_tensor_tensor(out=VAL, in0=LOC, scalar=float(P), in1=VAL, op0=ALU.is_lt, op1=ALU.mult))
            link(vs.scalar_tensor_tensor(out=LOC, in0=LOC, scalar=-FAR, in1=VAL, op0=ALU.add, op1=ALU.mult))
            link(vs.tensor_scalar(LOC, LOC, FAR, None, ALU.add))
            vs.tensor_copy(lastf[:, 3:4], LOC[:, 0:1]).then_inc(S("field"), 1)
            link(vs.scalar_tensor_tensor(out=SRC, in0=fldi[2], scalar=-16383.0, in1=VAL, op0=ALU.add, op1=ALU.mult))
            link(vs.tensor_scalar(SRC, SRC, 16383.0, None, ALU.add))
            vs.tensor_copy(lastf[:, 4:5], SRC[:, 0:1]).then_inc(S("field"), 1)
            vs.tensor_copy(fld[1].bitcast(bf16)[:, 0:SW], LOC).then_inc(S("loc_ready"), 1)

            dve.wait_ge(S("starts_ps_s"), 1)
            dve.wait_ge(S("fields_moved"), 8)
            link(vs.tensor_copy(lo_i, bank(7)[:, 256:256 + NBK]))
            link(vs.tensor_scalar(lo_i, lo_i, 7, None, ALU.logical_shift_right))
            link(vs.tensor_tensor(first_s, lo_i, const("blk"), ALU.add))
            vs.tensor_scalar(base_s, first_s, float(P), None, ALU.mult).then_inc(S("base_s"), 1)
            link(vs.tensor_scalar(lasti[0][0:1, :], first_s[0:1, 1:NBK], -1.0, None, ALU.add))
            link(vs.tensor_scalar(lasti[1][0:1, :], first_s[0:1, 1:NBK], -2.0, 0.0, ALU.add, ALU.max))
            for a in range(2):
                vs.tensor_scalar(lastrow[0:1, a, 0, :], lasti[a][0:1, :], 4, None, ALU.logical_shift_right)
                link(vs.tensor_scalar(lastrow[0:1, a, 1, :], lasti[a][0:1, :], CH - 1, None, ALU.bitwise_and))
            dve.wait_ge(S("fields_moved"), 12)
            step_blocks(first_s, bstep_s, blktmp)
            vs.tensor_scalar(boff_s, bstep_s, float(P), None, ALU.mult).then_inc(S("src_tables"), 1)
            link(vs.tensor_scalar(fldi[3], fldi[2], 7, None, ALU.logical_shift_right))
            vs.tensor_copy(sblkE[:, :], fldi[3])
            link(vs.tensor_scalar(fldi[4], fldi[2], P - 1, None, ALU.bitwise_and))
            for r in range(TSLOTS):
                dve.wait_ge(S(f"tab_out{r}"), LN_TURNS // 2 * TUSES[r] * 16)
            link(vs.tensor_copy(skeyE[:, :], fldi[4]))
            nc.vector.sem_inc(S("fields_read"), 1)

            def step_onehots(c, k):
                wait(dve, "agg_done", (c - 1) * GPC)
                vs.tensor_tensor(oh[:, k, :, :], locE[:, ds(c * CH, CH)].unsqueeze(2).to_broadcast([P, CH, P]),
                                 iota_f.unsqueeze(1).to_broadcast([P, CH, P]), ALU.is_equal).then_inc(S("oh_ready"), 1)

            def block_onehots(n, slot):
                wait(dve, "rank_counted", n - 3)
                vs.tensor_tensor(blk1h[:, slot, :, :], sblkE[:, ds(n * G, G)].unsqueeze(1).to_broadcast([P, NBK, G]),
                                 blk4_b[:, :, :], ALU.is_equal).then_inc(S("blk_ready"), 1)

            regs = [dve.alloc_register(f"group_off{q}") for q in range(GPC)]

            def group_offsets(c):
                vs.load(regs, steprow[0:1, ds(c * CH, CH)].rearrange("p (g q) -> p g q", q=G)[:, :, 0])
                return [dve.snap(r, min_val=0, max_val=(BLOCKS - 1) * P) for r in regs]

            def layer0(j, k):
                c = j * 2 + k
                offs = group_offsets(c)
                for g in range(GPC):
                    n = c * GPC + g
                    dve.wait_ge(S("rank_ps"), n + 1)
                    vs.tensor_tensor(ranked[:, g % 2, :, :], rank_ps, blk1h[:, g, :, :], ALU.mult).then_inc(S("rank_read"), 1)
                    block_onehots(n + 1, (g + 1) % G)
                    dve.wait_ge(S("rank_read"), n + 1)
                    vs.tensor_reduce(posE[:, ds(n * G, G)], ranked[:, g % 2, :, :].rearrange("p b q -> p q b"),
                                     axis=AX.X, op=ALU.add)
                    if g == 1:
                        dve.wait_ge(S(f"gathered{k}"), j * (CH * 16) + CH * 16)
                        place_idx(c + 2, k)
                    if g == 2:
                        step_onehots(c + 1, 1 - k)
                    dve.wait_ge(S("agg_done"), n + 1)
                    wait(dve, "agg_added", n)
                    yb = Y[:, ds(offs[g], 512)]
                    vs.tensor_tensor(yb, yb, bank(1 + g), ALU.add).then_inc(S("agg_added"), 1)

            dve.wait_ge(S("steprow_in"), 16)
            dve.wait_ge(S("hT_kept"), LN_TURNS)
            step_onehots(0, 0)
            block_onehots(0, 0)
            dve.wait_ge(S("y_zero"), 1)
            for k in range(2):
                layer0(0, k)
            with dve.Fori(1, PAIRS) as j:
                for k in range(2):
                    layer0(j, k)

            ta, tb = ringf[:, 0:STEPS_P].bitcast(i32), ringf[:, STEPS_P:2 * STEPS_P].bitcast(i32)
            dve.wait_ge(S("agg_added"), GROUPS)
            pe_, ta_, tb_ = posE[:, :], ta, tb
            vs.tensor_scalar(ta_, pe_, 127, 4, ALU.bitwise_and, ALU.logical_shift_left)
            link(vs.tensor_scalar(tb_, pe_, 7, CH - 1, ALU.logical_shift_right, ALU.bitwise_and))
            link(vs.tensor_tensor(ta_, ta_, tb_, ALU.bitwise_or))
            link(vs.tensor_scalar(tb_, pe_, 11, 11, ALU.logical_shift_right, ALU.logical_shift_left))
            link(vs.tensor_tensor(ta_, ta_, tb_, ALU.bitwise_or))
            link(vs.tensor_scalar(tb_, sblkE[:, 0:STEPS_P], float(BLOCKS), float(SKIP), ALU.is_ge, ALU.mult))
            link(vs.tensor_tensor(pe_, ta_, tb_, ALU.max))
            link(vs.memset(ringf, 0.0))
            vs.tensor_copy(lastf[:, 5:6], ringf[:, 0:1]).then_inc(S("ring_cleared"), 1)

            def cell_turn(i, k, j=None):
                first, last = (i, i) if isinstance(i, int) else (4, TURNS - 1)
                o = 1 - k
                gate, blend, add = last < TURNS, first >= 1 and last - 1 < TURNS, first >= 2 and last - 2 < TURNS
                var, keep = first >= 3 and last - 3 < TURNS, first >= 4
                if keep:
                    dve.wait_ge(S("bn3"), i - 3)
                    vs.tensor_copy(mvn[:, ds((i - 4) * (2 * NG), 2 * NG)], mv[:, 0:2 * NG]).then_inc(S("x1_stats"), 1)
                if gate:
                    dve.wait_ge(S("gates_rz"), i + 1)
                    wait(dve, "cand", i - 1)
                    vs.scalar_tensor_tensor(out=tbuf[k], in0=bank(2 * k + 1)[:, GW:2 * GW], scalar=bcol[:, 5:6],
                                            in1=rbuf[k], op0=ALU.add, op1=ALU.mult).then_inc(S("cell_t"), 1)
                if blend:
                    dve.wait_ge(S("cand"), i)
                    wait(dve, "hn_ps", i - 2)
                    vs.tensor_tensor(hnbuf[o], H[:, ds((i - 1) * GW, GW)], nbuf[o], ALU.subtract).then_inc(S("cell_h"), 1)
                if gate:
                    dve.wait_ge(S("cell_t"), i + 1)
                    vs.tensor_tensor(tbuf[k], tbuf[k], bank(2 * k + 1)[:, 0:GW], ALU.add).then_inc(S("cand_in"), 1)
                if blend:
                    dve.wait_ge(S("cell_h"), i)
                    vs.tensor_tensor(hnbuf[o], hnbuf[o], zbuf[o], ALU.mult).then_inc(S("zhn_ready"), 1)
                if var:
                    dve.wait_ge(S("x1_kept"), i - 2)
                    plain(dve)
                    for b in range(NG):
                        m = vs.bn_stats(stats[:, b * 6:(b + 1) * 6], H[:, ds((i - 3) * GW + b * P, P)])
                    m.then_inc(S("bn2"), 1)
                if add:
                    dve.wait_ge(S("hn_ps"), i - 1)
                    dve.wait_ge(S(f"cell_x{k}"), j * 16)
                    vs.tensor_tensor(H[:, ds((i - 2) * GW, GW)], cell_x[k], bank(4 + k)[:, 0:GW], ALU.add) \
                        .then_inc(S("x1_kept"), 1)
                if var:
                    dve.wait_ge(S("bn2"), i - 2)
                    dve.wait_ge(S("x1_stats"), i - 3) if keep else None
                    plain(dve)
                    for b in range(NG):
                        m = vs.bn_aggr(mv[:, 2 * b:2 * b + 2], stats[:, b * 6:(b + 1) * 6])
                    m.then_inc(S("bn3"), 1)

            for i in range(5):
                cell_turn(i, i % 2, i // 2)
            with dve.Fori(2, (TURNS - 1) // 2) as j:
                for k in range(2):
                    cell_turn(j * 2 + 1 + k, 1 - k, j + k)
            for i in range(TURNS, TURNS + 4):
                cell_turn(i, i % 2, i // 2)

            dve.wait_ge(S("sdn_ready"), 1)
            link(vs.reciprocal(rstdn, sdn))
            vs.scalar_tensor_tensor(out=nbn, in0=mvn.rearrange("p (b t) -> p b t", t=2)[:, :, 0], scalar=-1.0, in1=rstdn,
                                    op0=ALU.mult, op1=ALU.mult).then_inc(S("rstdn_ready"), 1)

            def h2_own(i, k):
                dve.wait_ge(S("h2_ready"), i + 1)
                vs.tensor_copy(H[:, ds(i * GW, GW)], hs[k]).then_inc(S("h2_kept"), 1)
                dve.wait_ge(S("h2_ps"), i + 1)
                vs.tensor_scalar(Y[:, ds(i * GW, GW)], bank(k)[:, 0:GW], one_eps, None, ALU.mult).then_inc(S("h2_done"), 1)

            norm_loop(dve, h2_own)

            dve.wait_ge(S("h2_kept"), TURNS)
            def layer1_pick(j, k):
                c = j * 2 + k
                wait(dve, f"scattered{k}", j * (CH * 16))
                vs.tensor_copy(ring[:, k * CH:(k + 1) * CH, KEY:KEY + 1],
                               skeyE[:, ds(c * CH, CH)].unsqueeze(2))
                vs.tensor_copy(idxslot[:, k, :], posE[:, ds(c * CH, CH)]).then_inc(S("keyed"), 1)
                dve.wait_ge(S(f"locb_in{k}"), j * 16 + 16)
                for g in range(GPC):
                    wait(dve, "picked", c * GPC + g - 3)
                    vs.tensor_scalar(pick[g], locb[k][:, g * 512:(g + 1) * 512], iota_p, None, ALU.is_equal) \
                        .then_inc(S("pick_oh"), 1)

            for k in range(2):
                layer1_pick(0, k)
            with dve.Fori(1, PAIRS) as j:
                for k in range(2):
                    layer1_pick(j, k)

            def key_onehots(c0, j, r, piece):
                k = r % 2
                dve.wait_ge(S(f"rows_in{r}"), j * 16 + 16)
                dve.wait_ge(S("sum_done"), (c0 + r + 1) * GPC)
                a, b = (piece * 2 + 1 if piece else 0), piece * 2 + 3
                vs.tensor_tensor(oh[:, k, a:b, :], rrows[r][:, a:b, KEY:KEY + 1].to_broadcast([P, b - a, P]),
                                 iota_f.unsqueeze(1).to_broadcast([P, b - a, P]), ALU.is_equal).then_inc(S("key_oh_v"), 1)

            def layer1_sum(c0, j, r):
                offs = group_offsets(c0 + r)
                for g in range(GPC):
                    n = (c0 + r) * GPC + g
                    if g < V_PIECES and not (isinstance(c0, int) and c0 + r == CHUNKS - 1):
                        if r < RSLOTS - 1:
                            key_onehots(c0, j, r + 1, g)
                        else:
                            key_onehots(c0 + RSLOTS, j + 1, 0, g)
                    dve.wait_ge(S("sum_done"), n + 1 + 2 * GPC)
                    dve.wait_ge(S("bank_free"), n + 2 * GPC)
                    yb = Y[:, ds(offs[g], 512)]
                    vs.tensor_tensor(yb, yb, bank(r % 2 * GPC + g), ALU.add).then_inc(S("bank_free"), 1)

            dve.wait_ge(S("steprow_in"), 32)
            dve.wait_ge(S("picked"), GROUPS)
            nc.vector.sem_inc(S("bank_free"), 2 * GPC)
            for piece in range(V_PIECES):
                key_onehots(0, 0, 0, piece)
            sum_loop(dve, layer1_sum)

            dve.wait_ge(S("lin1"), TURNS)
            link(vs.tensor_reduce(msum, fsum, axis=AX.X, op=ALU.add))
            vs.tensor_scalar(negmu, msum, -1.0 / N, None, ALU.mult).then_inc(S("negmu_ready"), 1)
            dve.wait_ge(S("fin_x"), FIN * 16)
            vs.tensor_tensor(H[:, :].rearrange("p (b f) -> p b f", f=F), H[:, :].rearrange("p (b f) -> p b f", f=F),
                             b2b[:, :].unsqueeze(1).to_broadcast([P, BLOCKS, F]), ALU.add).then_inc(S("b2_added"), 1)
            dve.wait_ge(S("sq_ready"), SQ_PASSES)
            vs.tensor_reduce(sq, sq_part, axis=AX.X, op=ALU.add).then_inc(S("sq_scaled"), 1)
            dve.wait_ge(S("bsd_ready"), 1)
            link(vs.reciprocal(brs, bsd))
            link(vs.tensor_tensor(scale_c, brs, bcol[:, 7:8], ALU.mult))
            vs.scalar_tensor_tensor(out=shift_c, in0=negmu, scalar=scale_c, in1=bcol[:, 8:9],
                                    op0=ALU.mult, op1=ALU.add).then_inc(S("bn_ready"), 1)

            def final(i, k):
                dve.wait_ge(S("lin2_ps"), i + 1)
                o = H[:, ds(i * GW, GW)]
                vs.tensor_tensor(o, o, bank(k)[:, 0:GW], ALU.add).then_inc(S("out_ready"), 1)

            dve.wait_ge(S("b2_added"), 1)
            with dve.Fori(0, (TURNS - 1) // 2) as j:
                for k in range(2):
                    final(j * 2 + k, k)
            final(TURNS - 1, 0)

        @block.tensor
        def _(pe):
            mm = nc.tensor.matmul
            pe.wait_ge(S("viol_summed"), 1)
            mm(bank(7)[:, 0:1], ones_f, vcol, start=True, stop=True).then_inc(S("viol_ps"), 1)
            pe.wait_ge(S("tiles_counted"), 1)
            mm(bank(6)[:, 0:NBK], ones_f, part_d, start=True, stop=True).then_inc(S("tiles_ps"), 1)
            pe.wait_ge(S("flag_set"), 1)
            unsorted = pe.value_load(flag[0:1, 0:1], min_val=0, max_val=1)
            with pe.If(unsorted != 0):
                pe.wait_ge(S("hist_d"), NBK)
                mm(bank(6)[:, 0:NBK], ones_f, part_d, start=True, stop=True).then_inc(S("starts_ps"), 1)
                pe.wait_ge(S("starts_d"), 1)
                mm(rank_ps, ident, start_d.unsqueeze(2).to_broadcast([P, NBK, G]), start=True, stop=True)
                with pe.Fori(0, COLS // G) as n:
                    pe.wait_ge(S("sort_oh"), n + 1)
                    rank_before(0).then_inc(S("sort_ps"), 1)
                    pe.wait_ge(S("sort_mul"), n + 1)
                    rank_after(0).then_inc(S("sort_after"), 1)

            pe.wait_ge(S("w_in"), 96)
            pe.wait_ge(S("step_tables"), 1)

            def norm0(j, k):
                i = j * 2 + k
                pe.wait_ge(S("h_ready"), i + 1)
                for b in range(LNG):
                    o = nc.tensor.transpose(bank(2 * k + b // 4)[:, b % 4 * P:(b % 4 + 1) * P],
                                            hbuf[k][:, b * P:(b + 1) * P], ident)
                o.then_inc(S("hT_ps"), 1)
                pe.wait_ge(S("hT_ready"), i + 1)
                wait(pe, "tab_ready", (i - 1) * LNG)
                for b in range(LNG):
                    o = mm(bank(4 + 2 * k + b // 4)[:, b % 4 * P:(b % 4 + 1) * P], hTs[k][:, b * P:(b + 1) * P],
                           wT[:, 0, :], start=True, stop=True)
                o.then_inc(S("m_ready"), 1)

            for k in range(2):
                norm0(0, k)
            with pe.Fori(1, LN_TURNS // 2) as j:
                for k in range(2):
                    norm0(j, k)

            pe.wait_ge(S("hT_ready"), LN_TURNS)
            for f, (src_f, need) in enumerate(((fld[3], 1), (fld[4], 2), (fld[6], 3))):
                pe.wait_ge(S("field"), need)
                if f == 1:
                    pe.wait_ge(S("tab_ready"), BLOCKS)
                    pe.wait_ge(S("src_counted"), 1)
                    mm(bank(7)[:, 256:256 + NBK], ones_f, part_s, start=True, stop=True).then_inc(S("starts_ps_s"), 1)
                for a in range(4):
                    if f == 2:
                        pe.wait_ge(S("fields_moved"), a + 1)
                    for s in range(a * 4, min(a * 4 + 4, SB)):
                        o = nc.tensor.transpose(bank((f % 2) * 4 + a)[:, s % 4 * P:(s % 4 + 1) * P],
                                                src_f[:, s * P:(s + 1) * P], ident)
                    o.then_inc(S("fields_T"), 1)

            regs = [pe.alloc_register(f"step_off{q}") for q in range(CH)]

            def step_offsets(c):
                nc.tensor.load(regs, steprow[0:1, ds(c * CH, CH)])

            def rel(g, q):
                first = pe.snap(regs[g * G], min_val=0, max_val=(BLOCKS - 1) * P)
                own = pe.snap(regs[g * G + q], min_val=0, max_val=(BLOCKS - 1) * P)
                return nc.s_assert_within(pe.snap(own - first), 0, q * P, 
                                          skip_runtime_bounds_check_because="consecutive steps' blocks differ by 0 or 1")

            def sum_group(g, k, free, free_value, done):
                wait(pe, free, free_value)
                mm(bank(1 + g), zeros_b[:, 0:P], zeros_b[:, :], start=True, stop=True, skip_group_check=True)
                for q in range(G):
                    s = g * G + q
                    o = bank(1 + g)[:, 0:P] if q == 0 else ps[:, 1 + g, ds(rel(g, q), P)]
                    m = mm(o, ring[:, k * CH + s, 0:F], oh[:, k, s, :], start=False, stop=True, skip_group_check=True)
                m.then_inc(S(done), 1)

            def layer0(j, k):
                c = j * 2 + k
                step_offsets(c)
                for g in range(GPC):
                    n = c * GPC + g
                    if not isinstance(n, int) or n > 0:
                        pe.wait_ge(S("rank_read"), n)
                        rank_after((g + 3) % G).then_inc(S("rank_counted"), 1)
                    pe.wait_ge(S("blk_ready"), n + 1)
                    rank_before(g).then_inc(S("rank_ps"), 1)
                    if g == 0:
                        pe.wait_ge(S("oh_ready"), c + 1)
                        pe.wait_ge(S(f"gathered{k}"), j * (CH * 16) + CH * 16)
                    sum_group(g, k, "agg_added", n - 3, "agg_done")

            pe.wait_ge(S("fields_moved"), 12)
            pe.wait_ge(S("steprow_in"), 16)
            pe.wait_ge(S("base_s"), 1)
            mm(rank_ps, ident, base_s.unsqueeze(2).to_broadcast([P, NBK, G]), start=True, stop=True)
            for k in range(2):
                layer0(0, k)
            with pe.Fori(1, PAIRS) as j:
                for k in range(2):
                    layer0(j, k)

            pe.wait_ge(S("agg_added"), GROUPS)

            def gates(i, k):
                wait(pe, "cand_in", i - 1)
                msg, h = Y[:, ds(i * GW, GW)], H[:, ds(i * GW, GW)]
                for a in range(2):
                    o = bank(2 * k)[:, a * GW:(a + 1) * GW]
                    mm(o, wT[:, 1 + a, :], msg, start=True, stop=False)
                    mm(o, wT[:, 4 + a, :], h, start=False, stop=True)
                mm(bank(2 * k + 1)[:, 0:GW], wT[:, 3, :], msg, start=True, stop=True)
                mm(bank(2 * k + 1)[:, GW:2 * GW], wT[:, 6, :], h, start=True, stop=True).then_inc(S("gates_ps"), 1)

            def back(i, k):
                pe.wait_ge(S("hn_ready"), i + 1)
                wait(pe, "x1_kept", i - 1)
                for b in range(NG):
                    m = nc.tensor.transpose(bank(4 + k)[:, b * P:(b + 1) * P], hnbuf[k][:, b * P:(b + 1) * P], ident)
                m.then_inc(S("hn_ps"), 1)

            gates(0, 0)
            gates(1, 1)
            for k in range(2):
                gates(k + 2, k)
                back(k, k)
            with pe.Fori(1, (TURNS - 3) // 2) as j:
                for k in range(2):
                    gates(j * 2 + k + 2, k)
                    back(j * 2 + k, k)
            gates(TURNS - 1, 0)
            for i in range(TURNS - 3, TURNS):
                back(i, i % 2)

            def h2T(i, k):
                pe.wait_ge(S("h2_ready"), i + 1)
                wait(pe, "h2_done", i - HSLOTS + 1)
                for b in range(NG):
                    o = nc.tensor.transpose(bank(k)[:, b * P:(b + 1) * P], hs[k][:, b * P:(b + 1) * P], ident)
                o.then_inc(S("h2_ps"), 1)

            norm_loop(pe, h2T)

            def picks(j, k):
                c = j * 2 + k
                step_offsets(c)
                for g in range(GPC):
                    n = c * GPC + g
                    pe.wait_ge(S("pick_oh"), n + 1)
                    wait(pe, "row_moved", n - 3)
                    for q in range(G):
                        off = pe.snap(regs[g * G + q], min_val=0, max_val=(BLOCKS - 1) * P)
                        m = mm(bank(g)[:, q * P:(q + 1) * P], pick[g][:, q * P:(q + 1) * P], H[:, ds(off, P)],
                               start=True, stop=True)
                    m.then_inc(S("picked"), 1)

            pe.wait_ge(S("h2_kept"), TURNS)
            pe.wait_ge(S("h2_done"), TURNS)
            for k in range(2):
                picks(0, k)
            with pe.Fori(1, PAIRS) as j:
                for k in range(2):
                    picks(j, k)

            def layer1_sum(c0, j, r):
                k = r % 2
                step_offsets(c0 + r)
                for g in range(GPC):
                    if g * G < OH_V:
                        pe.wait_ge(S("key_oh_v"), (c0 + r + 1) * V_PIECES)
                    if (g + 1) * G > OH_V:
                        pe.wait_ge(S("key_oh_p"), c0 + r + 1)
                    if (g + 1) * G > OH_V + OH_P:
                        pe.wait_ge(S("key_oh_a"), c0 + r + 1)
                    pe.wait_ge(S("bank_zero"), (c0 + r) * GPC + g + 1)
                    for q in range(G):
                        s = g * G + q
                        o = bank(r % 2 * GPC + g)[:, 0:P] if q == 0 else ps[:, r % 2 * GPC + g, ds(rel(g, q), P)]
                        m = mm(o, rrows[r][:, s, 0:F], oh[:, k, s, :], start=False, stop=True, skip_group_check=True)
                    m.then_inc(S("sum_done"), 1)

            pe.wait_ge(S("steprow_in"), 32)
            pe.wait_ge(S("row_moved"), GROUPS)
            nc.tensor.sem_inc(S("sum_done"), 2 * GPC)
            sum_loop(pe, layer1_sum)

            pe.wait_ge(S("bank_free"), GROUPS + 2 * GPC)

            def lin1(i, k):
                wait(pe, "lin1", i - 1)
                mm(bank(4 + k)[:, 0:GW], wT[:, 7, :], Y[:, ds(i * GW, GW)], start=True, stop=True).then_inc(S("lin1_ps"), 1)

            lin1(0, 0)
            lin1(1, 1)
            with pe.Fori(1, (TURNS - 1) // 2) as j:
                for k in range(2):
                    lin1(j * 2 + k, k)
            lin1(TURNS - 1, 0)

            def lin2(i, k):
                pe.wait_ge(S("z_ready"), i + 1)
                wait(pe, "out_ready", i - 1)
                for b in range(NG):
                    o = bank(k)[:, b * P:(b + 1) * P]
                    m = mm(o, fin_z[k][:, b * P:(b + 1) * P], wT[:, 8, :], start=True, stop=True)
                m.then_inc(S("lin2_ps"), 1)

            lin2(0, 0)
            lin2(1, 1)
            with pe.Fori(1, (TURNS - 1) // 2) as j:
                for k in range(2):
                    lin2(j * 2 + k, k)
            lin2(TURNS - 1, 0)


def shape_constants(np):
    c = np.zeros((P, CF_W), np.float32)

    def put(name, value):
        a, w = CF[name]
        c[:, a:a + w] = value

    put("ident", np.eye(P))
    put("ones", 1.0)
    put("before", np.triu(np.ones((P, P)), 1))
    put("iota", np.arange(P))
    put("iota_p", np.arange(P)[:, None])
    put("thr", np.arange(NBK) - 0.5)
    put("node", np.arange(NBK) * P - 0.5)
    put("blk", np.arange(NBK))
    put("step", np.arange(SB) * P + np.arange(P)[:, None])
    put("lneps", LN_EPS)
    put("bneps", BN_EPS)
    put("pad", np.where(np.arange(RW) == KEY, FAR, 0.0))
    put("blk4", np.repeat(np.arange(NBK), G))
    return c


def kernel(x, src, dst, edge_type_9, L0_gnn_W_msg, L0_gnn_b_msg, L0_gnn_edge_embed, L0_gnn_W_ih, L0_gnn_W_hh,
           L0_gnn_b_ih, L0_gnn_b_hh, L1_gnn_eps, L1_gnn_W1, L1_gnn_b1, L1_gnn_gamma, L1_gnn_beta, L1_gnn_W2, L1_gnn_b2):
    import numpy as np
    import concourse.bacc as bacc
    from concourse.bass_utils import run_bass_kernel_spmd

    def a(v):
        return np.asarray(v)

    def edge_rows(v, pad):
        return np.concatenate([a(v).astype(np.int32), np.full(EPAD - len(v), pad, np.int32)]).reshape(P, COLS)

    w_ih, w_hh = a(L0_gnn_W_ih), a(L0_gnn_W_hh)
    mats = [a(L0_gnn_W_msg)] + [w_ih[k * F:(k + 1) * F] for k in range(3)] + [w_hh[k * F:(k + 1) * F] for k in range(3)] \
        + [a(L1_gnn_W1), a(L1_gnn_W2)]
    b_ih, b_hh = a(L0_gnn_b_ih).reshape(3, F), a(L0_gnn_b_hh).reshape(3, F)
    arrays = {
        "in_x": np.concatenate([a(x), np.zeros((NPAD - N, F), np.float32)]),
        "in_edges": np.stack([edge_rows(dst, PADNODE), edge_rows(src, PADNODE), edge_rows(edge_type_9, 0)]),
        "in_dst_next": edge_rows(a(dst)[1:], PADNODE),
        "in_weights": np.ascontiguousarray(np.concatenate([m.T for m in mats], axis=1)),
        "in_bias_cols": np.ascontiguousarray(np.stack([*b_ih, *b_hh, a(L1_gnn_b1), a(L1_gnn_gamma), a(L1_gnn_beta)], axis=1)),
        "in_embed": a(L0_gnn_edge_embed),
        "in_b_msg": a(L0_gnn_b_msg),
        "in_b2": a(L1_gnn_b2),
        "in_eps": a(L1_gnn_eps).reshape(1, 1),
        "in_consts": shape_constants(np),
    }
    nc = bacc.Bacc("TRN2", target_bir_lowering=False, num_devices=1)
    args = [nc.dram_tensor(n, v.shape, mybir.dt.from_np(v.dtype), kind="ExternalInput").ap() for n, v in arrays.items()]
    out = nc.dram_tensor("out_x", (NPAD, F), mybir.dt.float32, kind="ExternalOutput").ap()
    build_gnn(nc, *args, out)
    r = run_bass_kernel_spmd(nc, [arrays], core_ids=[0])
    return r.results[0]["out_x"][:N]
```
